# Optimizing a Trainium2 kernel written in Bass

```python
import numpy as np
import jax
import jax.numpy as jnp

def _softmax(x, axis=-1):
    return jax.nn.softmax(x, axis=axis)

def _gelu(x):
    return jax.nn.gelu(x, approximate=True)

def _silu(x):
    return jax.nn.silu(x)

def _sigmoid(x):
    return jax.nn.sigmoid(x)

def _layernorm(x, axis=-1, eps=1e-05):
    m = jnp.mean(x, axis=axis, keepdims=True)
    v = jnp.var(x, axis=axis, keepdims=True)
    return (x - m) / jnp.sqrt(v + eps)

def _scatter_add(tgt, idx, src, axis=0):
    return tgt.at[idx].add(src)

def _segment_sum(src, seg, n):
    return jax.ops.segment_sum(src, seg, n)
kernel_name = 'mk_seq_preln_d2_jaxref_r8_a732f0'

def setup_inputs(seed: int=0):
    np.random.seed(seed)
    _w = jnp.asarray

    def _L0_attn_setup():
        import jax, jax.numpy as jnp
        import numpy as np
        N_HEADS, D_MODEL, D_HEAD, SEQ, BATCH = (16, 256, 128, 256, 1)
        ATTN_SCALE = float(np.sqrt(D_HEAD))
        ROPE_BASE = 10000.0

        def _rope_cos_sin(seq_len, d_head, dtype):
            inv_freq = 1.0 / ROPE_BASE ** (jnp.arange(0, d_head, 2, dtype=jnp.float32) / d_head)
            t = jnp.arange(seq_len, dtype=jnp.float32)
            freqs = t[:, None] * inv_freq[None, :]
            return (jnp.cos(freqs).astype(dtype), jnp.sin(freqs).astype(dtype))

        def _apply_rotary(x, cos, sin):
            B, S, H, D = x.shape
            x2 = x.reshape(B, S, H, D // 2, 2)
            xr, xi = (x2[..., 0], x2[..., 1])
            c = cos[None, :, None, :]
            s = sin[None, :, None, :]
            outr = xr * c - xi * s
            outi = xr * s + xi * c
            return jnp.stack([outr, outi], axis=-1).reshape(B, S, H, D)
        key = jax.random.key(seed)
        ks = jax.random.split(key, 9)
        std = 0.02
        return {'resid_pre': jax.random.normal(ks[0], (BATCH, SEQ, D_MODEL), dtype=jnp.float32), 'W_Q': jax.random.normal(ks[1], (N_HEADS, D_MODEL, D_HEAD), dtype=jnp.float32) * std, 'W_K': jax.random.normal(ks[2], (N_HEADS, D_MODEL, D_HEAD), dtype=jnp.float32) * std, 'W_V': jax.random.normal(ks[3], (N_HEADS, D_MODEL, D_HEAD), dtype=jnp.float32) * std, 'W_O': jax.random.normal(ks[4], (N_HEADS, D_HEAD, D_MODEL), dtype=jnp.float32) * std, 'b_Q': jnp.zeros((N_HEADS, D_HEAD), dtype=jnp.float32), 'b_K': jnp.zeros((N_HEADS, D_HEAD), dtype=jnp.float32), 'b_V': jnp.zeros((N_HEADS, D_HEAD), dtype=jnp.float32), 'b_O': jnp.zeros((D_MODEL,), dtype=jnp.float32)}
    _L0_attn_in = _L0_attn_setup()

    def _L0_ffn_setup():
        import jax, jax.numpy as jnp
        import numpy as np
        NUM_EXPERTS = 16
        TOP_K = 4
        N_GROUP = 4
        TOPK_GROUP = 2
        SCALING = 2.5

        def _route(x, gate_weight, expert_bias):
            logits = x @ gate_weight.T
            scores = jax.nn.sigmoid(logits)
            biased = scores + expert_bias[None, :]
            T = x.shape[0]
            gsz = NUM_EXPERTS // N_GROUP
            grp = biased.reshape(T, N_GROUP, gsz)
            top2, _ = jax.lax.top_k(grp, 2)
            group_scores = top2.sum(-1)
            _, gidx = jax.lax.top_k(group_scores, TOPK_GROUP)
            gmask = jax.nn.one_hot(gidx, N_GROUP, dtype=scores.dtype).sum(1)
            emask = jnp.repeat(gmask, gsz, axis=1)
            masked = jnp.where(emask > 0, biased, -jnp.inf)
            _, sel = jax.lax.top_k(masked, TOP_K)
            w = jnp.take_along_axis(scores, sel, axis=1)
            w = w / (w.sum(-1, keepdims=True) + 1e-20)
            return (w * SCALING, sel)

        def _moe(x, w, sel, gate_proj, up_proj, down_proj):
            cw = (jax.nn.one_hot(sel, NUM_EXPERTS, dtype=x.dtype) * w[..., None]).sum(1)

            def body(acc, inp):
                g, u, d, we = inp
                y = jax.nn.silu(x @ g.T) * (x @ u.T) @ d.T
                return (acc + we[:, None] * y, None)
            out, _ = jax.lax.scan(body, jnp.zeros_like(x), (gate_proj, up_proj, down_proj, cw.T))
            return out
        key = jax.random.key(seed)
        ks = jax.random.split(key, 9)
        B, S, H, I = (2, 128, 256, 128)
        w = lambda k, shape: jax.random.normal(k, shape, jnp.float32) * 0.02
        return {'hidden_states': jax.random.normal(ks[0], (B, S, H), jnp.float32), 'gate_weight': w(ks[1], (NUM_EXPERTS, H)), 'expert_bias': jnp.zeros((NUM_EXPERTS,), jnp.float32), 'gate_proj': w(ks[2], (NUM_EXPERTS, I, H)), 'up_proj': w(ks[3], (NUM_EXPERTS, I, H)), 'down_proj': w(ks[4], (NUM_EXPERTS, H, I)), 'shared_gate': w(ks[5], (I, H)), 'shared_up': w(ks[6], (I, H)), 'shared_down': w(ks[7], (H, I))}
    _L0_ffn_in = _L0_ffn_setup()

    def _L1_attn_setup():
        import jax, jax.numpy as jnp
        import numpy as np
        EMBED_DIM = 256
        NUM_HEADS = 16
        HEAD_DIM = EMBED_DIM // NUM_HEADS
        BASE = 10000.0

        def rotate_half(x):
            half = x.shape[-1] // 2
            x1, x2 = (x[..., :half], x[..., half:])
            return jnp.concatenate([-x2, x1], axis=-1)

        def apply_rope(x, base=BASE):
            S, Dh = (x.shape[-2], x.shape[-1])
            inv_freq = 1.0 / base ** (jnp.arange(0, Dh, 2, dtype=jnp.float32) / Dh)
            t = jnp.arange(S, dtype=jnp.float32)
            freqs = jnp.einsum('i,j->ij', t, inv_freq)
            emb = jnp.concatenate([freqs, freqs], axis=-1)
            return x * jnp.cos(emb) + rotate_half(x) * jnp.sin(emb)
        key = jax.random.key(seed)
        ks = jax.random.split(key, 9)
        B, S, D = (2, 256, EMBED_DIM)
        xavier = lambda k, shape: jax.random.uniform(k, shape, jnp.float32, -1.0, 1.0) * float(np.sqrt(6.0 / (shape[0] + shape[1])))
        return {'x': jax.random.normal(ks[0], (B, S, D), jnp.float32), 'q_w': xavier(ks[1], (D, D)), 'k_w': xavier(ks[2], (D, D)), 'v_w': xavier(ks[3], (D, D)), 'q_b': jnp.zeros((D,), jnp.float32), 'k_b': jnp.zeros((D,), jnp.float32), 'v_b': jnp.zeros((D,), jnp.float32), 'out_w': xavier(ks[4], (D, D)), 'out_b': jnp.zeros((D,), jnp.float32)}
    _L1_attn_in = _L1_attn_setup()

    def _L1_ffn_setup():
        import jax, jax.numpy as jnp
        import numpy as np
        from jax import lax
        TOP_K = 4
        ROUTED_SCALING = 1.0
        RENORMALIZE = True

        def _swiglu_ffn(x, wg, wu, wd):
            return jax.nn.silu(x @ wg.T) * (x @ wu.T) @ wd.T
        key = jax.random.key(seed)
        ks = jax.random.split(key, 9)
        H, I, E = (256, 128, 16)
        s = 0.02
        return {'hidden_states': jax.random.normal(ks[0], (2, 128, H), jnp.float32), 'gate_w': jax.random.normal(ks[1], (E, H), jnp.float32) * s, 'expert_bias': jax.random.normal(ks[2], (E,), jnp.float32) * s, 'w_gate': jax.random.normal(ks[3], (E, I, H), jnp.float32) * s, 'w_up': jax.random.normal(ks[4], (E, I, H), jnp.float32) * s, 'w_down': jax.random.normal(ks[5], (E, H, I), jnp.float32) * s, 'sw_gate': jax.random.normal(ks[6], (I, H), jnp.float32) * s, 'sw_up': jax.random.normal(ks[7], (I, H), jnp.float32) * s, 'sw_down': jax.random.normal(ks[8], (H, I), jnp.float32) * s}
    _L1_ffn_in = _L1_ffn_setup()
    _d = {'L0_attn_resid_pre': _L0_attn_in['resid_pre'], 'L0_attn_W_Q': _L0_attn_in['W_Q'], 'L0_attn_W_K': _L0_attn_in['W_K'], 'L0_attn_W_V': _L0_attn_in['W_V'], 'L0_attn_W_O': _L0_attn_in['W_O'], 'L0_attn_b_Q': _L0_attn_in['b_Q'], 'L0_attn_b_K': _L0_attn_in['b_K'], 'L0_attn_b_V': _L0_attn_in['b_V'], 'L0_attn_b_O': _L0_attn_in['b_O'], 'L0_ffn_gate_weight': _L0_ffn_in['gate_weight'], 'L0_ffn_expert_bias': _L0_ffn_in['expert_bias'], 'L0_ffn_gate_proj': _L0_ffn_in['gate_proj'], 'L0_ffn_up_proj': _L0_ffn_in['up_proj'], 'L0_ffn_down_proj': _L0_ffn_in['down_proj'], 'L0_ffn_shared_gate': _L0_ffn_in['shared_gate'], 'L0_ffn_shared_up': _L0_ffn_in['shared_up'], 'L0_ffn_shared_down': _L0_ffn_in['shared_down'], 'L1_attn_q_w': _L1_attn_in['q_w'], 'L1_attn_k_w': _L1_attn_in['k_w'], 'L1_attn_v_w': _L1_attn_in['v_w'], 'L1_attn_q_b': _L1_attn_in['q_b'], 'L1_attn_k_b': _L1_attn_in['k_b'], 'L1_attn_v_b': _L1_attn_in['v_b'], 'L1_attn_out_w': _L1_attn_in['out_w'], 'L1_attn_out_b': _L1_attn_in['out_b'], 'L1_ffn_gate_w': _L1_ffn_in['gate_w'], 'L1_ffn_expert_bias': _L1_ffn_in['expert_bias'], 'L1_ffn_w_gate': _L1_ffn_in['w_gate'], 'L1_ffn_w_up': _L1_ffn_in['w_up'], 'L1_ffn_w_down': _L1_ffn_in['w_down'], 'L1_ffn_sw_gate': _L1_ffn_in['sw_gate'], 'L1_ffn_sw_up': _L1_ffn_in['sw_up'], 'L1_ffn_sw_down': _L1_ffn_in['sw_down']}
    _x0 = _d['L0_attn_resid_pre']
    _d['L0_attn_resid_pre'] = jax.random.normal(jax.random.fold_in(jax.random.key(seed), 1), (2, 512, 256), dtype=_x0.dtype)
    del _x0
    return _d

def reference(L0_attn_resid_pre, L0_attn_W_Q, L0_attn_W_K, L0_attn_W_V, L0_attn_W_O, L0_attn_b_Q, L0_attn_b_K, L0_attn_b_V, L0_attn_b_O, L0_ffn_gate_weight, L0_ffn_expert_bias, L0_ffn_gate_proj, L0_ffn_up_proj, L0_ffn_down_proj, L0_ffn_shared_gate, L0_ffn_shared_up, L0_ffn_shared_down, L1_attn_q_w, L1_attn_k_w, L1_attn_v_w, L1_attn_q_b, L1_attn_k_b, L1_attn_v_b, L1_attn_out_w, L1_attn_out_b, L1_ffn_gate_w, L1_ffn_expert_bias, L1_ffn_w_gate, L1_ffn_w_up, L1_ffn_w_down, L1_ffn_sw_gate, L1_ffn_sw_up, L1_ffn_sw_down):

    def _L0_attn_ref(resid_pre, W_Q, W_K, W_V, W_O, b_Q, b_K, b_V, b_O):
        import jax, jax.numpy as jnp
        import numpy as np
        N_HEADS, D_MODEL, D_HEAD, SEQ, BATCH = (16, 256, 128, 256, 1)
        ATTN_SCALE = float(np.sqrt(D_HEAD))
        ROPE_BASE = 10000.0

        def _rope_cos_sin(seq_len, d_head, dtype):
            inv_freq = 1.0 / ROPE_BASE ** (jnp.arange(0, d_head, 2, dtype=jnp.float32) / d_head)
            t = jnp.arange(seq_len, dtype=jnp.float32)
            freqs = t[:, None] * inv_freq[None, :]
            return (jnp.cos(freqs).astype(dtype), jnp.sin(freqs).astype(dtype))

        def _apply_rotary(x, cos, sin):
            B, S, H, D = x.shape
            x2 = x.reshape(B, S, H, D // 2, 2)
            xr, xi = (x2[..., 0], x2[..., 1])
            c = cos[None, :, None, :]
            s = sin[None, :, None, :]
            outr = xr * c - xi * s
            outi = xr * s + xi * c
            return jnp.stack([outr, outi], axis=-1).reshape(B, S, H, D)
        B, S, _ = resid_pre.shape
        q = jnp.einsum('bpd,hde->bphe', resid_pre, W_Q) + b_Q
        k = jnp.einsum('bpd,hde->bphe', resid_pre, W_K) + b_K
        v = jnp.einsum('bpd,hde->bphe', resid_pre, W_V) + b_V
        cos, sin = _rope_cos_sin(S, D_HEAD, q.dtype)
        q = _apply_rotary(q, cos, sin)
        k = _apply_rotary(k, cos, sin)
        scores = jnp.einsum('bqhd,bkhd->bhqk', q, k) / ATTN_SCALE
        causal = jnp.tril(jnp.ones((S, S), dtype=bool))
        scores = jnp.where(causal[None, None], scores, jnp.zeros((), dtype=scores.dtype))
        max_v = jnp.max(jnp.abs(scores), axis=-1, keepdims=True)
        sgn = jnp.sign(scores)
        attn_w = sgn * jnp.exp(sgn * scores - max_v)
        attn = attn_w / (jnp.sum(jnp.abs(attn_w), axis=-1, keepdims=True) + 1e-06)
        z = jnp.einsum('bkhd,bhqk->bqhd', v, attn)
        out = jnp.einsum('bqhd,hdm->bqm', z, W_O) + b_O
        return out

    def _L0_ffn_ref(hidden_states, gate_weight, expert_bias, gate_proj, up_proj, down_proj, shared_gate, shared_up, shared_down):
        import jax, jax.numpy as jnp
        import numpy as np
        NUM_EXPERTS = 16
        TOP_K = 4
        N_GROUP = 4
        TOPK_GROUP = 2
        SCALING = 2.5

        def _route(x, gate_weight, expert_bias):
            logits = x @ gate_weight.T
            scores = jax.nn.sigmoid(logits)
            biased = scores + expert_bias[None, :]
            T = x.shape[0]
            gsz = NUM_EXPERTS // N_GROUP
            grp = biased.reshape(T, N_GROUP, gsz)
            top2, _ = jax.lax.top_k(grp, 2)
            group_scores = top2.sum(-1)
            _, gidx = jax.lax.top_k(group_scores, TOPK_GROUP)
            gmask = jax.nn.one_hot(gidx, N_GROUP, dtype=scores.dtype).sum(1)
            emask = jnp.repeat(gmask, gsz, axis=1)
            masked = jnp.where(emask > 0, biased, -jnp.inf)
            _, sel = jax.lax.top_k(masked, TOP_K)
            w = jnp.take_along_axis(scores, sel, axis=1)
            w = w / (w.sum(-1, keepdims=True) + 1e-20)
            return (w * SCALING, sel)

        def _moe(x, w, sel, gate_proj, up_proj, down_proj):
            cw = (jax.nn.one_hot(sel, NUM_EXPERTS, dtype=x.dtype) * w[..., None]).sum(1)

            def body(acc, inp):
                g, u, d, we = inp
                y = jax.nn.silu(x @ g.T) * (x @ u.T) @ d.T
                return (acc + we[:, None] * y, None)
            out, _ = jax.lax.scan(body, jnp.zeros_like(x), (gate_proj, up_proj, down_proj, cw.T))
            return out
        B, S, H = hidden_states.shape
        x = hidden_states.reshape(-1, H)
        w, sel = _route(x, gate_weight, expert_bias)
        out = _moe(x, w, sel, gate_proj, up_proj, down_proj)
        shared = jax.nn.silu(x @ shared_gate.T) * (x @ shared_up.T) @ shared_down.T
        return (out + shared).reshape(B, S, H)

    def _L1_attn_ref(x, q_w, k_w, v_w, q_b, k_b, v_b, out_w, out_b):
        import jax, jax.numpy as jnp
        import numpy as np
        EMBED_DIM = 256
        NUM_HEADS = 16
        HEAD_DIM = EMBED_DIM // NUM_HEADS
        BASE = 10000.0

        def rotate_half(x):
            half = x.shape[-1] // 2
            x1, x2 = (x[..., :half], x[..., half:])
            return jnp.concatenate([-x2, x1], axis=-1)

        def apply_rope(x, base=BASE):
            S, Dh = (x.shape[-2], x.shape[-1])
            inv_freq = 1.0 / base ** (jnp.arange(0, Dh, 2, dtype=jnp.float32) / Dh)
            t = jnp.arange(S, dtype=jnp.float32)
            freqs = jnp.einsum('i,j->ij', t, inv_freq)
            emb = jnp.concatenate([freqs, freqs], axis=-1)
            return x * jnp.cos(emb) + rotate_half(x) * jnp.sin(emb)
        B, S, D = x.shape
        H, Dh = (NUM_HEADS, HEAD_DIM)
        scaling = Dh ** (-0.5)
        q = (x @ q_w.T + q_b).reshape(B, S, H, Dh).transpose(0, 2, 1, 3)
        k = (x @ k_w.T + k_b).reshape(B, S, H, Dh).transpose(0, 2, 1, 3)
        v = (x @ v_w.T + v_b).reshape(B, S, H, Dh).transpose(0, 2, 1, 3)
        q = apply_rope(q)
        k = apply_rope(k)
        attn = jnp.einsum('bhqd,bhkd->bhqk', q, k) * scaling
        probs = jax.nn.softmax(attn, axis=-1)
        out = jnp.einsum('bhqk,bhkd->bhqd', probs, v)
        out = out.transpose(0, 2, 1, 3).reshape(B, S, D)
        return out @ out_w.T + out_b

    def _L1_ffn_ref(hidden_states, gate_w, expert_bias, w_gate, w_up, w_down, sw_gate, sw_up, sw_down):
        import jax, jax.numpy as jnp
        import numpy as np
        from jax import lax
        TOP_K = 4
        ROUTED_SCALING = 1.0
        RENORMALIZE = True

        def _swiglu_ffn(x, wg, wu, wd):
            return jax.nn.silu(x @ wg.T) * (x @ wu.T) @ wd.T
        orig_shape = hidden_states.shape
        H = orig_shape[-1]
        x = hidden_states.reshape(-1, H)
        T = x.shape[0]
        logits = x.astype(jnp.float32) @ gate_w.T
        scores = jax.nn.sigmoid(logits)
        _, topk_idx = lax.top_k(scores + expert_bias[None, :], TOP_K)
        topk_w = jnp.take_along_axis(scores, topk_idx, axis=-1)
        if RENORMALIZE:
            topk_w = topk_w / jnp.sum(topk_w, axis=-1, keepdims=True)
        topk_w = topk_w * ROUTED_SCALING
        E = gate_w.shape[0]
        combine = jnp.zeros((T, E), dtype=x.dtype).at[jnp.arange(T)[:, None], topk_idx].set(topk_w.astype(x.dtype))

        def step(acc, ws):
            wg, wu, wd, cw = ws
            return (acc + cw[:, None] * _swiglu_ffn(x, wg, wu, wd), None)
        routed, _ = lax.scan(step, jnp.zeros_like(x), (w_gate, w_up, w_down, combine.T))
        shared = _swiglu_ffn(x, sw_gate, sw_up, sw_down)
        return (routed + shared).reshape(orig_shape)
    x = L0_attn_resid_pre
    x = x + _L0_attn_ref(_layernorm(x, axis=-1), L0_attn_W_Q, L0_attn_W_K, L0_attn_W_V, L0_attn_W_O, L0_attn_b_Q, L0_attn_b_K, L0_attn_b_V, L0_attn_b_O)
    x = x + _L0_ffn_ref(_layernorm(x, axis=-1), L0_ffn_gate_weight, L0_ffn_expert_bias, L0_ffn_gate_proj, L0_ffn_up_proj, L0_ffn_down_proj, L0_ffn_shared_gate, L0_ffn_shared_up, L0_ffn_shared_down)
    x = x + _L1_attn_ref(_layernorm(x, axis=-1), L1_attn_q_w, L1_attn_k_w, L1_attn_v_w, L1_attn_q_b, L1_attn_k_b, L1_attn_v_b, L1_attn_out_w, L1_attn_out_b)
    x = x + _L1_ffn_ref(_layernorm(x, axis=-1), L1_ffn_gate_w, L1_ffn_expert_bias, L1_ffn_w_gate, L1_ffn_w_up, L1_ffn_w_down, L1_ffn_sw_gate, L1_ffn_sw_up, L1_ffn_sw_down)
    return x

_drawn_inputs = setup_inputs


def setup_inputs(seed=0):
    import zlib

    import numpy as np

    out = dict(_drawn_inputs(seed))
    spreads = {'L0_attn_b_Q': (0.0, 0.375),
     'L0_attn_b_K': (0.0, 0.293),
     'L0_attn_b_V': (0.0, 0.384),
     'L0_attn_b_O': (0.0, 0.1),
     'L0_ffn_expert_bias': (0.0, 0.539),
     'L1_attn_q_b': (0.0, 0.8),
     'L1_attn_k_b': (0.0, 0.588),
     'L1_attn_v_b': (0.0, 0.1),
     'L1_attn_out_b': (0.0, 0.1)}
    factors = {'L0_ffn_gate_weight': 5.661,
     'L0_ffn_gate_proj': 3.796,
     'L0_ffn_up_proj': 3.753,
     'L0_ffn_down_proj': 3.757,
     'L0_ffn_shared_gate': 4.85,
     'L0_ffn_shared_up': 4.769,
     'L0_ffn_shared_down': 4.769,
     'L1_ffn_gate_w': 8.0,
     'L1_ffn_expert_bias': 8.0,
     'L1_ffn_w_gate': 8.0,
     'L1_ffn_w_up': 8.0,
     'L1_ffn_w_down': 8.0,
     'L1_ffn_sw_gate': 4.934,
     'L1_ffn_sw_up': 4.901,
     'L1_ffn_sw_down': 4.915}
    for name, (base, spread) in spreads.items():
        noise = np.random.default_rng([zlib.crc32(name.encode()), seed]).standard_normal(out[name].shape)
        drawn = base * np.exp(spread * noise) if base else spread * noise
        out[name] = jnp.asarray(drawn.astype(out[name].dtype))
    for name, factor in factors.items():
        out[name] = (out[name] * factor).astype(out[name].dtype)
    return out
```

```python
from contextlib import ExitStack

import numpy as np
import concourse.bass as bass
from concourse import mybir

ALU = mybir.AluOpType
ACT = mybir.ActivationFunctionType
AX = mybir.AxisListType
F32 = mybir.dt.float32
F32R = mybir.dt.float32r
BF16 = mybir.dt.bfloat16

P = 128
B, S, D = 2, 512, 256
T = B * S
NT = T // P
QT = S // P
DC = D // P
BANK = 512
LN_EPS = 1e-5

H0, DH0 = 16, 128
N0 = B * H0
SCALE0 = float(1.0 / np.sqrt(DH0))

E, I = 16, 128
TOPK = 4
GROUPS, GROUP_KEEP = 4, 2
GSIZE = E // GROUPS
RENORM_EPS = (1e-20, 0.0)
ROUTE_SCALE = (2.5, 1.0)
BIG = 3.0e38

H1, DH1 = 16, 16
SCALE1 = float(DH1) ** -0.5
PAIRS = H1 // 2
N1 = B * PAIRS
STK = 64
ROWS_S = 3 * DH1
ROWS_M = ROWS_S + 2

PARTS = ((0, 0), (1, 0), (0, 1))


def fp(ap):
    return ap.bitcast(F32)


def build_program(nc, a, out):
    es = ExitStack()
    with es:
        sems = {}

        def sem(name):
            if name not in sems:
                sems[name] = es.enter_context(nc.semaphore(name))
            return sems[name]

        cursor = [(nc.sbuf_base + 31) // 32 * 32]

        def sb(name, shape, dt=F32):
            t = nc.alloc_sbuf_tensor_at(name, shape, dt, offset=cursor[0])
            size = int(np.prod(shape[1:])) * (2 if dt == BF16 else 4)
            cursor[0] += (size + 31) // 32 * 32
            return t

        x = sb("x", [P, NT, D])
        ident = sb("ident", [P, P])
        xn = sb("xn", [P, NT, D])
        xT_hi = sb("xT_hi", [P, DC, T], F32R)
        xT_lo = sb("xT_lo", [P, DC, T], F32R)
        aT = sb("aT", [P, DC, T])
        stats = sb("stats", [P, NT, 6])
        meanvar = sb("meanvar", [P, NT, 2])
        vareps = sb("vareps", [P, NT])
        rstd = sb("rstd", [P, NT])
        minus_half = sb("minus_half", [P, NT])

        region = cursor[0]
        cos0 = sb("cos0", [P, S])
        sin0 = sb("sin0", [P, S])
        bqkv0 = sb("bqkv0", [P, 3, N0])
        bo0 = sb("bo0", [P, DC])
        wqk_raw = sb("wqk_raw", [P, 2, DC, DH0])
        wqk = [sb(f"wqk_{p}", [P, 2, DC, DH0], F32R) for p in ("hi", "lo")]
        wv_raw = sb("wv_raw", [P, DC, DH0])
        wv = [sb(f"wv_{p}", [P, DC, DH0], F32R) for p in ("hi", "lo")]
        wo_raw = sb("wo_raw", [P, D])
        wo = [sb(f"wo_{p}", [P, D], F32R) for p in ("hi", "lo")]
        q_in = sb("q_in", [P, 2, S])
        q_sw = sb("q_sw", [P, 2, S])
        q_cos = sb("q_cos", [P, 2, S])
        q_sin = sb("q_sin", [P, 2, S])
        q_rot = sb("q_rot", [P, 2, S])
        qk = [sb(f"qk_{p}", [P, 2, S], F32R) for p in ("hi", "lo")]
        vT = sb("vT", [P, S])
        v0 = [sb(f"v0_{p}", [P, S], F32R) for p in ("hi", "lo")]
        sabs = sb("sabs", [P, QT, S])
        sgn = sb("sgn", [P, 2, QT, S], BF16)
        ex = sb("ex", [P, QT, S])
        w = sb("w", [P, QT, S])
        nmax = sb("nmax", [P, QT])
        den = sb("den", [P, QT])
        dene = sb("dene", [P, QT])
        rden = sb("rden", [P, QT])
        wT = [sb(f"wT_{p}", [P, QT, S], F32R) for p in ("hi", "lo")]
        z0 = [sb(f"z0_{p}", [P, S], F32R) for p in ("hi", "lo")]
        zero_r = sb("zero_r", [P, S], F32R)
        ones_r = sb("ones_r", [P, S], F32R)

        gw_raw = sb("gw_raw", [P, DC, E])
        gw = [sb(f"gw_{p}", [P, DC, E], F32R) for p in ("hi", "lo")]
        ebias = sb("ebias", [P, E])
        lower16 = sb("lower16", [P, E * E])
        lower4 = sb("lower4", [P, GROUPS * GROUPS])
        score = sb("score", [P, NT, E])
        biased = sb("biased", [P, NT, E])
        pairsum = sb("pairsum", [P, NT * GROUPS, 6])
        gscore = sb("gscore", [P, NT, GROUPS])
        ggt = sb("ggt", [P, NT, GROUPS * GROUPS])
        geq = sb("geq", [P, NT, GROUPS * GROUPS])
        grank = sb("grank", [P, NT * GROUPS])
        gkeep = sb("gkeep", [P, NT * GROUPS])
        gpen = sb("gpen", [P, NT * GROUPS])
        masked = sb("masked", [P, NT, E])
        erank = sb("erank", [P, NT * E])
        chosen = sb("chosen", [P, NT, E])
        wsum = sb("wsum", [P, NT])
        wsume = sb("wsume", [P, NT])
        wrec = sb("wrec", [P, NT])
        cw = sb("cw", [P, NT, E])
        cwT = sb("cwT", [E, T])
        ew_raw = sb("ew_raw", [P, 2, 3 * D])
        ew = [sb(f"ew_{p}", [P, 2, 3 * D], F32R) for p in ("hi", "lo")]
        cwb = sb("cwb", [P, 2, T])
        silu = sb("silu", [P, 2, S])
        gu = sb("gu", [P, 2, S])
        guw = sb("guw", [P, 2, S])
        hid = [sb(f"hid_{p}", [P, 2, S], F32R) for p in ("hi", "lo")]
        assert cursor[0] <= nc.sbuf_usable_end
        egt = cwb[:, :, :].rearrange("p a (t n) -> p (a t) n", n=E * E)
        eeq = aT[:, :, :].rearrange("p a (t n) -> p (a t) n", n=E * E)

        cursor[0] = region
        cos1 = sb("cos1", [P, S])
        sin1 = sb("sin1", [P, S])
        b1 = sb("b1", [P, 4, DC])
        bv1 = sb("bv1", [P, D])
        bo1 = sb("bo1", [P, DC])
        w1_raw = sb("w1_raw", [P, 6, DC, D])
        w1 = [sb(f"w1_{p}", [P, 6, DC, D], F32R) for p in ("hi", "lo")]
        rc = sb("rc", [P, 2, S])
        rs = sb("rs", [P, 2, S])
        rr = sb("rr", [P, 2, S])
        qk1 = [sb(f"qk1_{p}", [P, 2, DC, T], F32R) for p in ("hi", "lo")]
        v1 = sb("v1", [P, 2, D])
        v1s = sb("v1s", [P, NT, H1, 2, DH1], F32R)
        qs = sb("qs", [P, 2, S], F32R)
        ks = sb("ks", [P, 2, S], F32R)
        vs = sb("vs", [P, 2, QT, 2, P], F32R)
        nm1 = sb("nm1", [P, P])
        nmT = [sb(f"nmT_{p}", [P, P], F32R) for p in ("hi", "lo")]
        e1 = sb("e1", [P, 2, 2 * S])
        p1 = [sb(f"p1_{p}", [P, 2, 2 * S], F32R) for p in ("hi", "lo")]
        zst = sb("zst", [P, 2, S])
        den1 = sb("den1", [P, P])
        rden1 = sb("rden1", [P, P])
        assert cursor[0] <= nc.sbuf_usable_end
        zh1, zl1, rd1 = e1, xn[:, :, :].rearrange("p (c t) d -> p c (t d)", c=DC), aT

        ps = es.enter_context(nc.psum_tensor("ps", [P, 8, BANK], F32))

        cw_dram = [nc.dram_tensor(f"cw_dram{k}", (E, T), F32).ap() for k in range(2)]
        stk_dram = [nc.dram_tensor(f"stk_{t}", (H1 * STK, T), F32).ap() for t in ("q", "k")]
        z_dram = nc.dram_tensor("z_dram", (N1, P, S), F32).ap()
        rd_dram = nc.dram_tensor("rd_dram", (N1 * 2 * QT, P), F32).ap()

        def known(v):
            return isinstance(v, int)

        def wait(eng, name, value):
            if not known(value) or value > 0:
                eng.wait_ge(sem(name), value)

        def valid(n, count):
            return not known(n) or 0 <= n < count

        def ln_dve(dve, k):
            for t in range(NT):
                if k == 0:
                    dve.wait_ge(sem("x_ld"), 16)
                else:
                    dve.wait_ge(sem("x_add"), 4 * (k - 1) + t // 2 + 1)
                dve.bn_stats(stats[:, t, :], x[:, t, :]).then_inc(sem("ln_stats"), 1)
            for t in range(NT):
                dve.wait_ge(sem("ln_stats"), k * NT + t + 1)
                dve.bn_aggr(meanvar[:, t, :], stats[:, t, :]).then_inc(sem("ln_aggr"), 1)
            dve.wait_ge(sem("ln_aggr"), (k + 1) * NT)
            dve.tensor_scalar(vareps[:, :], meanvar[:, :, 1], LN_EPS, None, ALU.add).then_inc(sem("ln_var"), 1)
            dve.wait_ge(sem("ln_rstd"), k + 1)
            for t in range(NT):
                dve.tensor_scalar(xn[:, t, :], x[:, t, :], meanvar[:, t, 0:1], rstd[:, t:t + 1],
                                  ALU.subtract, ALU.mult).then_inc(sem("xn"), 1)
            for g in range(2 * DC):
                half, c = g // DC, g % DC
                dve.wait_ge(sem("xT_hi"), 2 * DC * k + g + 1)
                dve.tensor_tensor(xT_lo[:, c, half * S:(half + 1) * S], ps[:, 4 + g, :],
                                  fp(xT_hi[:, c, half * S:(half + 1) * S]), ALU.subtract).then_inc(sem("xT_lo"), 1)

        def ln_pool(pool, k):
            if k == 0:
                pool.memset(minus_half[:, :], -0.5).then_inc(sem("half"), 1)
                pool.wait_ge(sem("half"), 1)
            pool.wait_ge(sem("ln_var"), k + 1)
            pool.tensor_tensor(rstd[:, :], vareps[:, :], minus_half[:, :], ALU.pow).then_inc(sem("ln_rstd"), 1)

        def ln_pe(pe, k):
            if k == 0:
                pe.wait_ge(sem("ident"), 16)
            for g in range(2 * DC):
                half, c = g // DC, g % DC
                pe.wait_ge(sem("xn"), k * NT + QT * (half + 1))
                for t in range(QT):
                    last = pe.transpose(ps[:, 4 + g, t * P:(t + 1) * P],
                                        xn[:, half * QT + t, c * P:(c + 1) * P], ident[:, :])
                last.then_inc(sem("xT_ps"), 1)

        def ln_act(act, k):
            for g in range(2 * DC):
                half, c = g // DC, g % DC
                act.wait_ge(sem("xT_ps"), 2 * DC * k + g + 1)
                act.activation(xT_hi[:, c, half * S:(half + 1) * S], ps[:, 4 + g, :], ACT.Copy).then_inc(sem("xT_hi"), 1)

        def back_pe(pe, name, count, banks, tiles):
            for i, bank in enumerate(banks):
                wait(pe, name, count)
                for t2 in range(2):
                    t = tiles[2 * i + t2]
                    for c in range(DC):
                        last = pe.transpose(ps[:, bank, t2 * D + c * P:t2 * D + (c + 1) * P],
                                            aT[:, c, t * P:(t + 1) * P], ident[:, :])
                last.then_inc(sem("back"), 1)

        def back_dve(dve, done, banks, tiles):
            for i, bank in enumerate(banks):
                dve.wait_ge(sem("back"), done + i + 1)
                t = tiles[2 * i]
                dve.tensor_tensor(x[:, t:t + 2, :], x[:, t:t + 2, :],
                                  ps[:, bank, :].rearrange("p (t d) -> p t d", t=2), ALU.add).then_inc(sem("x_add"), 1)

        ROW = [slice(S - P * (qi + 1), S) for qi in range(QT)]
        QORDER = (3, 2, 0, 1)
        SPOT = {3: (2, 0), 2: (3, 0), 0: (3, 3 * P), 1: (4, 0)}
        TSPOT = {0: (7, 0), 1: (5, P), 3: (5, 0), 2: (6, 2 * P)}
        TGROUP = ((0,), (1, 3), (2,))

        def of_tile(n, qi):
            return QT * (n - 1) + QORDER.index(qi) + 1

        def of_pair(n, t):
            return 2 * (n - 1) + t + 1

        def of_group(n, g):
            return len(TGROUP) * (n - 1) + g + 1

        def a0_pe(pe, i):
            if valid(i + 2, N0):
                n = i + 2
                b = n // H0 if known(n) else batch[0]
                wait(pe, "wqk_lo", n + 1)
                wait(pe, "wT_lo", 3 * (n - 2))
                for t in range(2):
                    for j in range(3 * DC):
                        c, (pw, px) = j // 3, PARTS[j % 3]
                        last = pe.matmul(ps[:, 5 + t, :], wqk[pw][:, t, c, :], (xT_hi, xT_lo)[px][:, c, b * S:(b + 1) * S],
                                         start=j == 0, stop=j == 3 * DC - 1)
                    last.then_inc(sem("q_ps"), 1)
            if valid(i + 1, N0):
                n = i + 1
                wait(pe, "qk_lo", 2 * n + 2)
                wait(pe, "v_ev", n)
                wait(pe, "v_lo", n)
                for qi in QORDER:
                    wait(pe, "sgn", of_tile(n, qi))
                    bank, col = SPOT[qi]
                    for j, (pq, pk) in enumerate(PARTS):
                        last = pe.matmul(ps[:, bank, col:col + P * (qi + 1)], qk[pq][:, 0, qi * P:(qi + 1) * P],
                                         qk[pk][:, 1, 0:P * (qi + 1)], start=j == 0, stop=j == 2)
                    last.then_inc(sem("s"), 1)
            if valid(i - 1, N0):
                n = i - 1
                wait(pe, "z_lo", n + 1)
                wait(pe, "wo_lo", n + 1)
                for c in range(DC):
                    for j, (pw, pz) in enumerate(PARTS):
                        last = pe.matmul(ps[:, c, :], wo[pw][:, c * P:(c + 1) * P], z0[pz][:, :],
                                         start=False, stop=j == 2, skip_group_check=True)
                last.then_inc(sem("o"), 1)
            if valid(i, N0):
                n = i
                wait(pe, "w", QT * n + QT)
                wait(pe, "z_lo", n)
                for g, js in enumerate(TGROUP):
                    if g:
                        wait(pe, "q_ev", of_pair(min(n + 3, N0) if known(n) else n + 3, g - 1))
                    for j in js:
                        bank, col = TSPOT[j]
                        for qi in range(j, QT):
                            kc = (QT - 1 - qi + j) * P
                            last = pe.transpose(ps[:, bank, col + (qi - j) * P:col + (qi - j + 1) * P],
                                                w[:, qi, kc:kc + P], ident[:, :])
                    last.then_inc(sem("wT_ps"), 1)
            if valid(i + 1, N0):
                n = i + 1
                b = n // H0 if known(n) else batch[0]
                wait(pe, "wv_lo", n + 1)
                wait(pe, "sgn", of_tile(n + 1, 3))
                for j in range(3 * DC):
                    c, (pw, px) = j // 3, PARTS[j % 3]
                    last = pe.matmul(ps[:, 2, :], wv[pw][:, c, :], (xT_hi, xT_lo)[px][:, c, b * S:(b + 1) * S],
                                     start=j == 0, stop=j == 3 * DC - 1)
                last.then_inc(sem("v_ps"), 1)
            if valid(i, N0):
                n = i
                wait(pe, "v_lo", n + 1)
                wait(pe, "wT_lo", 3 * n + 3)
                for j in range(QT):
                    for m, (pv, pw) in enumerate(PARTS):
                        last = pe.matmul(ps[:, 7, j * P:S], v0[pv][:, j * P:(j + 1) * P], wT[pw][:, j, j * P:S],
                                         start=j == 0 and m == 0, stop=j == QT - 1 and m == 2, skip_group_check=True)
                last.then_inc(sem("pv"), 1)
            if valid(i + 1, N0):
                n = i + 1
                wait(pe, "v_ev", n + 1)
                for t in range(QT):
                    last = pe.transpose(ps[:, 4, t * P:(t + 1) * P], vT[:, t * P:(t + 1) * P], ident[:, :])
                last.then_inc(sem("vt_ps"), 1)

        def a0_act(act, i):
            if valid(i + 2, N0):
                n = i + 2
                for t in range(2):
                    wait(act, "q_ps", of_pair(n + 1, t))
                    wait(act, "q_cos", of_pair(n, t))
                    wait(act, "q_sin", of_pair(n, t))
                    act.activation(q_in[:, t, :], ps[:, 5 + t, :], ACT.Identity,
                                   bias=bqkv0[:, t, bass.ds(n, 1)]).then_inc(sem("q_ev"), 1)
            if valid(i + 3, N0):
                n = i + 3
                wait(act, "wqk_ld", 16 * (n + 1))
                wait(act, "q_ps", 2 * n)
                act.activation(wqk[0][:, :, :, :], wqk_raw[:, :, :, :], ACT.Copy).then_inc(sem("wqk_hi"), 1)
            if valid(i + 1, N0):
                n = i + 1
                for qi in QORDER:
                    wait(act, "s", of_tile(n + 1, qi))
                    if qi == 2:
                        wait(act, "s", of_tile(n + 1, 0))
                    wait(act, "ex", of_tile(n, qi))
                    bank, col = SPOT[qi]
                    src = ps[:, bank, col:col + P * (qi + 1)]
                    act.activation(sabs[:, qi, ROW[qi]], src, ACT.Abs, scale=SCALE0).then_inc(sem("sabs"), 1)
                    wait(act, "w", of_tile(n - 1, qi))
                    act.activation(sgn[:, par(1), qi, ROW[qi]], src, ACT.Sign).then_inc(sem("sgn"), 1)
            if valid(i, N0):
                n = i
                wait(act, "pv", n)
                for g, js in enumerate(TGROUP):
                    wait(act, "wT_ps", of_group(n + 1, g))
                    for j in js:
                        bank, col = TSPOT[j]
                        last = act.activation(wT[0][:, j, j * P:S], ps[:, bank, col:col + S - j * P], ACT.Copy)
                    last.then_inc(sem("wT_hi"), 1)
            if valid(i, N0):
                n = i
                wait(act, "wo_ld", 16 * (n + 1))
                wait(act, "o", n)
                act.activation(wo[0][:, :], wo_raw[:, :], ACT.Copy).then_inc(sem("wo_hi"), 1)
            if valid(i + 1, N0):
                n = i + 1
                wait(act, "v_ps", n + 1)
                wait(act, "vt_ps", n)
                act.activation(vT[:, :], ps[:, 2, :], ACT.Identity,
                               bias=bqkv0[:, 2, bass.ds(n, 1)]).then_inc(sem("v_ev"), 1)

            if valid(i + 1, N0):
                n = i + 1
                for qi in QORDER:
                    wait(act, "nmax", of_tile(n + 1, qi))
                    wait(act, "w", of_tile(n, qi))
                    act.activation(ex[:, qi, ROW[qi]], sabs[:, qi, ROW[qi]], ACT.Exp,
                                   bias=nmax[:, qi:qi + 1]).then_inc(sem("ex"), 1)
            if valid(i, N0):
                n = i
                wait(act, "pv", n + 1)
                wait(act, "o", n)
                act.activation(z0[0][:, :], ps[:, 7, :], ACT.Copy).then_inc(sem("z_hi"), 1)
            if valid(i + 1, N0):
                n = i + 1
                wait(act, "vt_ps", n + 1)
                wait(act, "pv", n)
                act.activation(v0[0][:, :], ps[:, 4, :], ACT.Copy).then_inc(sem("v_hi"), 1)
            if valid(i + 2, N0):
                n = i + 2
                wait(act, "wv_ld", 16 * (n + 1))
                wait(act, "v_ps", n)
                act.activation(wv[0][:, :, :], wv_raw[:, :, :], ACT.Copy).then_inc(sem("wv_hi"), 1)
        def a0_dve(dve, i):
            def rotated(t):
                n = i + 2
                wait(dve, "q_cos", of_pair(n + 1, t))
                wait(dve, "q_sin", of_pair(n + 1, t))
                wait(dve, "qk_lo", of_pair(n, t))
                dve.tensor_tensor(q_rot[:, t, :], q_cos[:, t, :], q_sin[:, t, :], ALU.add).then_inc(sem("q_rot"), 1)
                wait(dve, "q_rot", of_pair(n + 1, t))
                wait(dve, "s", QT * n)
                dve.tensor_copy(qk[0][:, t, :], q_rot[:, t, :]).then_inc(sem("qk_hi"), 1)

            if valid(i + 2, N0):
                n = i + 2
                for t in range(2):
                    wait(dve, "q_ev", of_pair(n + 1, t))
                    wait(dve, "q_rot", of_pair(n, t))
                    dve.tensor_tensor(q_cos[:, t, :], q_in[:, t, :], cos0[:, :], ALU.mult).then_inc(sem("q_cos"), 1)
            if valid(i, N0):
                n = i
                for g, js in enumerate(TGROUP):
                    wait(dve, "wT_hi", of_group(n + 1, g))
                    for j in js:
                        bank, col = TSPOT[j]
                        last = dve.tensor_tensor(wT[1][:, j, j * P:S], ps[:, bank, col:col + S - j * P],
                                                 fp(wT[0][:, j, j * P:S]), ALU.subtract)
                    last.then_inc(sem("wT_lo"), 1)

            if valid(i + 1, N0):
                n = i + 1
                wait(dve, "causal", 2 * n + 1)
                for qi in QORDER:
                    dve.tensor_reduce(nmax[:, qi:qi + 1], sabs[:, qi, ROW[qi]], AX.X, ALU.max,
                                      negate=True).then_inc(sem("nmax"), 1)
            if valid(i + 2, N0):
                rotated(0)
            if valid(i + 2, N0):
                rotated(1)
            if valid(i, N0):
                n = i
                wait(dve, "z_hi", n + 1)
                dve.tensor_tensor(z0[1][:, :], ps[:, 7, :], fp(z0[0][:, :]), ALU.subtract).then_inc(sem("z_lo"), 1)
            if valid(i + 1, N0):
                n = i + 1
                wait(dve, "v_hi", n + 1)
                dve.tensor_tensor(v0[1][:, :], ps[:, 4, :], fp(v0[0][:, :]), ALU.subtract).then_inc(sem("v_lo"), 1)
            if valid(i + 1, N0):
                n = i + 1
                wait(dve, "causal", 2 * n + 2)
                for qi in QORDER:
                    wait(dve, "ex", of_tile(n + 1, qi))
                    dve.scalar_tensor_tensor(out=ex[:, qi, ROW[qi]], in0=sgn[:, par(1), qi, ROW[qi]], scalar=0.0,
                                             in1=ex[:, qi, ROW[qi]], op0=ALU.not_equal, op1=ALU.mult,
                                             accum_out=den[:, qi:qi + 1]).then_inc(sem("den"), 1)
                wait(dve, "den", 4 * n + 4)
                dve.tensor_scalar(dene[:, :], den[:, :], 1e-6, None, ALU.add).then_inc(sem("dene"), 1)
                wait(dve, "dene", n + 1)
                dve.reciprocal(rden[:, :], dene[:, :]).then_inc(sem("rden"), 1)
            if valid(i + 1, N0):
                n = i + 1
                wait(dve, "rden", n + 1)
                wait(dve, "wT_ps", 3 * n)
                for qi in QORDER:
                    dve.scalar_tensor_tensor(out=w[:, qi, ROW[qi]], in0=ex[:, qi, ROW[qi]], scalar=rden[:, qi:qi + 1],
                                             in1=sgn[:, par(1), qi, ROW[qi]], op0=ALU.mult, op1=ALU.mult).then_inc(sem("w"), 1)
        def a0_pool(pool, i):
            if valid(i + 3, N0):
                n = i + 3
                wait(pool, "wqk_hi", n + 1)
                pool.tensor_tensor(wqk[1][:, :, :, :], wqk_raw[:, :, :, :], fp(wqk[0][:, :, :, :]),
                                   ALU.subtract).then_inc(sem("wqk_lo"), 1)
            if valid(i + 1, N0):
                n = i + 1
                wait(pool, "sgn", QT * n + QT)
                pool.sem_inc(sem("signed"), 1)
                for t in (sabs, sgn[:, par(1)]):
                    diag = t[:, :, S - P:S]
                    pool.affine_select(out=diag, in_=diag, compare_op=ALU.is_ge, fill=0.0, base=0,
                                       pattern=[[0, QT], [-1, P]], channel_multiplier=1).then_inc(sem("causal"), 1)
            if valid(i + 2, N0):
                n = i + 2
                for t in range(2):
                    wait(pool, f"swap{t}", 32 * (n + 1))
                    wait(pool, "q_rot", of_pair(n, t))
                    pool.tensor_tensor(q_sin[:, t, :], q_sw[:, t, :], sin0[:, :], ALU.mult).then_inc(sem("q_sin"), 1)
            if valid(i, N0):
                n = i
                wait(pool, "wo_hi", n + 1)
                pool.tensor_tensor(wo[1][:, :], wo_raw[:, :], fp(wo[0][:, :]), ALU.subtract).then_inc(sem("wo_lo"), 1)
            if valid(i + 2, N0):
                n = i + 2
                for t in range(2):
                    wait(pool, "qk_hi", of_pair(n + 1, t))
                    pool.tensor_tensor(qk[1][:, t, :], q_rot[:, t, :], fp(qk[0][:, t, :]),
                                       ALU.subtract).then_inc(sem("qk_lo"), 1)
                wait(pool, "wv_hi", n + 1)
                pool.tensor_tensor(wv[1][:, :, :], wv_raw[:, :, :], fp(wv[0][:, :, :]),
                                   ALU.subtract).then_inc(sem("wv_lo"), 1)

        def a0_sp(sp, i):
            def head(n):
                return n % H0 if known(n) else n - batch[0] * H0

            if valid(i + 2, N0):
                n = i + 2
                for t in range(2):
                    wait(sp, "q_ev", of_pair(n + 1, t))
                    for o in range(2):
                        sp.dma_start(q_sw[o:P:2, t, :], q_in[1 - o:P:2, t, :]).then_inc(sem(f"swap{t}"), 16)
            if valid(i + 1, N0):
                n = i + 1
                src = a["wo0"][head(n)]
                wait(sp, "wo_lo", n)
                sp.dma_start(wo_raw[:, :], src).then_inc(sem("wo_ld"), 16)
            if valid(i + 4, N0):
                n = i + 4
                src = a["wqk0"][head(n)]
                wait(sp, "wqk_lo", n)
                sp.dma_start(wqk_raw[:, :, :, :], src).then_inc(sem("wqk_ld"), 16)
            if valid(i + 3, N0):
                n = i + 3
                src = a["wv0"][head(n)]
                wait(sp, "wv_lo", n)
                sp.dma_start(wv_raw[:, :, :], src).then_inc(sem("wv_ld"), 16)

        batch = [0]
        odd = [0]
        LOOPS0 = {1: (H0 - 6, 0), H0 + 1: (N0 - 6, 1)}

        def par(ahead):
            return (odd[0] + ahead) % 2

        def a0_steps(eng, step, at=None):
            i = -4
            while i <= N0:
                if i in LOOPS0:
                    last, batch[0] = LOOPS0[i]
                    with eng.Fori(i // 2, last // 2) as r:
                        for k in range(2):
                            odd[0] = 1 - k
                            step(eng, 2 * r + 1 + k)
                    i = last + 1
                else:
                    odd[0] = i % 2
                    step(eng, i)
                    if at and i in (H0, N0):
                        at(eng, i // H0 - 1)
                    i += 1

        def a0_zero_pe(pe, b):
            if b == 0:
                pe.wait_ge(sem("zero"), 1)
            else:
                pe.wait_ge(sem("x_add"), 2 * b)
            for c in range(DC):
                pe.matmul(ps[:, c, :], zero_r[:, 0:P], zero_r[:, :], start=True, stop=True, skip_group_check=True)

        def a0_end_pe(pe, b):
            back_pe(pe, "aT", 2 * b + 2, (0, 1), range(QT * b, QT * b + QT))
            if b == 0:
                a0_zero_pe(pe, 1)

        def a0_end_act(act, b):
            act.wait_ge(sem("o"), H0 * (b + 1))
            for c in range(DC):
                act.activation(aT[:, c, b * S:(b + 1) * S], ps[:, c, :], ACT.Identity,
                               bias=bo0[:, c:c + 1]).then_inc(sem("aT"), 1)

        def a0_end_dve(dve, b):
            back_dve(dve, 2 * b, (0, 1), range(QT * b, QT * b + QT))

        M = E + 1
        PAIR_LOOP = (1, (M - 3) // 2)
        GATE_UP = slice(0, 2 * D)
        DOWN = slice(2 * D, 3 * D)
        PER_LAYER = {"gw_ld": 16, "ebias_ld": 48, "ew_ld_0": 16 * (M + 1) // 2, "ew_ld_1": 16 * (M // 2),
                     "cwb_0": 16 * (E // 2), "cwb_1": 16 * (E // 2), "cw_st": 16, "cwT": 2, "cwT_ps": NT, "gu": 2 * E, "gu_ps": 4 * M}
        ONCE = ("gw_hi", "gw_lo", "logits", "score", "cw")
        TWICE = ("guw", "hid_hi", "hid_lo", "y", "silu")

        def wait_f(eng, f, name, value):
            if not known(value) or value > 0:
                eng.wait_ge(sem(name), value + f * PER_LAYER.get(name, 1 if name in ONCE else 2 * M if name in TWICE else M))

        def ffn_steps(eng, step):
            for m in range(2):
                step(m, 0, m)
            with eng.Fori(*PAIR_LOOP) as r:
                for p in range(2):
                    step(2 * r + p, r, p)
            for m in range(2 * PAIR_LOOP[1], M + 1):
                step(m, m // 2, m % 2)

        def of_half(m, h):
            return 2 * (m - 1) + h + 1

        def half_of(t, h):
            return t[:, h * S:(h + 1) * S]

        def ffn_sp(sp, f):
            if f:
                sp.wait_ge(sem("x_add"), 12)
            sp.dma_start(gw_raw[:, :, :], a[f"gw{f}"]).then_inc(sem("gw_ld"), 16)
            sp.dma_start(ebias[:, :], a[f"ebias{f}"].partition_broadcast(P)).then_inc(sem("ebias_ld"), 16)
            sp.dma_start(lower16[:, :], a["lower16"].partition_broadcast(P)).then_inc(sem("ebias_ld"), 16)
            sp.dma_start(lower4[:, :], a["lower4"].partition_broadcast(P)).then_inc(sem("ebias_ld"), 16)
            for m in range(2):
                sp.dma_start(ew_raw[:, m, :], a[f"ew{f}"][m]).then_inc(sem(f"ew_ld_{m}"), 16)

        def ffn_sp_run(sp, f):
            wait_f(sp, f, "cwT", 2)
            sp.dma_start(cw_dram[f], cwT[:, :]).then_inc(sem("cw_st"), 16)
            wait_f(sp, f, "cw_st", 16)

            def step(m, k, p):
                if not known(m) or m + 1 < M:
                    src = cw_dram[f][bass.ds(m, 1), :].rearrange("e t -> (e t)").partition_broadcast(P)
                    wait_f(sp, f, "guw", 2 * m)
                    sp.dma_start(cwb[:, 1 - p, :], src).then_inc(sem(f"cwb_{1 - p}"), 16)
                if not known(m) or m + 2 < M:
                    src = a[f"ew{f}"][m + 2]
                    wait_f(sp, f, "down_lo", m + 1)
                    sp.dma_start(ew_raw[:, p, :], src).then_inc(sem(f"ew_ld_{p}"), 16)

            ffn_steps(sp, step)

        def ffn_pe(pe, f):
            wait_f(pe, f, "gw_lo", 1)
            pe.wait_ge(sem("xT_lo"), 2 * DC * (2 * f + 2))
            for t in range(NT):
                for j in range(3 * DC):
                    c, (pw, px) = j // 3, PARTS[j % 3]
                    last = pe.matmul(ps[:, 2, t * E:(t + 1) * E], (xT_hi, xT_lo)[px][:, c, t * P:(t + 1) * P],
                                     gw[pw][:, c, :], start=j == 0, stop=j == 3 * DC - 1)
            last.then_inc(sem("logits"), 1)

            def gate_up(m, p, h):
                if h == 0:
                    wait_f(pe, f, "gate_lo", m + 1)
                if known(m) and m == 1:
                    wait_f(pe, f, "guw", of_half(1, h))
                else:
                    wait_f(pe, f, "gu", of_half(m - 1, h))
                for u in range(2):
                    for j in range(3 * DC):
                        c, (pw, px) = j // 3, PARTS[j % 3]
                        col = (u * DC + c) * P
                        last = pe.matmul(ps[:, 4 + 2 * h + u, :], ew[pw][:, p, col:col + P],
                                         half_of((xT_hi, xT_lo)[px][:, c, :], h), start=j == 0, stop=j == 3 * DC - 1)
                    last.then_inc(sem("gu_ps"), 1)

            def down(m, p, h):
                if h == 0:
                    wait_f(pe, f, "down_lo", m + 1)
                wait_f(pe, f, "hid_lo", of_half(m + 1, h))
                first, end = known(m) and m == 0, known(m) and m == M - 1
                for c in range(DC):
                    for j, (pw, px) in enumerate(PARTS):
                        col = DOWN.start + c * P
                        last = pe.matmul(ps[:, 2 * h + c, :], ew[pw][:, p, col:col + P], hid[px][:, h, :],
                                         start=first and j == 0, stop=end and j == 2, skip_group_check=True)
                last.then_inc(sem("y"), 1)

            def step(m, k, p):
                for h in range(2):
                    if not known(m) or m < M:
                        gate_up(m, p, h)
                    if known(m) and m == 1 and h == 1:
                        wait_f(pe, f, "cw", 1)
                        for t in range(NT):
                            pe.transpose(ps[0:E, 2 + t // QT, t % QT * P:(t % QT + 1) * P], cw[:, t, :],
                                         ident[:, :]).then_inc(sem("cwT_ps"), 1)
                        wait_f(pe, f, "cwT", 2)
                    if not known(m) or m > 0:
                        down(m - 1, 1 - p, h)

            ffn_steps(pe, step)
            for h in range(2):
                back_pe(pe, "aT", 8 * f + 6 + 2 * h, (4 + 2 * h, 5 + 2 * h), range(QT * h, QT * h + QT))

        def ffn_act(act, f):
            wait_f(act, f, "logits", 1)
            act.activation(score[:, :, :].rearrange("p t e -> p (t e)"), ps[:, 2, 0:NT * E],
                           ACT.Sigmoid).then_inc(sem("score"), 1)

            def gate(m, h):
                wait_f(act, f, "gu_ps", 4 * m + 2 * h + 1)
                if known(m) and m == 1:
                    wait_f(act, f, "guw", of_half(1, h))
                else:
                    wait_f(act, f, "gu", of_half(m - 1, h))
                act.activation(silu[:, h, :], ps[:, 4 + 2 * h, :], ACT.Silu).then_inc(sem("silu"), 1)

            def hidden(m, h):
                wait_f(act, f, "guw", of_half(m + 1, h))
                wait_f(act, f, "y", of_half(m, h))
                act.activation(hid[0][:, h, :], guw[:, h, :], ACT.Copy).then_inc(sem("hid_hi"), 1)

            def step(m, k, p):
                runs = not known(m) or m < M
                if runs:
                    gate(m, 0)
                if not known(m) or m > 0:
                    hidden(m - 1, 1)
                if runs:
                    gate(m, 1)
                    hidden(m, 0)

            ffn_steps(act, step)
            for h in range(2):
                wait_f(act, f, "y", of_half(M, h))
                for c in range(DC):
                    act.activation(half_of(aT[:, c, :], h), ps[:, 2 * h + c, :], ACT.Copy).then_inc(sem("aT"), 1)

        def ffn_pool(pool, f):
            wait_f(pool, f, "gw_hi", 1)
            pool.tensor_tensor(gw[1][:, :, :], gw_raw[:, :, :], fp(gw[0][:, :, :]), ALU.subtract).then_inc(sem("gw_lo"), 1)

            def low(m, p, part, cols):
                wait_f(pool, f, f"{part}_hi", m + 1)
                pool.tensor_tensor(ew[1][:, p, cols], ew_raw[:, p, cols], fp(ew[0][:, p, cols]),
                                   ALU.subtract).then_inc(sem(f"{part}_lo"), 1)

            def weighted(m, k, p, h):
                if h == 0:
                    wait_f(pool, f, f"cwb_{p}", 16 * (k + p))
                wait_f(pool, f, "gu", of_half(m, h))
                wait_f(pool, f, "hid_lo", of_half(m, h))
                pool.tensor_tensor(guw[:, h, :], gu[:, h, :], half_of(cwb[:, p, :], h),
                                   ALU.mult).then_inc(sem("guw"), 1)

            def step(m, k, p):
                if known(m) and m == 0:
                    low(0, 0, "gate", GATE_UP)
                if known(m) and m == M:
                    return
                routed = not known(m) or m > 0
                if routed:
                    weighted(m, k, p, 0)
                if not known(m) or m + 1 < M:
                    low(m + 1, 1 - p, "gate", GATE_UP)
                if routed:
                    weighted(m, k, p, 1)
                low(m, p, "down", DOWN)

            ffn_steps(pool, step)

        def ffn_dve(dve, f):
            def high(m, k, p, part, cols):
                if part == "gate":
                    wait_f(dve, f, f"ew_ld_{p}", 16 * (k + 1))
                    wait_f(dve, f, "gu_ps", 4 * (m - 1))
                else:
                    wait_f(dve, f, "y", 2 * (m - 1))
                dve.tensor_copy(ew[0][:, p, cols], ew_raw[:, p, cols]).then_inc(sem(f"{part}_hi"), 1)

            def gated(m, h):
                wait_f(dve, f, "silu", of_half(m + 1, h))
                wait_f(dve, f, "gu_ps", 4 * m + 2 * h + 2)
                if known(m) and m == 0:
                    dve.tensor_tensor(guw[:, h, :], silu[:, h, :], ps[:, 5 + 2 * h, :], ALU.mult).then_inc(sem("guw"), 1)
                else:
                    if not known(m) or m > 1:
                        wait_f(dve, f, "guw", of_half(m, h))
                    dve.tensor_tensor(gu[:, h, :], silu[:, h, :], ps[:, 5 + 2 * h, :], ALU.mult).then_inc(sem("gu"), 1)

            def hidden(m, h):
                wait_f(dve, f, "hid_hi", of_half(m + 1, h))
                dve.tensor_tensor(hid[1][:, h, :], guw[:, h, :], fp(hid[0][:, h, :]), ALU.subtract).then_inc(sem("hid_lo"), 1)

            def step(m, k, p):
                if known(m) and m == 0:
                    high(0, 0, 0, "gate", GATE_UP)
                runs = not known(m) or m < M
                if runs:
                    gated(m, 0)
                if not known(m) or m > 0:
                    hidden(m - 1, 1)
                if not known(m) or m + 1 < M:
                    high(m + 1, k + p, 1 - p, "gate", GATE_UP)
                if runs:
                    gated(m, 1)
                    high(m, k, p, "down", DOWN)
                    hidden(m, 0)
                if known(m) and m == 0:
                    ffn_route(dve, f)

            wait_f(dve, f, "gw_ld", 16)
            dve.tensor_copy(gw[0][:, :, :], gw_raw[:, :, :]).then_inc(sem("gw_hi"), 1)
            ffn_steps(dve, step)
            for h in range(2):
                back_dve(dve, 8 * f + 4 + 2 * h, (4 + 2 * h, 5 + 2 * h), range(QT * h, QT * h + QT))

        def ffn_route(dve, f):
            done = [0]

            def then(ins):
                ins.then_inc(sem(f"route{f}"), 1)
                done[0] += 1

            def prev():
                dve.wait_ge(sem(f"route{f}"), done[0])

            def ranked(count, n, value, gt, eq, lower, rank):
                of_j = value.unsqueeze(2).broadcast_to([P, count, n, n])
                of_i = value.unsqueeze(3).broadcast_to([P, count, n, n])
                sq = [v.rearrange("p t (i j) -> p t i j", i=n) for v in (gt, eq)]
                then(dve.tensor_tensor(sq[0], of_j, of_i, ALU.is_gt))
                then(dve.tensor_tensor(sq[1], of_j, of_i, ALU.is_equal))
                prev()
                then(dve.tensor_tensor(eq, eq, lower.unsqueeze(1).broadcast_to([P, count, n * n]), ALU.mult))
                prev()
                then(dve.tensor_tensor(gt, gt, eq, ALU.add))
                prev()
                then(dve.tensor_reduce(rank.rearrange("p (t i) -> p t i", i=n), sq[0], AX.X, ALU.add))
                prev()

            wait_f(dve, f, "ebias_ld", 48)
            wait_f(dve, f, "score", 1)
            then(dve.tensor_tensor(biased[:, :, :], score[:, :, :], ebias[:, :].unsqueeze(1).broadcast_to([P, NT, E]), ALU.add))
            prev()
            value = biased
            if f == 0:
                grp = biased[:, :, :].rearrange("p t (g i) -> p (t g) i", i=GSIZE)
                for col, gap in ((0, 1), (3, 2), (5, 3)):
                    n = GSIZE - gap
                    then(dve.tensor_tensor(pairsum[:, :, col:col + n], grp[:, :, 0:n], grp[:, :, gap:GSIZE], ALU.add))
                prev()
                then(dve.tensor_reduce(gscore[:, :, :].rearrange("p t g -> p (t g)"), pairsum[:, :, :], AX.X, ALU.max))
                prev()
                ranked(NT, GROUPS, gscore[:, :, :], ggt[:, :, :], geq[:, :, :], lower4[:, :], grank[:, :])
                then(dve.tensor_scalar(gkeep[:, :], grank[:, :], float(GROUP_KEEP), None, ALU.is_lt))
                prev()
                then(dve.tensor_scalar(gpen[:, :], gkeep[:, :], BIG, -BIG, ALU.mult, ALU.add))
                msk = masked[:, :, :].rearrange("p t (g i) -> p (t g) i", i=GSIZE)
                over = [P, NT * GROUPS, GSIZE]
                then(dve.tensor_tensor(msk, grp, gkeep[:, :].unsqueeze(2).broadcast_to(over), ALU.mult))
                prev()
                then(dve.tensor_tensor(msk, msk, gpen[:, :].unsqueeze(2).broadcast_to(over), ALU.add))
                prev()
                value = masked
            ranked(NT, E, value[:, :, :], egt, eeq, lower16[:, :], erank[:, :])
            then(dve.tensor_scalar(chosen[:, :, :].rearrange("p t e -> p (t e)"), erank[:, :], float(TOPK), None, ALU.is_lt))
            prev()
            then(dve.tensor_tensor(chosen[:, :, :], chosen[:, :, :], score[:, :, :], ALU.mult))
            prev()
            then(dve.tensor_reduce(wsum[:, :], chosen[:, :, :], AX.X, ALU.add))
            prev()
            then(dve.tensor_scalar(wsume[:, :], wsum[:, :], RENORM_EPS[f], None, ALU.add))
            prev()
            then(dve.reciprocal(wrec[:, :], wsume[:, :]))
            prev()
            dve.scalar_tensor_tensor(out=cw[:, :, :], in0=chosen[:, :, :], scalar=ROUTE_SCALE[f],
                                     in1=wrec[:, :].unsqueeze(2).broadcast_to([P, NT, E]),
                                     op0=ALU.mult, op1=ALU.mult).then_inc(sem("cw"), 1)
            for k in range(2):
                wait_f(dve, f, "cwT_ps", NT)
                dve.tensor_copy(half_of(cwT, k), ps[0:E, 2 + k, :]).then_inc(sem("cwT"), 1)

        GROUPS1 = [(t, mt, h) for t in range(2) for mt in range(DC) for h in range(2)]
        AHEAD = 2
        PASS1 = range(4)
        LO_DVE = 576

        def a1_pairs(eng, step):
            for b in range(B):
                with eng.Fori(0, PAIRS // 2) as r:
                    for p in range(2):
                        step(b, 2 * r + p, b * PAIRS + 2 * r + p, b * (PAIRS // 2) + r, p)

        def a1_sp(sp):
            sp.wait_ge(sem("x_add"), 4)
            for part in range(6):
                sp.dma_start(w1_raw[:, part, :, :], a["w1"][:, part]).then_inc(sem(f"w1_ld{part // 3}"), 16)
            for dst, name in ((cos1, "cos1"), (sin1, "sin1"), (bo1, "bo1")):
                sp.dma_start(dst[:, :], a[name]).then_inc(sem("tab1"), 16)
            sp.dma_start(b1[:, :, :], a["b1"]).then_inc(sem("tab1"), 16)
            sp.dma_start(bv1[:, :], a["bv1"].partition_broadcast(P)).then_inc(sem("tab1"), 16)
            for g, (t, mt, h) in enumerate(GROUPS1):
                rows = stk_dram[t].rearrange("(h r) t -> h r t", r=STK)[mt * H1 // 2:(mt + 1) * H1 // 2]
                for part in range(2):
                    sp.wait_ge(sem(f"qk1_{part}"), g + 1)
                    for j in range(3):
                        if PARTS[j][t] == part:
                            sp.dma_start(rows[:, j * DH1:(j + 1) * DH1, h * S:(h + 1) * S],
                                         fp(qk1[part][:, t, mt, h * S:(h + 1) * S])).then_inc(sem("stk_st"), 16)

            def stage(phase):
                def step(b, pair, n, turn, p):
                    src = [stk_dram[t][bass.ds(pair * P, P), b * S:(b + 1) * S] for t in range(2)]
                    if phase == 0:
                        wait(sp, "s1", 2 * n + 2)
                    else:
                        wait(sp, "st_ps", 4 * n + 4)
                    sp.dma_start(fp(qs[:, p, :]), src[0]).then_inc(sem(f"stage_ld{p}"), 16)
                    sp.dma_start(fp(ks[:, p, :]), src[1]).then_inc(sem(f"stage_ld{p}"), 16)
                return step

            sp.wait_ge(sem("ones_st"), 16 * 8)
            sp.wait_ge(sem("stk_st"), 16 * 24)
            a1_pairs(sp, stage(0))
            for part in range(2):
                sp.wait_ge(sem(f"nmT_{part}"), 1)
                for b in range(B):
                    rows = stk_dram[0].rearrange("(h r) (b i q) -> r b h i q", r=STK, b=B, q=P)
                    sp.dma_start(rows[ROWS_S + part, b], fp(nmT[part][b * P // 2:(b + 1) * P // 2, :])).then_inc(sem("nm_st"), 16)
            sp.wait_ge(sem("nm_st"), 16 * 4)
            a1_pairs(sp, stage(1))

            sp.wait_ge(sem("z_st0"), 16 * N1 // 2)
            sp.wait_ge(sem("z_st1"), 16 * N1 // 2)
            z_rows = z_dram.rearrange("n p t -> (n p) t").rearrange("(b h r) t -> b h r t", b=B, r=STK)
            sp.dma_start(den1[:, :], z_dram.rearrange("n p t -> (n p) t").rearrange("(h r) (i q) -> r h i q", r=STK, q=P)[2 * DH1]
                         ).then_inc(sem("den1_ld"), 16)
            for h in range(B):
                for mt in range(DC):
                    for part, dst in ((0, zh1), (1, zl1)):
                        sp.dma_start(dst[:, mt, h * S:(h + 1) * S],
                                     z_rows[h, mt * H1 // 2:(mt + 1) * H1 // 2, part * DH1:(part + 1) * DH1, :]
                                     ).then_inc(sem(f"z_ld{h}"), 16)
            sp.wait_ge(sem("rden1"), 1)
            sp.dma_start(rd_dram, rden1[:, :]).then_inc(sem("rd_st"), 16)
            sp.wait_ge(sem("rd_st"), 16)
            rd_rows = rd_dram.rearrange("(b h i) q -> b h (i q)", b=B, i=QT)
            for h in range(B):
                for mt in range(DC):
                    src = rd_rows[h, mt * H1 // 2:(mt + 1) * H1 // 2].unsqueeze(1).broadcast_to([H1 // 2, DH1, S])
                    sp.dma_start(rd1[:, mt, h * S:(h + 1) * S], src).then_inc(sem(f"rd_ld{h}"), 16)

        def a1_pe(pe):
            pe.sem_inc(sem("s1"), 2 * AHEAD)
            pe.sem_inc(sem("st_ps"), 4 * AHEAD)
            pe.sem_inc(sem("pv1"), 2)
            pe.wait_ge(sem("xT_lo"), 2 * DC * 3)
            for g, (t, mt, h) in enumerate(GROUPS1):
                wait(pe, "w1_lo", 2 * t + 2)
                wait(pe, "rs", 2 * (g - 3))
                for sw in range(2):
                    for j in range(3 * DC):
                        c, (pw, px) = j // 3, PARTS[j % 3]
                        last = pe.matmul(ps[:, 2 * (g % 4) + sw, :], w1[pw][:, 2 * t + sw, c, mt * P:(mt + 1) * P],
                                         half_of((xT_hi, xT_lo)[px][:, c, :], h), start=j == 0, stop=j == 3 * DC - 1)
                    last.then_inc(sem("qk1_ps"), 1)
            pe.wait_ge(sem("w1_lo"), 5)
            for v in range(NT // 2):
                pe.wait_ge(sem("rs"), 2 * (5 + v // 2))
                for t2 in range(2):
                    t = 2 * v + t2
                    for j in range(3 * DC):
                        c, (pw, px) = j // 3, PARTS[j % 3]
                        last = pe.matmul(ps[:, v, t2 * D:(t2 + 1) * D], (xT_hi, xT_lo)[px][:, c, t * P:(t + 1) * P],
                                         w1[pw][:, 4, c, :], start=j == 0, stop=j == 3 * DC - 1)
                last.then_inc(sem("v1_ps"), 1)
            pe.wait_ge(sem("rs"), 16)
            pe.wait_ge(sem("v1"), NT // 2)

            def maxima(b, pair, n, turn, p):
                wait(pe, f"stage_ld{p}", 32 * (turn + 1))
                wait(pe, "max_free", 2 * n + 2)
                for qi in range(QT):
                    for hd in range(2):
                        rows = slice(hd * STK, hd * STK + ROWS_S)
                        mm = pe.matmul(ps[:, 4 * hd + qi, :], qs[rows, p, qi * P:(qi + 1) * P], ks[rows, p, :],
                                       start=True, stop=True)
                        if qi == QT - 1:
                            mm.then_inc(sem("s1"), 1)

            a1_pairs(pe, maxima)
            pe.wait_ge(sem("max_free"), 2 * N1 + 2)
            pe.transpose(ps[:, 6, 0:P], nm1[:, :], ident[:, :]).then_inc(sem("nmT_ps"), 1)

            def scores(n, turn, p, c):
                hd, slot = c // 2, c % 2
                if c == 0:
                    wait(pe, f"stage_ld{p}", 32 * (N1 // 2 + turn + 1))
                wait(pe, "st_free", 4 * n + c + 1)
                rows = slice(hd * STK, hd * STK + ROWS_M)
                for kk in range(2):
                    kt = 2 * slot + kk
                    last = pe.matmul(ps[:, 2 * slot + kk, :], ks[rows, p, kt * P:(kt + 1) * P], qs[rows, p, :],
                                     start=True, stop=True)
                last.then_inc(sem("st_ps"), 1)

            def pv(n, p, c):
                hd, slot = c // 2, c % 2
                if c == 0:
                    wait(pe, "vs", n + 1)
                    wait(pe, "zev_free", n + 1)
                wait(pe, "p_lo_dve", 4 * n + c + 1)
                wait(pe, "p_lo_pool", 4 * n + c + 1)
                for kk in range(2):
                    kt = 2 * slot + kk
                    for part in range(2):
                        last = pe.matmul(ps[:, 4 + p, :], vs[:, p, kt, hd, :], p1[part][:, slot, kk * S:(kk + 1) * S],
                                         start=c == 0 and kk == 0 and part == 0, stop=c == 3 and kk == 1 and part == 1,
                                         skip_group_check=True)
                last.then_inc(sem("pv1"), 1)

            def step(n, turn, p, more=True):
                for c in PASS1:
                    if c < 3:
                        scores(n, turn, p, c + 1)
                    elif more:
                        scores(n + 1, turn + p, 1 - p, 0)
                    pv(n, p, c)

            scores(0, 0, 0, 0)
            with pe.Fori(0, N1 // 2 - 1) as r:
                for p in range(2):
                    step(2 * r + p, r, p)
            for p in range(2):
                step(N1 - 2 + p, N1 // 2 - 1, p, more=p == 0)

            pe.wait_ge(sem("w1_lo"), 6)
            for h in range(B):
                pe.wait_ge(sem("zc_lo"), DC * (h + 1))
                for m in range(DC):
                    for j in range(3 * DC):
                        c, (pw, pz) = j // 3, PARTS[j % 3]
                        last = pe.matmul(ps[:, 2 * h + m, :], w1[pw][:, 5, c, m * P:(m + 1) * P],
                                         half_of(p1[pz][:, c, :], h), start=j == 0, stop=j == 3 * DC - 1)
                    last.then_inc(sem("o1"), 1)
            for h in range(2):
                back_pe(pe, "aT", 10 + 2 * h, (4 + 2 * h, 5 + 2 * h), range(QT * h, QT * h + QT))

        def a1_act(act):
            act.wait_ge(sem("tab1"), 16 * 5)
            for g, (t, mt, h) in enumerate(GROUPS1):
                act.wait_ge(sem("rr"), g + 1)
                act.activation(half_of(qk1[0][:, t, mt, :], h), rr[:, g % 2, :], ACT.Copy,
                               scale=SCALE1 if t == 0 else 1.0).then_inc(sem("qk1_0"), 1)
            for v in range(NT // 2):
                act.wait_ge(sem("v1"), v + 1)
                act.activation(v1s[:, 2 * v:2 * v + 2, :, 0, :], v1[:, :, :].rearrange("p t (h d) -> p t h d", h=H1),
                               ACT.Copy).then_inc(sem("v1_hi"), 1)
            act.wait_ge(sem("nmT_ps"), 1)
            act.activation(nmT[0][:, :], ps[:, 6, 0:P], ACT.Copy).then_inc(sem("nmT_0"), 1)
            act.sem_inc(sem("st_free"), 2)
            act.sem_inc(sem("zev_free"), 2)

            def read_out(n, turn, p):
                wait(act, "pv1", 4 * n + 6)
                if not known(n) or n >= 2:
                    wait(act, f"z_st{p}", 16 * turn)
                act.activation(zst[:, p, :], ps[:, 4 + p, :], ACT.Copy).then_inc(sem("zev_free"), 1)
                wait(act, "zev_free", n + 3)
                dst = z_dram[bass.ds(n, 1)].rearrange("n p t -> (n p) t")
                act.dma_start(dst, zst[:, p, :]).then_inc(sem(f"z_st{p}"), 16)

            def step(n, turn, p):
                for c in PASS1:
                    hd, slot = c // 2, c % 2
                    wait(act, "st_ps", 4 * n + c + 1 + 4 * AHEAD)
                    wait(act, "p_lo_dve", 4 * n + c - 1)
                    wait(act, "p_lo_pool", 4 * n + c - 1)
                    act.activation(e1[:, slot, :].rearrange("p (k t) -> p k t", k=2), ps[:, 2 * slot:2 * slot + 2, :],
                                   ACT.Exp).then_inc(sem("st_free"), 1)
                    if c == 1 and (not known(n) or n > 0):
                        read_out(n - 1, turn - 1 + p, 1 - p)

            for p in range(2):
                step(p, 0, p)
            with act.Fori(1, N1 // 2) as r:
                for p in range(2):
                    step(2 * r + p, r, p)
            read_out(N1 - 1, N1 // 2 - 1, 1)

            for h in range(B):
                for c in range(DC):
                    act.wait_ge(sem("zn"), DC * h + c + 1)
                    act.activation(half_of(p1[0][:, c, :], h), half_of(zh1[:, c, :], h), ACT.Copy).then_inc(sem("zc_hi"), 1)
            for h in range(B):
                for m in range(DC):
                    act.wait_ge(sem("o1"), DC * h + m + 1)
                    act.activation(half_of(aT[:, m, :], h), ps[:, 2 * h + m, :], ACT.Identity,
                                   bias=bo1[:, m:m + 1]).then_inc(sem("aT"), 1)

        def a1_pool(pool):
            pool.wait_ge(sem("x_add"), 8)
            pool.memset(vs[:, :, :, :, :].bitcast(F32), 0.0).then_inc(sem("vs_zero"), 1)
            pool.wait_ge(sem("vs_zero"), 1)
            for hd in range(2):
                for p in range(2):
                    pool.memset(vs[:, p, :, hd, hd * STK + 2 * DH1:hd * STK + 3 * DH1].bitcast(F32), 1.0).then_inc(sem("vs_one"), 1)
            for part in range(6):
                pool.wait_ge(sem("w1_hi"), part + 1)
                pool.tensor_tensor(w1[1][:, part, :, :], w1_raw[:, part, :, :], fp(w1[0][:, part, :, :]),
                                   ALU.subtract).then_inc(sem("w1_lo"), 1)
            for g in range(len(GROUPS1)):
                pool.wait_ge(sem("rs"), 2 * (g + 1))
                wait(pool, "qk1_1", g - 1)
                pool.tensor_tensor(rr[:, g % 2, :], rc[:, g % 2, :], rs[:, g % 2, :], ALU.add).then_inc(sem("rr"), 1)

            def step(b, pair, n, turn, p):
                for c in PASS1:
                    hd, slot = c // 2, c % 2
                    wait(pool, "p_hi", 4 * n + c + 1)
                    pool.tensor_tensor(p1[1][:, slot, LO_DVE:], e1[:, slot, LO_DVE:], fp(p1[0][:, slot, LO_DVE:]),
                                       ALU.subtract).then_inc(sem("p_lo_pool"), 1)

            a1_pairs(pool, step)

        def a1_dve(dve):
            for part in range(6):
                dve.wait_ge(sem(f"w1_ld{part // 3}"), 48)
                dve.tensor_copy(w1[0][:, part, :, :], w1_raw[:, part, :, :]).then_inc(sem("w1_hi"), 1)
            dve.wait_ge(sem("tab1"), 16 * 5)

            def low(g):
                t, mt, h = GROUPS1[g]
                dve.wait_ge(sem("qk1_0"), g + 1)
                dve.scalar_tensor_tensor(out=half_of(qk1[1][:, t, mt, :], h), in0=rr[:, g % 2, :],
                                         scalar=SCALE1 if t == 0 else 1.0, in1=fp(half_of(qk1[0][:, t, mt, :], h)),
                                         op0=ALU.mult, op1=ALU.subtract).then_inc(sem("qk1_1"), 1)

            for g, (t, mt, h) in enumerate(GROUPS1):
                for sw, (dst, table, name) in enumerate(((rc, cos1, "rs"), (rs, sin1, "rs"))):
                    dve.wait_ge(sem("qk1_ps"), 2 * g + sw + 1)
                    wait(dve, "rr", g - 1)
                    dve.scalar_tensor_tensor(out=dst[:, g % 2, :], in0=ps[:, 2 * (g % 4) + sw, :],
                                             scalar=b1[:, 2 * t + sw, mt:mt + 1], in1=table[:, :],
                                             op0=ALU.add, op1=ALU.mult).then_inc(sem(name), 1)
                if g:
                    low(g - 1)
            low(len(GROUPS1) - 1)
            for v in range(NT // 2):
                dve.wait_ge(sem("v1_ps"), v + 1)
                wait(dve, "v1_lo", v)
                dve.tensor_tensor(v1[:, :, :], ps[:, v, :].rearrange("p (t d) -> p t d", t=2),
                                  bv1[:, :].unsqueeze(1).broadcast_to([P, 2, D]), ALU.add).then_inc(sem("v1"), 1)
                dve.wait_ge(sem("v1_hi"), v + 1)
                dve.tensor_tensor(v1s[:, 2 * v:2 * v + 2, :, 1, :], v1[:, :, :].rearrange("p t (h d) -> p t h d", h=H1),
                                  fp(v1s[:, 2 * v:2 * v + 2, :, 0, :]), ALU.subtract).then_inc(sem("v1_lo"), 1)
            dve.sem_inc(sem("max_free"), 2)

            def maxima(b, pair, n, turn, p):
                for hd in range(2):
                    col = n * 8 + 4 * hd
                    wait(dve, "s1", 2 * n + hd + 1 + 2 * AHEAD)
                    dve.sem_inc(sem("max_go"), 1)
                    dve.tensor_reduce(nm1[:, bass.ds(col, QT)], ps[:, 4 * hd:4 * hd + QT, :], AX.X, ALU.max,
                                      negate=True).then_inc(sem("max_free"), 1)

            a1_pairs(dve, maxima)
            dve.wait_ge(sem("nmT_0"), 1)
            dve.tensor_tensor(nmT[1][:, :], ps[:, 6, 0:P], fp(nmT[0][:, :]), ALU.subtract).then_inc(sem("nmT_1"), 1)
            dve.wait_ge(sem("vs_one"), 4)
            dve.wait_ge(sem("v1_lo"), NT // 2)

            def step(b, pair, n, turn, p):
                for c in PASS1:
                    hd, slot = c // 2, c % 2
                    wait(dve, "st_free", 4 * n + c + 3)
                    wait(dve, "pv1", 4 * n + c + 1)
                    dve.tensor_copy(p1[0][:, slot, :], e1[:, slot, :]).then_inc(sem("p_hi"), 1)
                    if c == 0:
                        for k in range(2):
                            src = v1s[:, b * QT:(b + 1) * QT, bass.ds(2 * pair + k, 1), :, :]
                            cp = dve.tensor_copy(vs[:, p, :, k, k * STK:k * STK + 2 * DH1],
                                                 src.rearrange("p t h u d -> p t (h u d)"))
                        cp.then_inc(sem("vs"), 1)
                    wait(dve, "p_hi", 4 * n + c + 1)
                    dve.tensor_tensor(p1[1][:, slot, 0:LO_DVE], e1[:, slot, 0:LO_DVE], fp(p1[0][:, slot, 0:LO_DVE]),
                                      ALU.subtract).then_inc(sem("p_lo_dve"), 1)

            a1_pairs(dve, step)

            dve.wait_ge(sem("den1_ld"), 16)
            dve.reciprocal(rden1[:, :], den1[:, :]).then_inc(sem("rden1"), 1)
            for h in range(B):
                dve.wait_ge(sem(f"z_ld{h}"), 16 * 4)
                for c in range(DC):
                    dve.tensor_tensor(half_of(zh1[:, c, :], h), half_of(zh1[:, c, :], h), half_of(zl1[:, c, :], h),
                                      ALU.add).then_inc(sem("zsum"), 1)
            for h in range(B):
                dve.wait_ge(sem(f"rd_ld{h}"), 16 * DC)
                dve.wait_ge(sem("zsum"), DC * B)
                for c in range(DC):
                    dve.tensor_tensor(half_of(zh1[:, c, :], h), half_of(zh1[:, c, :], h), half_of(rd1[:, c, :], h),
                                      ALU.mult).then_inc(sem("zn"), 1)
                for c in range(DC):
                    dve.wait_ge(sem("zc_hi"), DC * h + c + 1)
                    dve.tensor_tensor(half_of(p1[1][:, c, :], h), half_of(zh1[:, c, :], h), fp(half_of(p1[0][:, c, :], h)),
                                      ALU.subtract).then_inc(sem("zc_lo"), 1)
            for h in range(2):
                back_dve(dve, 8 + 2 * h, (4 + 2 * h, 5 + 2 * h), range(QT * h, QT * h + QT))

        block = es.enter_context(nc.Block())

        @block.sync
        def _(sp):
            sp.dma_start(x[:, :, :], a["x"].rearrange("(t p) d -> p t d", p=P)).then_inc(sem("x_ld"), 16)
            sp.dma_start(ident[:, :], a["ident"]).then_inc(sem("ident"), 16)
            for dst, name in ((cos0, "cos0"), (sin0, "sin0"), (bo0, "bo0")):
                sp.dma_start(dst[:, :], a[name]).then_inc(sem("tab0"), 16)
            sp.dma_start(bqkv0[:, :, :], a["bqkv0"]).then_inc(sem("tab0"), 16)
            sp.wait_ge(sem("ones"), 1)
            for t in range(2):
                rows = stk_dram[t].rearrange("(h r) t -> h r t", r=STK)
                for g in range(DC):
                    for h in range(B):
                        sp.dma_start(rows[g * H1 // 2:(g + 1) * H1 // 2, ROWS_S:STK, h * S:(h + 1) * S],
                                     fp(ones_r[:, :])).then_inc(sem("ones_st"), 16)
            a0_steps(sp, a0_sp)
            ffn_sp(sp, 0)
            ffn_sp_run(sp, 0)
            a1_sp(sp)
            ffn_sp(sp, 1)
            ffn_sp_run(sp, 1)
            sp.wait_ge(sem("x_add"), 4 * 4)
            sp.dma_start(out.rearrange("(t p) d -> p t d", p=P), x[:, :, :]).then_inc(sem("out"), 16)
            sp.wait_ge(sem("out"), 16)

        @block.tensor
        def _(pe):
            ln_pe(pe, 0)
            a0_zero_pe(pe, 0)
            pe.wait_ge(sem("xT_lo"), 2 * DC)
            a0_steps(pe, a0_pe, a0_end_pe)
            ln_pe(pe, 1)
            ffn_pe(pe, 0)
            ln_pe(pe, 2)
            a1_pe(pe)
            ln_pe(pe, 3)
            ffn_pe(pe, 1)

        @block.scalar
        def _(act):
            ln_act(act, 0)
            act.wait_ge(sem("tab0"), 64)
            a0_steps(act, a0_act, a0_end_act)
            ln_act(act, 1)
            ffn_act(act, 0)
            ln_act(act, 2)
            a1_act(act)
            ln_act(act, 3)
            ffn_act(act, 1)

        @block.vector
        def _(dve):
            dve.memset(zero_r[:, :].bitcast(F32), 0.0).then_inc(sem("zero"), 1)
            dve.memset(ones_r[:, :].bitcast(F32), 1.0).then_inc(sem("ones"), 1)
            ln_dve(dve, 0)
            dve.wait_ge(sem("tab0"), 64)
            a0_steps(dve, a0_dve, a0_end_dve)
            ln_dve(dve, 1)
            ffn_dve(dve, 0)
            ln_dve(dve, 2)
            a1_dve(dve)
            ln_dve(dve, 3)
            ffn_dve(dve, 1)

        @block.gpsimd
        def _(pool):
            ln_pool(pool, 0)
            pool.wait_ge(sem("tab0"), 64)
            a0_steps(pool, a0_pool)
            ln_pool(pool, 1)
            ffn_pool(pool, 0)
            ln_pool(pool, 2)
            a1_pool(pool)
            ln_pool(pool, 3)
            ffn_pool(pool, 1)


def _rope_tables():
    pos = np.arange(S, dtype=np.float32)
    inv0 = (1.0 / np.float32(10000.0) ** (np.arange(0, DH0, 2, dtype=np.float32) / np.float32(DH0))).astype(np.float32)
    f0 = (pos[None, :] * inv0[:, None]).astype(np.float32)
    cos0, sin0 = np.repeat(np.cos(f0), 2, 0), np.repeat(np.sin(f0), 2, 0)
    sin0[0::2] *= -1.0
    inv1 = (1.0 / np.float32(10000.0) ** (np.arange(0, DH1, 2, dtype=np.float32) / np.float32(DH1))).astype(np.float32)
    f1 = (pos[None, :] * inv1[:, None]).astype(np.float32)
    cos1 = np.tile(np.concatenate([np.cos(f1), np.cos(f1)]), (P // DH1, 1))
    sin1 = np.tile(np.concatenate([-np.sin(f1), np.sin(f1)]), (P // DH1, 1))
    return cos0, sin0, cos1, sin1


def _layout(i):
    def chunks(m):
        return m.reshape(-1, P, m.shape[-1]).transpose(1, 0, 2)

    i = {k: np.asarray(v) for k, v in i.items()}
    d = {"x": i["L0_attn_resid_pre"].reshape(T, D), "ident": np.eye(P, dtype=np.float32)}
    d["cos0"], d["sin0"], d["cos1"], d["sin1"] = _rope_tables()

    def heads(wt):
        return wt.reshape(H0, DC, P, DH0).transpose(0, 2, 1, 3)

    d["wqk0"] = np.stack([heads(i["L0_attn_W_Q"]), heads(i["L0_attn_W_K"])], axis=2)
    d["wv0"] = heads(i["L0_attn_W_V"])
    d["wo0"] = i["L0_attn_W_O"].reshape(H0, DH0, D)
    bias = np.stack([i["L0_attn_b_Q"], i["L0_attn_b_K"], i["L0_attn_b_V"]])
    d["bqkv0"] = np.tile(bias.transpose(2, 0, 1), (1, 1, B))
    d["bo0"] = i["L0_attn_b_O"].reshape(DC, P).T

    lower = np.arange(E)[None, :] < np.arange(E)[:, None]
    d["lower16"] = lower.astype(np.float32).reshape(-1)
    d["lower4"] = lower[:GROUPS, :GROUPS].astype(np.float32).reshape(-1)
    names = (("gate_weight", "expert_bias", "gate_proj", "up_proj", "down_proj", "shared_gate", "shared_up", "shared_down"),
             ("gate_w", "expert_bias", "w_gate", "w_up", "w_down", "sw_gate", "sw_up", "sw_down"))
    for f in range(2):
        gate_w, ebias, g, u, dn, sg, su, sd = (i[f"L{f}_ffn_{n}"] for n in names[f])
        d[f"gw{f}"] = chunks(gate_w.T)
        d[f"ebias{f}"] = ebias
        every = [(sg, su, sd)] + [(g[e], u[e], dn[e]) for e in range(E)]
        d[f"ew{f}"] = np.stack([np.concatenate([chunks(g_.T).reshape(P, D), chunks(u_.T).reshape(P, D), dn_.T], axis=1)
                                for g_, u_, dn_ in every])

    swap = (np.arange(D) // DH1) * DH1 + (np.arange(D) + DH1 // 2) % DH1
    q, k = i["L1_attn_q_w"], i["L1_attn_k_w"]
    d["w1"] = np.stack([chunks(m.T) for m in (q, q[swap], k, k[swap], i["L1_attn_v_w"], i["L1_attn_out_w"])], axis=1)
    qb, kb = i["L1_attn_q_b"], i["L1_attn_k_b"]
    d["b1"] = np.stack([v.reshape(DC, P).T for v in (qb, qb[swap], kb, kb[swap])], axis=1)
    d["bv1"] = i["L1_attn_v_b"]
    d["bo1"] = i["L1_attn_out_b"].reshape(DC, P).T
    return {k: np.ascontiguousarray(v) for k, v in d.items()}


def kernel(**inputs):
    import concourse.bacc as bacc
    from concourse.bass_utils import run_bass_kernel_spmd

    nc = bacc.Bacc("TRN2", target_bir_lowering=False, num_devices=1)
    arrays = {f"in_{k}": v for k, v in _layout(inputs).items()}
    aps = {k[3:]: nc.dram_tensor(k, v.shape, mybir.dt.from_np(v.dtype), kind="ExternalInput").ap() for k, v in arrays.items()}
    out = nc.dram_tensor("out", (T, D), F32, kind="ExternalOutput").ap()
    build_program(nc, aps, out)
    r = run_bass_kernel_spmd(nc, [arrays], core_ids=[0])
    return r.results[0]["out"].reshape(B, S, D)
```

```python
from contextlib import ExitStack

import numpy as np
import concourse.bass as bass
from concourse import mybir

ALU = mybir.AluOpType
ACT = mybir.ActivationFunctionType
AX = mybir.AxisListType
F32 = mybir.dt.float32
F32R = mybir.dt.float32r
BF16 = mybir.dt.bfloat16

P = 128
B, S, D = 2, 512, 256
T = B * S
NT = T // P
QT = S // P
DC = D // P
BANK = 512
LN_EPS = 1e-5

H0, DH0 = 16, 128
N0 = B * H0
SCALE0 = float(1.0 / np.sqrt(DH0))

E, I = 16, 128
TOPK = 4
GROUPS, GROUP_KEEP = 4, 2
GSIZE = E // GROUPS
RENORM_EPS = (1e-20, 0.0)
ROUTE_SCALE = (2.5, 1.0)
BIG = 3.0e38

H1, DH1 = 16, 16
SCALE1 = float(DH1) ** -0.5
PAIRS = H1 // 2
N1 = B * PAIRS
STK = 64
ROWS_S = 3 * DH1
ROWS_M = ROWS_S + 2

PARTS = ((0, 0), (1, 0), (0, 1))


def fp(ap):
    return ap.bitcast(F32)


def build_program(nc, a, out):
    es = ExitStack()
    with es:
        sems = {}

        def sem(name):
            if name not in sems:
                sems[name] = es.enter_context(nc.semaphore(name))
            return sems[name]

        cursor = [(nc.sbuf_base + 31) // 32 * 32]

        def sb(name, shape, dt=F32):
            t = nc.alloc_sbuf_tensor_at(name, shape, dt, offset=cursor[0])
            size = int(np.prod(shape[1:])) * (2 if dt == BF16 else 4)
            cursor[0] += (size + 31) // 32 * 32
            return t

        x = sb("x", [P, NT, D])
        ident = sb("ident", [P, P])
        xn = sb("xn", [P, NT, D])
        xT_hi = sb("xT_hi", [P, DC, T], F32R)
        xT_lo = sb("xT_lo", [P, DC, T], F32R)
        aT = sb("aT", [P, DC, T])
        stats = sb("stats", [P, NT, 6])
        meanvar = sb("meanvar", [P, NT, 2])
        vareps = sb("vareps", [P, NT])
        rstd = sb("rstd", [P, NT])
        minus_half = sb("minus_half", [P, NT])

        region = cursor[0]
        cos0 = sb("cos0", [P, S])
        sin0 = sb("sin0", [P, S])
        bqkv0 = sb("bqkv0", [P, 3, N0])
        bo0 = sb("bo0", [P, DC])
        wqk_raw = sb("wqk_raw", [P, 2, DC, DH0])
        wqk = [sb(f"wqk_{p}", [P, 2, DC, DH0], F32R) for p in ("hi", "lo")]
        wv_raw = sb("wv_raw", [P, DC, DH0])
        wv = [sb(f"wv_{p}", [P, DC, DH0], F32R) for p in ("hi", "lo")]
        wo_raw = sb("wo_raw", [P, D])
        wo = [sb(f"wo_{p}", [P, D], F32R) for p in ("hi", "lo")]
        q_in = sb("q_in", [P, 2, S])
        q_sw = sb("q_sw", [P, 2, S])
        q_cos = sb("q_cos", [P, 2, S])
        q_sin = sb("q_sin", [P, 2, S])
        q_rot = sb("q_rot", [P, 2, S])
        qk = [sb(f"qk_{p}", [P, 2, S], F32R) for p in ("hi", "lo")]
        vT = sb("vT", [P, S])
        v0 = [sb(f"v0_{p}", [P, S], F32R) for p in ("hi", "lo")]
        sabs = sb("sabs", [P, QT, S])
        sgn = sb("sgn", [P, 2, QT, S], BF16)
        ex = sb("ex", [P, QT, S])
        w = sb("w", [P, QT, S])
        nmax = sb("nmax", [P, QT])
        den = sb("den", [P, QT])
        dene = sb("dene", [P, QT])
        rden = sb("rden", [P, QT])
        wT = [sb(f"wT_{p}", [P, QT, S], F32R) for p in ("hi", "lo")]
        z0 = [sb(f"z0_{p}", [P, S], F32R) for p in ("hi", "lo")]
        zero_r = sb("zero_r", [P, S], F32R)
        ones_r = sb("ones_r", [P, S], F32R)

        gw_raw = sb("gw_raw", [P, DC, E])
        gw = [sb(f"gw_{p}", [P, DC, E], F32R) for p in ("hi", "lo")]
        ebias = sb("ebias", [P, E])
        lower16 = sb("lower16", [P, E * E])
        lower4 = sb("lower4", [P, GROUPS * GROUPS])
        score = sb("score", [P, NT, E])
        biased = sb("biased", [P, NT, E])
        pairsum = sb("pairsum", [P, NT * GROUPS, 6])
        gscore = sb("gscore", [P, NT, GROUPS])
        ggt = sb("ggt", [P, NT, GROUPS * GROUPS])
        geq = sb("geq", [P, NT, GROUPS * GROUPS])
        grank = sb("grank", [P, NT * GROUPS])
        gkeep = sb("gkeep", [P, NT * GROUPS])
        gpen = sb("gpen", [P, NT * GROUPS])
        masked = sb("masked", [P, NT, E])
        erank = sb("erank", [P, NT * E])
        chosen = sb("chosen", [P, NT, E])
        wsum = sb("wsum", [P, NT])
        wsume = sb("wsume", [P, NT])
        wrec = sb("wrec", [P, NT])
        cw = sb("cw", [P, NT, E])
        cwT = sb("cwT", [E, T])
        ew_raw = sb("ew_raw", [P, 2, 3 * D])
        ew = [sb(f"ew_{p}", [P, 2, 3 * D], F32R) for p in ("hi", "lo")]
        cwb = sb("cwb", [P, 2, T])
        silu = sb("silu", [P, 2, S])
        gu = sb("gu", [P, 2, S])
        guw = sb("guw", [P, 2, S])
        hid = [sb(f"hid_{p}", [P, 2, S], F32R) for p in ("hi", "lo")]
        assert cursor[0] <= nc.sbuf_usable_end
        egt = cwb[:, :, :].rearrange("p a (t n) -> p (a t) n", n=E * E)
        eeq = aT[:, :, :].rearrange("p a (t n) -> p (a t) n", n=E * E)

        cursor[0] = region
        cos1 = sb("cos1", [P, S])
        sin1 = sb("sin1", [P, S])
        b1 = sb("b1", [P, 4, DC])
        bv1 = sb("bv1", [P, D])
        bo1 = sb("bo1", [P, DC])
        sel = sb("sel", [P, QT * P])
        w1_raw = sb("w1_raw", [P, 6, DC, D])
        w1 = [sb(f"w1_{p}", [P, 6, DC, D], F32R) for p in ("hi", "lo")]
        e1 = sb("e1", [P, 2 * QT, S])
        rc, rs, rr = (e1[:, k:k + 2, :] for k in (0, 2, 4))
        qk1 = [sb(f"qk1_{p}", [P, 2, DC, T], F32R) for p in ("hi", "lo")]
        v1 = sb("v1", [P, 2, D])
        v1s = sb("v1s", [P, NT, H1, 2, DH1], F32R)
        qs = sb("qs", [P, 2, S], F32R)
        ks = sb("ks", [P, 2, S], F32R)
        vs = sb("vs", [P, 2, QT, 2, P], F32R)
        nm1 = sb("nm1", [P, P])
        nmT = [sb(f"nmT_{p}", [P, P], F32R) for p in ("hi", "lo")]
        p1 = [sb(f"p1_{p}", [P, 2 * QT, S], F32R) for p in ("hi", "lo")]
        zst = sb("zst", [3 * 2 * DH1, 2, S])
        den1 = sb("den1", [P, P])
        rden1 = sb("rden1", [P, P])
        rden_s = [sb(f"rden_{p}", [P, P], F32R) for p in ("hi", "lo")]
        sel_r = sb("sel_r", [P, QT, P], F32R)
        assert cursor[0] <= nc.sbuf_usable_end
        zh = w1_raw[:, 0:4, :, :].rearrange("p g c d -> p g (c d)")
        zl = xn[:, :, :].rearrange("p (g t) d -> p g (t d)", g=B * DC)

        ps = es.enter_context(nc.psum_tensor("ps", [P, 8, BANK], F32))

        cw_dram = [nc.dram_tensor(f"cw_dram{k}", (E, T), F32).ap() for k in range(2)]
        den_dram = nc.dram_tensor("den_dram", (P, P), F32).ap()
        stk_dram = [nc.dram_tensor(f"stk_{t}", (H1 * STK, T), F32).ap() for t in ("q", "k")]

        def known(v):
            return isinstance(v, int)

        def wait(eng, name, value):
            if not known(value) or value > 0:
                eng.wait_ge(sem(name), value)

        def valid(n, count):
            return not known(n) or 0 <= n < count

        def ln_dve(dve, k):
            for t in range(NT):
                if k == 0:
                    dve.wait_ge(sem("x_ld"), 16)
                else:
                    dve.wait_ge(sem("x_add"), 4 * (k - 1) + t // 2 + 1)
                dve.bn_stats(stats[:, t, :], x[:, t, :]).then_inc(sem("ln_stats"), 1)
            for t in range(NT):
                dve.wait_ge(sem("ln_stats"), k * NT + t + 1)
                dve.bn_aggr(meanvar[:, t, :], stats[:, t, :]).then_inc(sem("ln_aggr"), 1)
            dve.wait_ge(sem("ln_aggr"), (k + 1) * NT)
            dve.tensor_scalar(vareps[:, :], meanvar[:, :, 1], LN_EPS, None, ALU.add).then_inc(sem("ln_var"), 1)
            dve.wait_ge(sem("ln_rstd"), k + 1)
            for t in range(NT):
                dve.tensor_scalar(xn[:, t, :], x[:, t, :], meanvar[:, t, 0:1], rstd[:, t:t + 1],
                                  ALU.subtract, ALU.mult).then_inc(sem("xn"), 1)
            for g in range(2 * DC):
                half, c = g // DC, g % DC
                dve.wait_ge(sem("xT_hi"), 2 * DC * k + g + 1)
                dve.tensor_tensor(xT_lo[:, c, half * S:(half + 1) * S], ps[:, 4 + g, :],
                                  fp(xT_hi[:, c, half * S:(half + 1) * S]), ALU.subtract).then_inc(sem("xT_lo"), 1)

        def ln_pool(pool, k):
            if k == 0:
                pool.memset(minus_half[:, :], -0.5).then_inc(sem("half"), 1)
                pool.wait_ge(sem("half"), 1)
            pool.wait_ge(sem("ln_var"), k + 1)
            pool.tensor_tensor(rstd[:, :], vareps[:, :], minus_half[:, :], ALU.pow).then_inc(sem("ln_rstd"), 1)

        def ln_pe(pe, k):
            if k == 0:
                pe.wait_ge(sem("ident"), 16)
            for g in range(2 * DC):
                half, c = g // DC, g % DC
                pe.wait_ge(sem("xn"), k * NT + QT * (half + 1))
                for t in range(QT):
                    last = pe.transpose(ps[:, 4 + g, t * P:(t + 1) * P],
                                        xn[:, half * QT + t, c * P:(c + 1) * P], ident[:, :])
                last.then_inc(sem("xT_ps"), 1)

        def ln_act(act, k):
            for g in range(2 * DC):
                half, c = g // DC, g % DC
                act.wait_ge(sem("xT_ps"), 2 * DC * k + g + 1)
                act.activation(xT_hi[:, c, half * S:(half + 1) * S], ps[:, 4 + g, :], ACT.Copy).then_inc(sem("xT_hi"), 1)

        def back_pe(pe, name, count, banks, tiles):
            for i, bank in enumerate(banks):
                wait(pe, name, count)
                for t2 in range(2):
                    t = tiles[2 * i + t2]
                    for c in range(DC):
                        last = pe.transpose(ps[:, bank, t2 * D + c * P:t2 * D + (c + 1) * P],
                                            aT[:, c, t * P:(t + 1) * P], ident[:, :])
                last.then_inc(sem("back"), 1)

        def back_dve(dve, done, banks, tiles):
            for i, bank in enumerate(banks):
                dve.wait_ge(sem("back"), done + i + 1)
                t = tiles[2 * i]
                dve.tensor_tensor(x[:, t:t + 2, :], x[:, t:t + 2, :],
                                  ps[:, bank, :].rearrange("p (t d) -> p t d", t=2), ALU.add).then_inc(sem("x_add"), 1)

        ROW = [slice(S - P * (qi + 1), S) for qi in range(QT)]
        QORDER = (3, 2, 0, 1)
        SPOT = {3: (2, 0), 2: (3, 0), 0: (3, 3 * P), 1: (4, 0)}
        TSPOT = {0: (7, 0), 1: (5, P), 3: (5, 0), 2: (6, 2 * P)}
        TGROUP = ((0,), (1, 3), (2,))

        def of_tile(n, qi):
            return QT * (n - 1) + QORDER.index(qi) + 1

        def of_pair(n, t):
            return 2 * (n - 1) + t + 1

        def of_group(n, g):
            return len(TGROUP) * (n - 1) + g + 1

        def a0_pe(pe, i):
            if valid(i + 2, N0):
                n = i + 2
                b = n // H0 if known(n) else batch[0]
                wait(pe, "wqk_lo", n + 1)
                wait(pe, "wT_lo", 3 * (n - 2))
                for t in range(2):
                    for j in range(3 * DC):
                        c, (pw, px) = j // 3, PARTS[j % 3]
                        last = pe.matmul(ps[:, 5 + t, :], wqk[pw][:, t, c, :], (xT_hi, xT_lo)[px][:, c, b * S:(b + 1) * S],
                                         start=j == 0, stop=j == 3 * DC - 1)
                    last.then_inc(sem("q_ps"), 1)
            if valid(i + 1, N0):
                n = i + 1
                wait(pe, "qk_lo", 2 * n + 2)
                wait(pe, "v_ev", n)
                wait(pe, "v_lo", n)
                for qi in QORDER:
                    wait(pe, "sgn", of_tile(n, qi))
                    bank, col = SPOT[qi]
                    for j, (pq, pk) in enumerate(PARTS):
                        last = pe.matmul(ps[:, bank, col:col + P * (qi + 1)], qk[pq][:, 0, qi * P:(qi + 1) * P],
                                         qk[pk][:, 1, 0:P * (qi + 1)], start=j == 0, stop=j == 2)
                    last.then_inc(sem("s"), 1)
            if valid(i - 1, N0):
                n = i - 1
                wait(pe, "z_lo", n + 1)
                wait(pe, "wo_lo", n + 1)
                for c in range(DC):
                    for j, (pw, pz) in enumerate(PARTS):
                        last = pe.matmul(ps[:, c, :], wo[pw][:, c * P:(c + 1) * P], z0[pz][:, :],
                                         start=False, stop=j == 2, skip_group_check=True)
                last.then_inc(sem("o"), 1)
            if valid(i, N0):
                n = i
                wait(pe, "w", QT * n + QT)
                wait(pe, "z_lo", n)
                for g, js in enumerate(TGROUP):
                    if g:
                        wait(pe, "q_ev", of_pair(min(n + 3, N0) if known(n) else n + 3, g - 1))
                    for j in js:
                        bank, col = TSPOT[j]
                        for qi in range(j, QT):
                            kc = (QT - 1 - qi + j) * P
                            last = pe.transpose(ps[:, bank, col + (qi - j) * P:col + (qi - j + 1) * P],
                                                w[:, qi, kc:kc + P], ident[:, :])
                    last.then_inc(sem("wT_ps"), 1)
            if valid(i + 1, N0):
                n = i + 1
                b = n // H0 if known(n) else batch[0]
                wait(pe, "wv_lo", n + 1)
                wait(pe, "sgn", of_tile(n + 1, 3))
                for j in range(3 * DC):
                    c, (pw, px) = j // 3, PARTS[j % 3]
                    last = pe.matmul(ps[:, 2, :], wv[pw][:, c, :], (xT_hi, xT_lo)[px][:, c, b * S:(b + 1) * S],
                                     start=j == 0, stop=j == 3 * DC - 1)
                last.then_inc(sem("v_ps"), 1)
            if valid(i, N0):
                n = i
                wait(pe, "v_lo", n + 1)
                wait(pe, "wT_lo", 3 * n + 3)
                for j in range(QT):
                    for m, (pv, pw) in enumerate(PARTS):
                        last = pe.matmul(ps[:, 7, j * P:S], v0[pv][:, j * P:(j + 1) * P], wT[pw][:, j, j * P:S],
                                         start=j == 0 and m == 0, stop=j == QT - 1 and m == 2, skip_group_check=True)
                last.then_inc(sem("pv"), 1)
            if valid(i + 1, N0):
                n = i + 1
                wait(pe, "v_ev", n + 1)
                for t in range(QT):
                    last = pe.transpose(ps[:, 4, t * P:(t + 1) * P], vT[:, t * P:(t + 1) * P], ident[:, :])
                last.then_inc(sem("vt_ps"), 1)

        def a0_act(act, i):
            if valid(i + 2, N0):
                n = i + 2
                for t in range(2):
                    wait(act, "q_ps", of_pair(n + 1, t))
                    wait(act, "q_cos", of_pair(n, t))
                    wait(act, "q_sin", of_pair(n, t))
                    act.activation(q_in[:, t, :], ps[:, 5 + t, :], ACT.Identity,
                                   bias=bqkv0[:, t, bass.ds(n, 1)]).then_inc(sem("q_ev"), 1)
            if valid(i + 3, N0):
                n = i + 3
                wait(act, "wqk_ld", 16 * (n + 1))
                wait(act, "q_ps", 2 * n)
                act.activation(wqk[0][:, :, :, :], wqk_raw[:, :, :, :], ACT.Copy).then_inc(sem("wqk_hi"), 1)
            if valid(i + 1, N0):
                n = i + 1
                for qi in QORDER:
                    wait(act, "s", of_tile(n + 1, qi))
                    if qi == 2:
                        wait(act, "s", of_tile(n + 1, 0))
                    wait(act, "ex", of_tile(n, qi))
                    bank, col = SPOT[qi]
                    src = ps[:, bank, col:col + P * (qi + 1)]
                    act.activation(sabs[:, qi, ROW[qi]], src, ACT.Abs, scale=SCALE0).then_inc(sem("sabs"), 1)
                    wait(act, "w", of_tile(n - 1, qi))
                    act.activation(sgn[:, par(1), qi, ROW[qi]], src, ACT.Sign).then_inc(sem("sgn"), 1)
            if valid(i, N0):
                n = i
                wait(act, "pv", n)
                for g, js in enumerate(TGROUP):
                    wait(act, "wT_ps", of_group(n + 1, g))
                    for j in js:
                        bank, col = TSPOT[j]
                        last = act.activation(wT[0][:, j, j * P:S], ps[:, bank, col:col + S - j * P], ACT.Copy)
                    last.then_inc(sem("wT_hi"), 1)
            if valid(i, N0):
                n = i
                wait(act, "wo_ld", 16 * (n + 1))
                wait(act, "o", n)
                act.activation(wo[0][:, :], wo_raw[:, :], ACT.Copy).then_inc(sem("wo_hi"), 1)
            if valid(i + 1, N0):
                n = i + 1
                wait(act, "v_ps", n + 1)
                wait(act, "vt_ps", n)
                act.activation(vT[:, :], ps[:, 2, :], ACT.Identity,
                               bias=bqkv0[:, 2, bass.ds(n, 1)]).then_inc(sem("v_ev"), 1)

            if valid(i + 1, N0):
                n = i + 1
                for qi in QORDER:
                    wait(act, "nmax", of_tile(n + 1, qi))
                    wait(act, "w", of_tile(n, qi))
                    act.activation(ex[:, qi, ROW[qi]], sabs[:, qi, ROW[qi]], ACT.Exp,
                                   bias=nmax[:, qi:qi + 1]).then_inc(sem("ex"), 1)
            if valid(i, N0):
                n = i
                wait(act, "pv", n + 1)
                wait(act, "o", n)
                act.activation(z0[0][:, :], ps[:, 7, :], ACT.Copy).then_inc(sem("z_hi"), 1)
            if valid(i + 1, N0):
                n = i + 1
                wait(act, "vt_ps", n + 1)
                wait(act, "pv", n)
                act.activation(v0[0][:, :], ps[:, 4, :], ACT.Copy).then_inc(sem("v_hi"), 1)
            if valid(i + 2, N0):
                n = i + 2
                wait(act, "wv_ld", 16 * (n + 1))
                wait(act, "v_ps", n)
                act.activation(wv[0][:, :, :], wv_raw[:, :, :], ACT.Copy).then_inc(sem("wv_hi"), 1)
        def a0_dve(dve, i):
            def rotated(t):
                n = i + 2
                wait(dve, "q_cos", of_pair(n + 1, t))
                wait(dve, "q_sin", of_pair(n + 1, t))
                wait(dve, "qk_lo", of_pair(n, t))
                dve.tensor_tensor(q_rot[:, t, :], q_cos[:, t, :], q_sin[:, t, :], ALU.add).then_inc(sem("q_rot"), 1)
                wait(dve, "q_rot", of_pair(n + 1, t))
                wait(dve, "s", QT * n)
                dve.tensor_copy(qk[0][:, t, :], q_rot[:, t, :]).then_inc(sem("qk_hi"), 1)

            if valid(i + 2, N0):
                n = i + 2
                for t in range(2):
                    wait(dve, "q_ev", of_pair(n + 1, t))
                    wait(dve, "q_rot", of_pair(n, t))
                    dve.tensor_tensor(q_cos[:, t, :], q_in[:, t, :], cos0[:, :], ALU.mult).then_inc(sem("q_cos"), 1)
            if valid(i, N0):
                n = i
                for g, js in enumerate(TGROUP):
                    wait(dve, "wT_hi", of_group(n + 1, g))
                    for j in js:
                        bank, col = TSPOT[j]
                        last = dve.tensor_tensor(wT[1][:, j, j * P:S], ps[:, bank, col:col + S - j * P],
                                                 fp(wT[0][:, j, j * P:S]), ALU.subtract)
                    last.then_inc(sem("wT_lo"), 1)

            if valid(i + 1, N0):
                n = i + 1
                wait(dve, "causal", 2 * n + 1)
                for qi in QORDER:
                    dve.tensor_reduce(nmax[:, qi:qi + 1], sabs[:, qi, ROW[qi]], AX.X, ALU.max,
                                      negate=True).then_inc(sem("nmax"), 1)
            if valid(i + 2, N0):
                rotated(0)
            if valid(i + 2, N0):
                rotated(1)
            if valid(i, N0):
                n = i
                wait(dve, "z_hi", n + 1)
                dve.tensor_tensor(z0[1][:, :], ps[:, 7, :], fp(z0[0][:, :]), ALU.subtract).then_inc(sem("z_lo"), 1)
            if valid(i + 1, N0):
                n = i + 1
                wait(dve, "v_hi", n + 1)
                dve.tensor_tensor(v0[1][:, :], ps[:, 4, :], fp(v0[0][:, :]), ALU.subtract).then_inc(sem("v_lo"), 1)
            if valid(i + 1, N0):
                n = i + 1
                wait(dve, "causal", 2 * n + 2)
                for qi in QORDER:
                    wait(dve, "ex", of_tile(n + 1, qi))
                    dve.scalar_tensor_tensor(out=ex[:, qi, ROW[qi]], in0=sgn[:, par(1), qi, ROW[qi]], scalar=0.0,
                                             in1=ex[:, qi, ROW[qi]], op0=ALU.not_equal, op1=ALU.mult,
                                             accum_out=den[:, qi:qi + 1]).then_inc(sem("den"), 1)
                wait(dve, "den", 4 * n + 4)
                dve.tensor_scalar(dene[:, :], den[:, :], 1e-6, None, ALU.add).then_inc(sem("dene"), 1)
                wait(dve, "dene", n + 1)
                dve.reciprocal(rden[:, :], dene[:, :]).then_inc(sem("rden"), 1)
            if valid(i + 1, N0):
                n = i + 1
                wait(dve, "rden", n + 1)
                wait(dve, "wT_ps", 3 * n)
                for qi in QORDER:
                    dve.scalar_tensor_tensor(out=w[:, qi, ROW[qi]], in0=ex[:, qi, ROW[qi]], scalar=rden[:, qi:qi + 1],
                                             in1=sgn[:, par(1), qi, ROW[qi]], op0=ALU.mult, op1=ALU.mult).then_inc(sem("w"), 1)
        def a0_pool(pool, i):
            if valid(i + 3, N0):
                n = i + 3
                wait(pool, "wqk_hi", n + 1)
                pool.tensor_tensor(wqk[1][:, :, :, :], wqk_raw[:, :, :, :], fp(wqk[0][:, :, :, :]),
                                   ALU.subtract).then_inc(sem("wqk_lo"), 1)
            if valid(i + 1, N0):
                n = i + 1
                wait(pool, "sgn", QT * n + QT)
                pool.sem_inc(sem("signed"), 1)
                for t in (sabs, sgn[:, par(1)]):
                    diag = t[:, :, S - P:S]
                    pool.affine_select(out=diag, in_=diag, compare_op=ALU.is_ge, fill=0.0, base=0,
                                       pattern=[[0, QT], [-1, P]], channel_multiplier=1).then_inc(sem("causal"), 1)
            if valid(i + 2, N0):
                n = i + 2
                for t in range(2):
                    wait(pool, f"swap{t}", 32 * (n + 1))
                    wait(pool, "q_rot", of_pair(n, t))
                    pool.tensor_tensor(q_sin[:, t, :], q_sw[:, t, :], sin0[:, :], ALU.mult).then_inc(sem("q_sin"), 1)
            if valid(i, N0):
                n = i
                wait(pool, "wo_hi", n + 1)
                pool.tensor_tensor(wo[1][:, :], wo_raw[:, :], fp(wo[0][:, :]), ALU.subtract).then_inc(sem("wo_lo"), 1)
            if valid(i + 2, N0):
                n = i + 2
                for t in range(2):
                    wait(pool, "qk_hi", of_pair(n + 1, t))
                    pool.tensor_tensor(qk[1][:, t, :], q_rot[:, t, :], fp(qk[0][:, t, :]),
                                       ALU.subtract).then_inc(sem("qk_lo"), 1)
                wait(pool, "wv_hi", n + 1)
                pool.tensor_tensor(wv[1][:, :, :], wv_raw[:, :, :], fp(wv[0][:, :, :]),
                                   ALU.subtract).then_inc(sem("wv_lo"), 1)

        def a0_sp(sp, i):
            def head(n):
                return n % H0 if known(n) else n - batch[0] * H0

            if valid(i + 2, N0):
                n = i + 2
                for t in range(2):
                    wait(sp, "q_ev", of_pair(n + 1, t))
                    for o in range(2):
                        sp.dma_start(q_sw[o:P:2, t, :], q_in[1 - o:P:2, t, :]).then_inc(sem(f"swap{t}"), 16)
            if valid(i + 1, N0):
                n = i + 1
                src = a["wo0"][head(n)]
                wait(sp, "wo_lo", n)
                sp.dma_start(wo_raw[:, :], src).then_inc(sem("wo_ld"), 16)
            if valid(i + 4, N0):
                n = i + 4
                src = a["wqk0"][head(n)]
                wait(sp, "wqk_lo", n)
                sp.dma_start(wqk_raw[:, :, :, :], src).then_inc(sem("wqk_ld"), 16)
            if valid(i + 3, N0):
                n = i + 3
                src = a["wv0"][head(n)]
                wait(sp, "wv_lo", n)
                sp.dma_start(wv_raw[:, :, :], src).then_inc(sem("wv_ld"), 16)

        batch = [0]
        odd = [0]
        LOOPS0 = {1: (H0 - 6, 0), H0 + 1: (N0 - 6, 1)}

        def par(ahead):
            return (odd[0] + ahead) % 2

        def a0_steps(eng, step, at=None):
            i = -4
            while i <= N0:
                if i in LOOPS0:
                    last, batch[0] = LOOPS0[i]
                    with eng.Fori(i // 2, last // 2) as r:
                        for k in range(2):
                            odd[0] = 1 - k
                            step(eng, 2 * r + 1 + k)
                    i = last + 1
                else:
                    odd[0] = i % 2
                    step(eng, i)
                    if at and i in (H0, N0):
                        at(eng, i // H0 - 1)
                    i += 1

        def a0_zero_pe(pe, b):
            if b == 0:
                pe.wait_ge(sem("zero"), 1)
            else:
                pe.wait_ge(sem("x_add"), 2 * b)
            for c in range(DC):
                pe.matmul(ps[:, c, :], zero_r[:, 0:P], zero_r[:, :], start=True, stop=True, skip_group_check=True)

        def a0_end_pe(pe, b):
            back_pe(pe, "aT", 2 * b + 2, (0, 1), range(QT * b, QT * b + QT))
            if b == 0:
                a0_zero_pe(pe, 1)

        def a0_end_act(act, b):
            act.wait_ge(sem("o"), H0 * (b + 1))
            for c in range(DC):
                act.activation(aT[:, c, b * S:(b + 1) * S], ps[:, c, :], ACT.Identity,
                               bias=bo0[:, c:c + 1]).then_inc(sem("aT"), 1)

        def a0_end_dve(dve, b):
            back_dve(dve, 2 * b, (0, 1), range(QT * b, QT * b + QT))

        M = E + 1
        PAIR_LOOP = (1, (M - 3) // 2)
        GATE_UP = slice(0, 2 * D)
        DOWN = slice(2 * D, 3 * D)
        PER_LAYER = {"gw_ld": 16, "ebias_ld": 48, "ew_ld_0": 16 * (M + 1) // 2, "ew_ld_1": 16 * (M // 2),
                     "cwb_0": 16 * (E // 2), "cwb_1": 16 * (E // 2), "cw_st": 16, "cwT": 2, "cwT_ps": NT, "gu": 2 * E, "gu_ps": 4 * M}
        ONCE = ("gw_hi", "gw_lo", "logits", "score", "cw")
        TWICE = ("guw", "hid_hi", "hid_lo", "y", "silu")

        def wait_f(eng, f, name, value):
            if not known(value) or value > 0:
                eng.wait_ge(sem(name), value + f * PER_LAYER.get(name, 1 if name in ONCE else 2 * M if name in TWICE else M))

        def ffn_steps(eng, step):
            for m in range(2):
                step(m, 0, m)
            with eng.Fori(*PAIR_LOOP) as r:
                for p in range(2):
                    step(2 * r + p, r, p)
            for m in range(2 * PAIR_LOOP[1], M + 1):
                step(m, m // 2, m % 2)

        def of_half(m, h):
            return 2 * (m - 1) + h + 1

        def half_of(t, h):
            return t[:, h * S:(h + 1) * S]

        def ffn_sp(sp, f):
            if f:
                sp.wait_ge(sem("x_add"), 12)
            sp.dma_start(gw_raw[:, :, :], a[f"gw{f}"]).then_inc(sem("gw_ld"), 16)
            sp.dma_start(ebias[:, :], a[f"ebias{f}"].partition_broadcast(P)).then_inc(sem("ebias_ld"), 16)
            sp.dma_start(lower16[:, :], a["lower16"].partition_broadcast(P)).then_inc(sem("ebias_ld"), 16)
            sp.dma_start(lower4[:, :], a["lower4"].partition_broadcast(P)).then_inc(sem("ebias_ld"), 16)
            for m in range(2):
                sp.dma_start(ew_raw[:, m, :], a[f"ew{f}"][m]).then_inc(sem(f"ew_ld_{m}"), 16)

        def ffn_sp_run(sp, f):
            wait_f(sp, f, "cwT", 2)
            sp.dma_start(cw_dram[f], cwT[:, :]).then_inc(sem("cw_st"), 16)
            wait_f(sp, f, "cw_st", 16)

            def step(m, k, p):
                if not known(m) or m + 1 < M:
                    src = cw_dram[f][bass.ds(m, 1), :].rearrange("e t -> (e t)").partition_broadcast(P)
                    wait_f(sp, f, "guw", 2 * m)
                    sp.dma_start(cwb[:, 1 - p, :], src).then_inc(sem(f"cwb_{1 - p}"), 16)
                if not known(m) or m + 2 < M:
                    src = a[f"ew{f}"][m + 2]
                    wait_f(sp, f, "down_lo", m + 1)
                    sp.dma_start(ew_raw[:, p, :], src).then_inc(sem(f"ew_ld_{p}"), 16)

            ffn_steps(sp, step)

        def ffn_pe(pe, f):
            wait_f(pe, f, "gw_lo", 1)
            pe.wait_ge(sem("xT_lo"), 2 * DC * (2 * f + 2))
            for t in range(NT):
                for j in range(3 * DC):
                    c, (pw, px) = j // 3, PARTS[j % 3]
                    last = pe.matmul(ps[:, 2, t * E:(t + 1) * E], (xT_hi, xT_lo)[px][:, c, t * P:(t + 1) * P],
                                     gw[pw][:, c, :], start=j == 0, stop=j == 3 * DC - 1)
            last.then_inc(sem("logits"), 1)

            def gate_up(m, p, h):
                if h == 0:
                    wait_f(pe, f, "gate_lo", m + 1)
                if known(m) and m == 1:
                    wait_f(pe, f, "guw", of_half(1, h))
                else:
                    wait_f(pe, f, "gu", of_half(m - 1, h))
                for u in range(2):
                    for j in range(3 * DC):
                        c, (pw, px) = j // 3, PARTS[j % 3]
                        col = (u * DC + c) * P
                        last = pe.matmul(ps[:, 4 + 2 * h + u, :], ew[pw][:, p, col:col + P],
                                         half_of((xT_hi, xT_lo)[px][:, c, :], h), start=j == 0, stop=j == 3 * DC - 1)
                    last.then_inc(sem("gu_ps"), 1)

            def down(m, p, h):
                if h == 0:
                    wait_f(pe, f, "down_lo", m + 1)
                wait_f(pe, f, "hid_lo", of_half(m + 1, h))
                first, end = known(m) and m == 0, known(m) and m == M - 1
                for c in range(DC):
                    for j, (pw, px) in enumerate(PARTS):
                        col = DOWN.start + c * P
                        last = pe.matmul(ps[:, 2 * h + c, :], ew[pw][:, p, col:col + P], hid[px][:, h, :],
                                         start=first and j == 0, stop=end and j == 2, skip_group_check=True)
                last.then_inc(sem("y"), 1)

            def step(m, k, p):
                for h in range(2):
                    if not known(m) or m < M:
                        gate_up(m, p, h)
                    if known(m) and m == 1 and h == 1:
                        wait_f(pe, f, "cw", 1)
                        for t in range(NT):
                            pe.transpose(ps[0:E, 2 + t // QT, t % QT * P:(t % QT + 1) * P], cw[:, t, :],
                                         ident[:, :]).then_inc(sem("cwT_ps"), 1)
                        wait_f(pe, f, "cwT", 2)
                    if not known(m) or m > 0:
                        down(m - 1, 1 - p, h)

            ffn_steps(pe, step)
            for h in range(2):
                back_pe(pe, "aT", 8 * f + 6 + 2 * h, (4 + 2 * h, 5 + 2 * h), range(QT * h, QT * h + QT))

        def ffn_act(act, f):
            wait_f(act, f, "logits", 1)
            act.activation(score[:, :, :].rearrange("p t e -> p (t e)"), ps[:, 2, 0:NT * E],
                           ACT.Sigmoid).then_inc(sem("score"), 1)

            def gate(m, h):
                wait_f(act, f, "gu_ps", 4 * m + 2 * h + 1)
                if known(m) and m == 1:
                    wait_f(act, f, "guw", of_half(1, h))
                else:
                    wait_f(act, f, "gu", of_half(m - 1, h))
                act.activation(silu[:, h, :], ps[:, 4 + 2 * h, :], ACT.Silu).then_inc(sem("silu"), 1)

            def hidden(m, h):
                wait_f(act, f, "guw", of_half(m + 1, h))
                wait_f(act, f, "y", of_half(m, h))
                act.activation(hid[0][:, h, :], guw[:, h, :], ACT.Copy).then_inc(sem("hid_hi"), 1)

            def step(m, k, p):
                runs = not known(m) or m < M
                if runs:
                    gate(m, 0)
                if not known(m) or m > 0:
                    hidden(m - 1, 1)
                if runs:
                    gate(m, 1)
                    hidden(m, 0)

            ffn_steps(act, step)
            for h in range(2):
                wait_f(act, f, "y", of_half(M, h))
                for c in range(DC):
                    act.activation(half_of(aT[:, c, :], h), ps[:, 2 * h + c, :], ACT.Copy).then_inc(sem("aT"), 1)

        def ffn_pool(pool, f):
            wait_f(pool, f, "gw_hi", 1)
            pool.tensor_tensor(gw[1][:, :, :], gw_raw[:, :, :], fp(gw[0][:, :, :]), ALU.subtract).then_inc(sem("gw_lo"), 1)

            def low(m, p, part, cols):
                wait_f(pool, f, f"{part}_hi", m + 1)
                pool.tensor_tensor(ew[1][:, p, cols], ew_raw[:, p, cols], fp(ew[0][:, p, cols]),
                                   ALU.subtract).then_inc(sem(f"{part}_lo"), 1)

            def weighted(m, k, p, h):
                if h == 0:
                    wait_f(pool, f, f"cwb_{p}", 16 * (k + p))
                wait_f(pool, f, "gu", of_half(m, h))
                wait_f(pool, f, "hid_lo", of_half(m, h))
                pool.tensor_tensor(guw[:, h, :], gu[:, h, :], half_of(cwb[:, p, :], h),
                                   ALU.mult).then_inc(sem("guw"), 1)

            def step(m, k, p):
                if known(m) and m == 0:
                    low(0, 0, "gate", GATE_UP)
                if known(m) and m == M:
                    return
                routed = not known(m) or m > 0
                if routed:
                    weighted(m, k, p, 0)
                if not known(m) or m + 1 < M:
                    low(m + 1, 1 - p, "gate", GATE_UP)
                if routed:
                    weighted(m, k, p, 1)
                low(m, p, "down", DOWN)

            ffn_steps(pool, step)

        def ffn_dve(dve, f):
            def high(m, k, p, part, cols):
                if part == "gate":
                    wait_f(dve, f, f"ew_ld_{p}", 16 * (k + 1))
                    wait_f(dve, f, "gu_ps", 4 * (m - 1))
                else:
                    wait_f(dve, f, "y", 2 * (m - 1))
                dve.tensor_copy(ew[0][:, p, cols], ew_raw[:, p, cols]).then_inc(sem(f"{part}_hi"), 1)

            def gated(m, h):
                wait_f(dve, f, "silu", of_half(m + 1, h))
                wait_f(dve, f, "gu_ps", 4 * m + 2 * h + 2)
                if known(m) and m == 0:
                    dve.tensor_tensor(guw[:, h, :], silu[:, h, :], ps[:, 5 + 2 * h, :], ALU.mult).then_inc(sem("guw"), 1)
                else:
                    if not known(m) or m > 1:
                        wait_f(dve, f, "guw", of_half(m, h))
                    dve.tensor_tensor(gu[:, h, :], silu[:, h, :], ps[:, 5 + 2 * h, :], ALU.mult).then_inc(sem("gu"), 1)

            def hidden(m, h):
                wait_f(dve, f, "hid_hi", of_half(m + 1, h))
                dve.tensor_tensor(hid[1][:, h, :], guw[:, h, :], fp(hid[0][:, h, :]), ALU.subtract).then_inc(sem("hid_lo"), 1)

            def step(m, k, p):
                if known(m) and m == 0:
                    high(0, 0, 0, "gate", GATE_UP)
                runs = not known(m) or m < M
                if runs:
                    gated(m, 0)
                if not known(m) or m > 0:
                    hidden(m - 1, 1)
                if not known(m) or m + 1 < M:
                    high(m + 1, k + p, 1 - p, "gate", GATE_UP)
                if runs:
                    gated(m, 1)
                    high(m, k, p, "down", DOWN)
                    hidden(m, 0)
                if known(m) and m == 0:
                    ffn_route(dve, f)

            wait_f(dve, f, "gw_ld", 16)
            dve.tensor_copy(gw[0][:, :, :], gw_raw[:, :, :]).then_inc(sem("gw_hi"), 1)
            ffn_steps(dve, step)
            for h in range(2):
                back_dve(dve, 8 * f + 4 + 2 * h, (4 + 2 * h, 5 + 2 * h), range(QT * h, QT * h + QT))

        def ffn_route(dve, f):
            done = [0]

            def then(ins):
                ins.then_inc(sem(f"route{f}"), 1)
                done[0] += 1

            def prev():
                dve.wait_ge(sem(f"route{f}"), done[0])

            def ranked(count, n, value, gt, eq, lower, rank):
                of_j = value.unsqueeze(2).broadcast_to([P, count, n, n])
                of_i = value.unsqueeze(3).broadcast_to([P, count, n, n])
                sq = [v.rearrange("p t (i j) -> p t i j", i=n) for v in (gt, eq)]
                then(dve.tensor_tensor(sq[0], of_j, of_i, ALU.is_gt))
                then(dve.tensor_tensor(sq[1], of_j, of_i, ALU.is_equal))
                prev()
                then(dve.tensor_tensor(eq, eq, lower.unsqueeze(1).broadcast_to([P, count, n * n]), ALU.mult))
                prev()
                then(dve.tensor_tensor(gt, gt, eq, ALU.add))
                prev()
                then(dve.tensor_reduce(rank.rearrange("p (t i) -> p t i", i=n), sq[0], AX.X, ALU.add))
                prev()

            wait_f(dve, f, "ebias_ld", 48)
            wait_f(dve, f, "score", 1)
            then(dve.tensor_tensor(biased[:, :, :], score[:, :, :], ebias[:, :].unsqueeze(1).broadcast_to([P, NT, E]), ALU.add))
            prev()
            value = biased
            if f == 0:
                grp = biased[:, :, :].rearrange("p t (g i) -> p (t g) i", i=GSIZE)
                for col, gap in ((0, 1), (3, 2), (5, 3)):
                    n = GSIZE - gap
                    then(dve.tensor_tensor(pairsum[:, :, col:col + n], grp[:, :, 0:n], grp[:, :, gap:GSIZE], ALU.add))
                prev()
                then(dve.tensor_reduce(gscore[:, :, :].rearrange("p t g -> p (t g)"), pairsum[:, :, :], AX.X, ALU.max))
                prev()
                ranked(NT, GROUPS, gscore[:, :, :], ggt[:, :, :], geq[:, :, :], lower4[:, :], grank[:, :])
                then(dve.tensor_scalar(gkeep[:, :], grank[:, :], float(GROUP_KEEP), None, ALU.is_lt))
                prev()
                then(dve.tensor_scalar(gpen[:, :], gkeep[:, :], BIG, -BIG, ALU.mult, ALU.add))
                msk = masked[:, :, :].rearrange("p t (g i) -> p (t g) i", i=GSIZE)
                over = [P, NT * GROUPS, GSIZE]
                then(dve.tensor_tensor(msk, grp, gkeep[:, :].unsqueeze(2).broadcast_to(over), ALU.mult))
                prev()
                then(dve.tensor_tensor(msk, msk, gpen[:, :].unsqueeze(2).broadcast_to(over), ALU.add))
                prev()
                value = masked
            ranked(NT, E, value[:, :, :], egt, eeq, lower16[:, :], erank[:, :])
            then(dve.tensor_scalar(chosen[:, :, :].rearrange("p t e -> p (t e)"), erank[:, :], float(TOPK), None, ALU.is_lt))
            prev()
            then(dve.tensor_tensor(chosen[:, :, :], chosen[:, :, :], score[:, :, :], ALU.mult))
            prev()
            then(dve.tensor_reduce(wsum[:, :], chosen[:, :, :], AX.X, ALU.add))
            prev()
            then(dve.tensor_scalar(wsume[:, :], wsum[:, :], RENORM_EPS[f], None, ALU.add))
            prev()
            then(dve.reciprocal(wrec[:, :], wsume[:, :]))
            prev()
            dve.scalar_tensor_tensor(out=cw[:, :, :], in0=chosen[:, :, :], scalar=ROUTE_SCALE[f],
                                     in1=wrec[:, :].unsqueeze(2).broadcast_to([P, NT, E]),
                                     op0=ALU.mult, op1=ALU.mult).then_inc(sem("cw"), 1)
            for k in range(2):
                wait_f(dve, f, "cwT_ps", NT)
                dve.tensor_copy(half_of(cwT, k), ps[0:E, 2 + k, :]).then_inc(sem("cwT"), 1)

        GROUPS1 = [(t, mt, h) for t in range(2) for mt in range(DC) for h in range(2)]
        AHEAD = 2
        CHUNKS = 2 * QT
        BANKS1, SLOTS = QT, 2 * QT
        LOOK = 4
        V_HI, V_LO, V_ONE = (k * 2 * DH1 for k in range(3))
        QUADS = B * DC

        def a1_pairs(eng, step):
            for b in range(B):
                with eng.Fori(0, PAIRS // 2) as r:
                    for p in range(2):
                        step(b, 2 * r + p, b * PAIRS + 2 * r + p, b * (PAIRS // 2) + r, p)

        def a1_sp(sp):
            sp.wait_ge(sem("x_add"), 4)
            for part in range(6):
                sp.dma_start(w1_raw[:, part, :, :], a["w1"][:, part]).then_inc(sem(f"w1_ld{part // 3}"), 16)
            for dst, name in ((cos1, "cos1"), (sin1, "sin1"), (bo1, "bo1"), (sel, "sel1")):
                sp.dma_start(dst[:, :], a[name]).then_inc(sem("tab1"), 16)
            sp.dma_start(b1[:, :, :], a["b1"]).then_inc(sem("tab1"), 16)
            sp.dma_start(bv1[:, :], a["bv1"].partition_broadcast(P)).then_inc(sem("tab1"), 16)
            for g, (t, mt, h) in enumerate(GROUPS1):
                rows = stk_dram[t].rearrange("(h r) t -> h r t", r=STK)[mt * H1 // 2:(mt + 1) * H1 // 2]
                for part in range(2):
                    sp.wait_ge(sem(f"qk1_{part}"), g + 1)
                    for j in range(3):
                        if PARTS[j][t] == part:
                            sp.dma_start(rows[:, j * DH1:(j + 1) * DH1, h * S:(h + 1) * S],
                                         fp(qk1[part][:, t, mt, h * S:(h + 1) * S])).then_inc(sem("stk_st"), 16)

            def load(b, pair, p, name, count):
                src = [stk_dram[t][bass.ds(pair * P, P), b * S:(b + 1) * S] for t in range(2)]
                wait(sp, name, count)
                sp.dma_start(fp(qs[:, p, :]), src[0]).then_inc(sem(f"stage_ld{p}"), 16)
                sp.dma_start(fp(ks[:, p, :]), src[1]).then_inc(sem(f"stage_ld{p}"), 16)

            def store(quad, k):
                p = k % 2
                dst = [t[2 * DH1 * k:2 * DH1 * (k + 1), bass.ds(quad, 1), :].rearrange("p q t -> p (q t)") for t in (zh, zl)]
                den_rows = den_dram[bass.ds(quad * 8 * QT + k * 2 * QT, 2 * QT), :]
                dens = zst[V_ONE:V_ONE + 2 * DH1:DH1, p, :].rearrange("h (i q) -> h i q", q=P)
                wait(sp, "zev_free", 4 * quad + k + 3)
                for j in range(2):
                    sp.dma_start(dst[j], zst[j * 2 * DH1:(j + 1) * 2 * DH1, p, :]).then_inc(sem(f"z_st{p}"), 16)
                sp.dma_start(den_rows, dens).then_inc(sem(f"z_st{p}"), 16)

            sp.wait_ge(sem("ones_st"), 16 * 8)
            sp.wait_ge(sem("stk_st"), 16 * 24)
            a1_pairs(sp, lambda b, pair, n, turn, p: load(b, pair, p, "s1", 2 * n + 2))
            for part in range(2):
                sp.wait_ge(sem(f"nmT_{part}"), 1)
                for b in range(B):
                    rows = stk_dram[0].rearrange("(h r) (b i q) -> r b h i q", r=STK, b=B, q=P)
                    sp.dma_start(rows[ROWS_S + part, b], fp(nmT[part][b * P // 2:(b + 1) * P // 2, :])).then_inc(sem("nm_st"), 16)
            sp.wait_ge(sem("nm_st"), 16 * 4)

            def second(b, mt, k):
                quad = b * DC + mt
                load(b, 4 * mt + k, k % 2, "st_ps", CHUNKS * (4 * quad + k + 1))
                if not known(quad) or 4 * quad + k >= 2:
                    store(quad if k >= 2 else quad - 1, (k - 2) % 4)

            for mt in range(DC):
                for k in range(4):
                    second(0, mt, k)
            with sp.Fori(0, DC) as r:
                for k in range(4):
                    second(1, r, k)
            for k in range(2, 4):
                store(QUADS - 1, k)
            for p in range(2):
                sp.wait_ge(sem(f"z_st{p}"), 48 * N1 // 2)
            sp.dma_start(den1[:, :], den_dram).then_inc(sem("den1_ld"), 16)

        def a1_pe(pe):
            pe.sem_inc(sem("s1"), 2 * AHEAD)
            pe.sem_inc(sem("st_ps"), CHUNKS * AHEAD)
            pe.sem_inc(sem("pv1"), SLOTS)
            pe.wait_ge(sem("xT_lo"), 2 * DC * 3)
            for g, (t, mt, h) in enumerate(GROUPS1):
                wait(pe, "w1_lo", 2 * t + 2)
                wait(pe, "rs", 2 * (g - 3))
                for sw in range(2):
                    for j in range(3 * DC):
                        c, (pw, px) = j // 3, PARTS[j % 3]
                        last = pe.matmul(ps[:, 2 * (g % 4) + sw, :], w1[pw][:, 2 * t + sw, c, mt * P:(mt + 1) * P],
                                         half_of((xT_hi, xT_lo)[px][:, c, :], h), start=j == 0, stop=j == 3 * DC - 1)
                    last.then_inc(sem("qk1_ps"), 1)
            pe.wait_ge(sem("w1_lo"), 5)
            for v in range(NT // 2):
                pe.wait_ge(sem("rs"), 2 * (5 + v // 2))
                for t2 in range(2):
                    t = 2 * v + t2
                    for j in range(3 * DC):
                        c, (pw, px) = j // 3, PARTS[j % 3]
                        last = pe.matmul(ps[:, v, t2 * D:(t2 + 1) * D], (xT_hi, xT_lo)[px][:, c, t * P:(t + 1) * P],
                                         w1[pw][:, 4, c, :], start=j == 0, stop=j == 3 * DC - 1)
                last.then_inc(sem("v1_ps"), 1)
            pe.wait_ge(sem("rs"), 16)
            pe.wait_ge(sem("v1"), NT // 2)

            def maxima(b, pair, n, turn, p):
                wait(pe, f"stage_ld{p}", 32 * (turn + 1))
                for hd in range(2):
                    wait(pe, "max_free", 2 * n + hd + 1)
                    for qi in range(QT):
                        rows = slice(hd * STK, hd * STK + ROWS_S)
                        mm = pe.matmul(ps[:, 4 * hd + qi, :], qs[rows, p, qi * P:(qi + 1) * P], ks[rows, p, :],
                                       start=True, stop=True)
                        if qi == QT - 1:
                            mm.then_inc(sem("s1"), 1)

            a1_pairs(pe, maxima)
            pe.wait_ge(sem("max_free"), 2 * N1 + 2)
            pe.transpose(ps[:, 6, 0:P], nm1[:, :], ident[:, :]).then_inc(sem("nmT_ps"), 1)

            def scores(n, turn, p, c):
                hd, kt = c // QT, c % QT
                if c == 0:
                    wait(pe, f"stage_ld{p}", 32 * (N1 // 2 + turn + 1))
                wait(pe, "st_free", CHUNKS * n + c + 1)
                rows = slice(hd * STK, hd * STK + ROWS_M)
                pe.matmul(ps[:, kt, :], ks[rows, p, kt * P:(kt + 1) * P], qs[rows, p, :],
                          start=True, stop=True).then_inc(sem("st_ps"), 1)

            def pv(n, p, c):
                hd, kt = c // QT, c % QT
                if c == 0:
                    wait(pe, "vs", n + 1)
                    wait(pe, "zev_free", n + 1)
                wait(pe, ("p_lo_dve", "p_lo_pool")[c % 2], CHUNKS // 2 * n + c // 2 + 1)
                for part in range(2):
                    last = pe.matmul(ps[:, 4 + p, :], vs[:, p, kt, hd, :], p1[part][:, c, :],
                                     start=c == 0 and part == 0, stop=c == CHUNKS - 1 and part == 1, skip_group_check=True)
                last.then_inc(sem("pv1"), 1)

            def step(n, turn, p, more=True):
                for c in range(CHUNKS):
                    if c + LOOK < CHUNKS:
                        scores(n, turn, p, c + LOOK)
                    elif more:
                        scores(n + 1, turn + p, 1 - p, c + LOOK - CHUNKS)
                    pv(n, p, c)

            for c in range(LOOK):
                scores(0, 0, 0, c)
            with pe.Fori(0, N1 // 2 - 1) as r:
                for p in range(2):
                    step(2 * r + p, r, p)
            for p in range(2):
                step(N1 - 2 + p, N1 // 2 - 1, p, more=p == 0)

            pe.wait_ge(sem("st_free"), CHUNKS * N1 + BANKS1)
            pe.wait_ge(sem("rden_lo"), 1)
            for g in range(QUADS):
                rows = slice(g * 8 * QT, (g + 1) * 8 * QT)
                for i in range(QT):
                    for part in range(2):
                        last = pe.matmul(ps[:, g, i * P:(i + 1) * P], sel_r[rows, i, :], rden_s[part][rows, :],
                                         start=part == 0, stop=part == 1)
                last.then_inc(sem("rd_ps"), 1)
            pe.wait_ge(sem("w1_lo"), 6)
            for h in range(B):
                pe.wait_ge(sem("zc_lo"), DC * (h + 1))
                for m in range(DC):
                    for j in range(3 * DC):
                        c, (pw, pz) = j // 3, PARTS[j % 3]
                        last = pe.matmul(ps[:, 4 + 2 * h + m, :], w1[pw][:, 5, c, m * P:(m + 1) * P],
                                         p1[pz][:, h * DC + c, :], start=j == 0, stop=j == 3 * DC - 1)
                    last.then_inc(sem("o1"), 1)
            for h in range(2):
                back_pe(pe, "aT", 10 + 2 * h, (2 * h, 2 * h + 1), range(QT * h, QT * h + QT))

        def a1_act(act):
            act.wait_ge(sem("tab1"), 16 * 6)
            for g, (t, mt, h) in enumerate(GROUPS1):
                act.wait_ge(sem("rr"), g + 1)
                act.activation(half_of(qk1[0][:, t, mt, :], h), rr[:, g % 2, :], ACT.Copy,
                               scale=SCALE1 if t == 0 else 1.0).then_inc(sem("qk1_0"), 1)
            for v in range(NT // 2):
                act.wait_ge(sem("v1"), v + 1)
                act.activation(v1s[:, 2 * v:2 * v + 2, :, 0, :], v1[:, :, :].rearrange("p t (h d) -> p t h d", h=H1),
                               ACT.Copy).then_inc(sem("v1_hi"), 1)
            act.wait_ge(sem("nmT_ps"), 1)
            act.activation(nmT[0][:, :], ps[:, 6, 0:P], ACT.Copy).then_inc(sem("nmT_0"), 1)
            act.sem_inc(sem("st_free"), BANKS1)
            act.sem_inc(sem("zev_free"), 2)

            def read_out(quad, k):
                n, p = 4 * quad + k, k % 2
                wait(act, "pv1", CHUNKS * n + CHUNKS + SLOTS)
                if not known(n) or n >= 2:
                    wait(act, f"z_st{p}", 48 * (2 * quad + k // 2))
                act.activation(zst[:, p, :], ps[0:3 * 2 * DH1, 4 + p, :], ACT.Copy).then_inc(sem("zev_free"), 1)

            def step(quad, k):
                n = 4 * quad + k
                for c in range(CHUNKS):
                    wait(act, "st_ps", CHUNKS * n + c + 1 + CHUNKS * AHEAD)
                    wait(act, ("p_lo_dve", "p_lo_pool")[c % 2], CHUNKS // 2 * (n - 1) + c // 2 + 1)
                    act.activation(e1[:, c, :], ps[:, c % BANKS1, :], ACT.Exp).then_inc(sem("st_free"), 1)
                    if c == 3 and (not known(n) or n > 0):
                        read_out(quad if k else quad - 1, (k - 1) % 4)

            for k in range(4):
                step(0, k)
            with act.Fori(1, QUADS) as r:
                for k in range(4):
                    step(r, k)
            read_out(QUADS - 1, 3)

            for g in range(QUADS):
                act.wait_ge(sem("zn"), g + 1)
                act.activation(p1[0][:, g, :], zh[:, g, :], ACT.Copy).then_inc(sem("zc_hi"), 1)
            for h in range(B):
                for m in range(DC):
                    act.wait_ge(sem("o1"), DC * h + m + 1)
                    act.activation(half_of(aT[:, m, :], h), ps[:, 4 + 2 * h + m, :], ACT.Identity,
                                   bias=bo1[:, m:m + 1]).then_inc(sem("aT"), 1)

        def a1_pool(pool):
            pool.wait_ge(sem("x_add"), 8)
            pool.memset(vs[:, :, :, :, :].bitcast(F32), 0.0).then_inc(sem("vs_zero"), 1)
            pool.wait_ge(sem("vs_zero"), 1)
            for hd in range(2):
                ones = vs[:, :, :, hd, V_ONE + hd * DH1:V_ONE + (hd + 1) * DH1]
                pool.memset(ones.bitcast(F32), 1.0).then_inc(sem("vs_one"), 1)
            for part in range(6):
                pool.wait_ge(sem("w1_hi"), part + 1)
                pool.tensor_tensor(w1[1][:, part, :, :], w1_raw[:, part, :, :], fp(w1[0][:, part, :, :]),
                                   ALU.subtract).then_inc(sem("w1_lo"), 1)
            for g in range(len(GROUPS1)):
                pool.wait_ge(sem("rs"), 2 * (g + 1))
                wait(pool, "qk1_1", g - 1)
                pool.tensor_tensor(rr[:, g % 2, :], rc[:, g % 2, :], rs[:, g % 2, :], ALU.add).then_inc(sem("rr"), 1)

            def step(b, pair, n, turn, p):
                for c in range(1, CHUNKS, 2):
                    wait(pool, "p_hi", CHUNKS * n + c + 1)
                    pool.tensor_tensor(p1[1][:, c, :], e1[:, c, :], fp(p1[0][:, c, :]),
                                       ALU.subtract).then_inc(sem("p_lo_pool"), 1)

            a1_pairs(pool, step)
            pool.wait_ge(sem("rden_hi"), 1)
            pool.tensor_tensor(rden_s[1][:, :], rden1[:, :], fp(rden_s[0][:, :]), ALU.subtract).then_inc(sem("rden_lo"), 1)

        def a1_dve(dve):
            for part in range(6):
                dve.wait_ge(sem(f"w1_ld{part // 3}"), 48)
                dve.tensor_copy(w1[0][:, part, :, :], w1_raw[:, part, :, :]).then_inc(sem("w1_hi"), 1)
            dve.wait_ge(sem("tab1"), 16 * 6)

            dve.tensor_copy(sel_r[:, :, :].rearrange("p i n -> p (i n)"), sel[:, :]).then_inc(sem("sel"), 1)

            def low(g):
                t, mt, h = GROUPS1[g]
                dve.wait_ge(sem("qk1_0"), g + 1)
                dve.scalar_tensor_tensor(out=half_of(qk1[1][:, t, mt, :], h), in0=rr[:, g % 2, :],
                                         scalar=SCALE1 if t == 0 else 1.0, in1=fp(half_of(qk1[0][:, t, mt, :], h)),
                                         op0=ALU.mult, op1=ALU.subtract).then_inc(sem("qk1_1"), 1)

            for g, (t, mt, h) in enumerate(GROUPS1):
                for sw, (dst, table, name) in enumerate(((rc, cos1, "rs"), (rs, sin1, "rs"))):
                    dve.wait_ge(sem("qk1_ps"), 2 * g + sw + 1)
                    wait(dve, "rr", g - 1)
                    dve.scalar_tensor_tensor(out=dst[:, g % 2, :], in0=ps[:, 2 * (g % 4) + sw, :],
                                             scalar=b1[:, 2 * t + sw, mt:mt + 1], in1=table[:, :],
                                             op0=ALU.add, op1=ALU.mult).then_inc(sem(name), 1)
                if g:
                    low(g - 1)
            low(len(GROUPS1) - 1)
            for v in range(NT // 2):
                dve.wait_ge(sem("v1_ps"), v + 1)
                wait(dve, "v1_lo", v)
                dve.tensor_tensor(v1[:, :, :], ps[:, v, :].rearrange("p (t d) -> p t d", t=2),
                                  bv1[:, :].unsqueeze(1).broadcast_to([P, 2, D]), ALU.add).then_inc(sem("v1"), 1)
                dve.wait_ge(sem("v1_hi"), v + 1)
                dve.tensor_tensor(v1s[:, 2 * v:2 * v + 2, :, 1, :], v1[:, :, :].rearrange("p t (h d) -> p t h d", h=H1),
                                  fp(v1s[:, 2 * v:2 * v + 2, :, 0, :]), ALU.subtract).then_inc(sem("v1_lo"), 1)
            dve.sem_inc(sem("max_free"), 2)

            def maxima(b, pair, n, turn, p):
                for hd in range(2):
                    col = n * 8 + 4 * hd
                    wait(dve, "s1", 2 * n + hd + 1 + 2 * AHEAD)
                    dve.sem_inc(sem("max_go"), 1)
                    dve.tensor_reduce(nm1[:, bass.ds(col, QT)], ps[:, 4 * hd:4 * hd + QT, :], AX.X, ALU.max,
                                      negate=True).then_inc(sem("max_free"), 1)

            a1_pairs(dve, maxima)
            dve.wait_ge(sem("nmT_0"), 1)
            dve.tensor_tensor(nmT[1][:, :], ps[:, 6, 0:P], fp(nmT[0][:, :]), ALU.subtract).then_inc(sem("nmT_1"), 1)
            dve.wait_ge(sem("vs_one"), 2)
            dve.wait_ge(sem("v1_lo"), NT // 2)

            def step(b, pair, n, turn, p):
                for c in range(CHUNKS):
                    wait(dve, "st_free", CHUNKS * n + c + 1 + BANKS1)
                    wait(dve, "pv1", CHUNKS * n + c + 1)
                    dve.tensor_copy(p1[0][:, c, :], e1[:, c, :]).then_inc(sem("p_hi"), 1)
                    if c == 0:
                        for k in range(2):
                            src = v1s[:, b * QT:(b + 1) * QT, bass.ds(2 * pair + k, 1), :, :].rearrange("p t h u d -> p t (h u) d")
                            dst = vs[:, p, :, k, V_HI:V_ONE].rearrange("p t (u h d) -> p t u h d", u=2, h=2)[:, :, :, k, :]
                            cp = dve.tensor_copy(dst, src)
                        cp.then_inc(sem("vs"), 1)
                    if c % 2 == 0:
                        wait(dve, "p_hi", CHUNKS * n + c + 1)
                        dve.tensor_tensor(p1[1][:, c, :], e1[:, c, :], fp(p1[0][:, c, :]),
                                          ALU.subtract).then_inc(sem("p_lo_dve"), 1)

            a1_pairs(dve, step)

            for p in range(2):
                dve.wait_ge(sem(f"z_st{p}"), 48 * N1 // 2)
            dve.wait_ge(sem("den1_ld"), 16)
            dve.reciprocal(rden1[:, :], den1[:, :]).then_inc(sem("rden1"), 1)
            dve.wait_ge(sem("rden1"), 1)
            dve.tensor_copy(rden_s[0][:, :], rden1[:, :]).then_inc(sem("rden_hi"), 1)
            for g in range(QUADS):
                dve.tensor_tensor(zh[:, g, :], zh[:, g, :], zl[:, g, :], ALU.add).then_inc(sem("zsum"), 1)
            for g in range(QUADS):
                dve.wait_ge(sem("zsum"), g + 1)
                dve.wait_ge(sem("rd_ps"), g + 1)
                dve.tensor_tensor(zh[:, g, :], zh[:, g, :], ps[:, g, :], ALU.mult).then_inc(sem("zn"), 1)
                dve.wait_ge(sem("zc_hi"), g + 1)
                dve.tensor_tensor(p1[1][:, g, :], zh[:, g, :], fp(p1[0][:, g, :]), ALU.subtract).then_inc(sem("zc_lo"), 1)
            for h in range(2):
                back_dve(dve, 8 + 2 * h, (2 * h, 2 * h + 1), range(QT * h, QT * h + QT))

        block = es.enter_context(nc.Block())

        @block.sync
        def _(sp):
            sp.dma_start(x[:, :, :], a["x"].rearrange("(t p) d -> p t d", p=P)).then_inc(sem("x_ld"), 16)
            sp.dma_start(ident[:, :], a["ident"]).then_inc(sem("ident"), 16)
            for dst, name in ((cos0, "cos0"), (sin0, "sin0"), (bo0, "bo0")):
                sp.dma_start(dst[:, :], a[name]).then_inc(sem("tab0"), 16)
            sp.dma_start(bqkv0[:, :, :], a["bqkv0"]).then_inc(sem("tab0"), 16)
            sp.wait_ge(sem("ones"), 1)
            for t in range(2):
                rows = stk_dram[t].rearrange("(h r) t -> h r t", r=STK)
                for g in range(DC):
                    for h in range(B):
                        sp.dma_start(rows[g * H1 // 2:(g + 1) * H1 // 2, ROWS_S:STK, h * S:(h + 1) * S],
                                     fp(ones_r[:, :])).then_inc(sem("ones_st"), 16)
            a0_steps(sp, a0_sp)
            ffn_sp(sp, 0)
            ffn_sp_run(sp, 0)
            a1_sp(sp)
            ffn_sp(sp, 1)
            ffn_sp_run(sp, 1)
            sp.wait_ge(sem("x_add"), 4 * 4)
            sp.dma_start(out.rearrange("(t p) d -> p t d", p=P), x[:, :, :]).then_inc(sem("out"), 16)
            sp.wait_ge(sem("out"), 16)

        @block.tensor
        def _(pe):
            ln_pe(pe, 0)
            a0_zero_pe(pe, 0)
            pe.wait_ge(sem("xT_lo"), 2 * DC)
            a0_steps(pe, a0_pe, a0_end_pe)
            ln_pe(pe, 1)
            ffn_pe(pe, 0)
            ln_pe(pe, 2)
            a1_pe(pe)
            ln_pe(pe, 3)
            ffn_pe(pe, 1)

        @block.scalar
        def _(act):
            ln_act(act, 0)
            act.wait_ge(sem("tab0"), 64)
            a0_steps(act, a0_act, a0_end_act)
            ln_act(act, 1)
            ffn_act(act, 0)
            ln_act(act, 2)
            a1_act(act)
            ln_act(act, 3)
            ffn_act(act, 1)

        @block.vector
        def _(dve):
            dve.memset(zero_r[:, :].bitcast(F32), 0.0).then_inc(sem("zero"), 1)
            dve.memset(ones_r[:, :].bitcast(F32), 1.0).then_inc(sem("ones"), 1)
            ln_dve(dve, 0)
            dve.wait_ge(sem("tab0"), 64)
            a0_steps(dve, a0_dve, a0_end_dve)
            ln_dve(dve, 1)
            ffn_dve(dve, 0)
            ln_dve(dve, 2)
            a1_dve(dve)
            ln_dve(dve, 3)
            ffn_dve(dve, 1)

        @block.gpsimd
        def _(pool):
            ln_pool(pool, 0)
            pool.wait_ge(sem("tab0"), 64)
            a0_steps(pool, a0_pool)
            ln_pool(pool, 1)
            ffn_pool(pool, 0)
            ln_pool(pool, 2)
            a1_pool(pool)
            ln_pool(pool, 3)
            ffn_pool(pool, 1)


def _rope_tables():
    pos = np.arange(S, dtype=np.float32)
    inv0 = (1.0 / np.float32(10000.0) ** (np.arange(0, DH0, 2, dtype=np.float32) / np.float32(DH0))).astype(np.float32)
    f0 = (pos[None, :] * inv0[:, None]).astype(np.float32)
    cos0, sin0 = np.repeat(np.cos(f0), 2, 0), np.repeat(np.sin(f0), 2, 0)
    sin0[0::2] *= -1.0
    inv1 = (1.0 / np.float32(10000.0) ** (np.arange(0, DH1, 2, dtype=np.float32) / np.float32(DH1))).astype(np.float32)
    f1 = (pos[None, :] * inv1[:, None]).astype(np.float32)
    cos1 = np.tile(np.concatenate([np.cos(f1), np.cos(f1)]), (P // DH1, 1))
    sin1 = np.tile(np.concatenate([-np.sin(f1), np.sin(f1)]), (P // DH1, 1))
    return cos0, sin0, cos1, sin1


def _layout(i):
    def chunks(m):
        return m.reshape(-1, P, m.shape[-1]).transpose(1, 0, 2)

    i = {k: np.asarray(v) for k, v in i.items()}
    d = {"x": i["L0_attn_resid_pre"].reshape(T, D), "ident": np.eye(P, dtype=np.float32)}
    d["cos0"], d["sin0"], d["cos1"], d["sin1"] = _rope_tables()

    def heads(wt):
        return wt.reshape(H0, DC, P, DH0).transpose(0, 2, 1, 3)

    d["wqk0"] = np.stack([heads(i["L0_attn_W_Q"]), heads(i["L0_attn_W_K"])], axis=2)
    d["wv0"] = heads(i["L0_attn_W_V"])
    d["wo0"] = i["L0_attn_W_O"].reshape(H0, DH0, D)
    bias = np.stack([i["L0_attn_b_Q"], i["L0_attn_b_K"], i["L0_attn_b_V"]])
    d["bqkv0"] = np.tile(bias.transpose(2, 0, 1), (1, 1, B))
    d["bo0"] = i["L0_attn_b_O"].reshape(DC, P).T

    lower = np.arange(E)[None, :] < np.arange(E)[:, None]
    d["lower16"] = lower.astype(np.float32).reshape(-1)
    d["lower4"] = lower[:GROUPS, :GROUPS].astype(np.float32).reshape(-1)
    names = (("gate_weight", "expert_bias", "gate_proj", "up_proj", "down_proj", "shared_gate", "shared_up", "shared_down"),
             ("gate_w", "expert_bias", "w_gate", "w_up", "w_down", "sw_gate", "sw_up", "sw_down"))
    for f in range(2):
        gate_w, ebias, g, u, dn, sg, su, sd = (i[f"L{f}_ffn_{n}"] for n in names[f])
        d[f"gw{f}"] = chunks(gate_w.T)
        d[f"ebias{f}"] = ebias
        every = [(sg, su, sd)] + [(g[e], u[e], dn[e]) for e in range(E)]
        d[f"ew{f}"] = np.stack([np.concatenate([chunks(g_.T).reshape(P, D), chunks(u_.T).reshape(P, D), dn_.T], axis=1)
                                for g_, u_, dn_ in every])

    swap = (np.arange(D) // DH1) * DH1 + (np.arange(D) + DH1 // 2) % DH1
    q, k = i["L1_attn_q_w"], i["L1_attn_k_w"]
    d["w1"] = np.stack([chunks(m.T) for m in (q, q[swap], k, k[swap], i["L1_attn_v_w"], i["L1_attn_out_w"])], axis=1)
    qb, kb = i["L1_attn_q_b"], i["L1_attn_k_b"]
    d["b1"] = np.stack([v.reshape(DC, P).T for v in (qb, qb[swap], kb, kb[swap])], axis=1)
    row, col = np.arange(P)[:, None, None], np.arange(P)[None, None, :]
    i_ = np.arange(QT)[None, :, None]
    d["sel1"] = (row % (8 * QT) == QT * (col // DH1) + i_).astype(np.float32).reshape(P, QT * P)
    d["bv1"] = i["L1_attn_v_b"]
    d["bo1"] = i["L1_attn_out_b"].reshape(DC, P).T
    return {k: np.ascontiguousarray(v) for k, v in d.items()}


def kernel(**inputs):
    import concourse.bacc as bacc
    from concourse.bass_utils import run_bass_kernel_spmd

    nc = bacc.Bacc("TRN2", target_bir_lowering=False, num_devices=1)
    arrays = {f"in_{k}": v for k, v in _layout(inputs).items()}
    aps = {k[3:]: nc.dram_tensor(k, v.shape, mybir.dt.from_np(v.dtype), kind="ExternalInput").ap() for k, v in arrays.items()}
    out = nc.dram_tensor("out", (T, D), F32, kind="ExternalOutput").ap()
    build_program(nc, aps, out)
    r = run_bass_kernel_spmd(nc, [arrays], core_ids=[0])
    return r.results[0]["out"].reshape(B, S, D)
```

```python
from contextlib import ExitStack

import numpy as np
import concourse.bass as bass
from concourse import mybir

ALU = mybir.AluOpType
ACT = mybir.ActivationFunctionType
AX = mybir.AxisListType
F32 = mybir.dt.float32
F32R = mybir.dt.float32r
BF16 = mybir.dt.bfloat16

P = 128
B, S, D = 2, 512, 256
T = B * S
NT = T // P
QT = S // P
DC = D // P
BANK = 512
LN_EPS = 1e-5

H0, DH0 = 16, 128
N0 = B * H0
SCALE0 = float(1.0 / np.sqrt(DH0))

E, I = 16, 128
TOPK = 4
GROUPS, GROUP_KEEP = 4, 2
GSIZE = E // GROUPS
RENORM_EPS = (1e-20, 0.0)
ROUTE_SCALE = (2.5, 1.0)
BIG = 3.0e38

H1, DH1 = 16, 16
SCALE1 = float(DH1) ** -0.5
PAIRS = H1 // 2
N1 = B * PAIRS
STK = 64
ROWS_S = 3 * DH1
ROWS_M = ROWS_S + 2

PARTS = ((0, 0), (1, 0), (0, 1))


def fp(ap):
    return ap.bitcast(F32)


def build_program(nc, a, out):
    es = ExitStack()
    with es:
        sems = {}

        def sem(name):
            if name not in sems:
                sems[name] = es.enter_context(nc.semaphore(name))
            return sems[name]

        cursor = [(nc.sbuf_base + 31) // 32 * 32]

        def sb(name, shape, dt=F32):
            t = nc.alloc_sbuf_tensor_at(name, shape, dt, offset=cursor[0])
            size = int(np.prod(shape[1:])) * (2 if dt == BF16 else 4)
            cursor[0] += (size + 31) // 32 * 32
            return t

        x = sb("x", [P, NT, D])
        ident = sb("ident", [P, P])
        xn = sb("xn", [P, NT, D])
        xT_at = cursor[0]
        xT_hi = sb("xT_hi", [P, DC, T], F32R)
        xT_lo = sb("xT_lo", [P, DC, T], F32R)
        aT = sb("aT", [P, DC, T])
        stats = sb("stats", [P, NT, 6])
        meanvar = sb("meanvar", [P, NT, 2])
        vareps = sb("vareps", [P, NT])
        rstd = sb("rstd", [P, NT])
        minus_half = sb("minus_half", [P, NT])

        region = cursor[0]
        cos0 = sb("cos0", [P, S])
        sin0 = sb("sin0", [P, S])
        bqkv0 = sb("bqkv0", [P, 3, N0])
        bo0 = sb("bo0", [P, DC])
        wqk_raw = sb("wqk_raw", [P, 2, DC, DH0])
        wqk = [sb(f"wqk_{p}", [P, 2, DC, DH0], F32R) for p in ("hi", "lo")]
        wv_raw = sb("wv_raw", [P, DC, DH0])
        wv = [sb(f"wv_{p}", [P, DC, DH0], F32R) for p in ("hi", "lo")]
        wo_raw = sb("wo_raw", [P, D])
        wo = [sb(f"wo_{p}", [P, D], F32R) for p in ("hi", "lo")]
        q_in = sb("q_in", [P, 2, S])
        q_sw = sb("q_sw", [P, 2, S])
        q_cos = sb("q_cos", [P, 2, S])
        q_sin = sb("q_sin", [P, 2, S])
        q_rot = sb("q_rot", [P, 2, S])
        qk = [sb(f"qk_{p}", [P, 2, S], F32R) for p in ("hi", "lo")]
        vT = sb("vT", [P, S])
        v0 = [sb(f"v0_{p}", [P, S], F32R) for p in ("hi", "lo")]
        sabs = sb("sabs", [P, QT, S])
        sgn = sb("sgn", [P, 2, QT, S], BF16)
        ex = sb("ex", [P, QT, S])
        w = sb("w", [P, QT, S])
        nmax = sb("nmax", [P, QT])
        den = sb("den", [P, QT])
        dene = sb("dene", [P, QT])
        rden = sb("rden", [P, QT])
        wT = [sb(f"wT_{p}", [P, QT, S], F32R) for p in ("hi", "lo")]
        z0 = [sb(f"z0_{p}", [P, S], F32R) for p in ("hi", "lo")]
        zero_r = sb("zero_r", [P, S], F32R)
        ones_r = sb("ones_r", [P, S], F32R)

        gw_raw = sb("gw_raw", [P, DC, E])
        gw = [sb(f"gw_{p}", [P, DC, E], F32R) for p in ("hi", "lo")]
        ebias = sb("ebias", [P, E])
        lower4 = sb("lower4", [P, GROUPS * GROUPS])
        score = sb("score", [P, NT, E])
        biased = sb("biased", [P, NT, E])
        pairsum = sb("pairsum", [P, NT * GROUPS, 6])
        gscore = sb("gscore", [P, NT, GROUPS])
        ggt = sb("ggt", [P, NT, GROUPS * GROUPS])
        geq = sb("geq", [P, NT, GROUPS * GROUPS])
        grank = sb("grank", [P, NT * GROUPS])
        gkeep = sb("gkeep", [P, NT * GROUPS])
        gpen = sb("gpen", [P, NT * GROUPS])
        masked = sb("masked", [P, NT, E])
        best = sb("best", [P, NT, 8])
        above = sb("above", [P, NT, E])
        nabove = sb("nabove", [P, NT])
        fits = sb("fits", [P, NT, E])
        chosen = sb("chosen", [P, NT, E])
        wsum = sb("wsum", [P, NT])
        wsume = sb("wsume", [P, NT])
        wrec = sb("wrec", [P, NT])
        cw = sb("cw", [P, NT, E])
        cwT = sb("cwT", [E, T])
        ew_raw = sb("ew_raw", [P, 2, 3 * D])
        ew = [sb(f"ew_{p}", [P, 2, 3 * D], F32R) for p in ("hi", "lo")]
        cwb = sb("cwb", [P, 2, T])
        silu = sb("silu", [P, 2, S])
        gu = sb("gu", [P, 2, S])
        guw = sb("guw", [P, 2, S])
        hid = [sb(f"hid_{p}", [P, 2, S], F32R) for p in ("hi", "lo")]
        assert cursor[0] <= nc.sbuf_usable_end
        runs = [cwb[:, :, :].rearrange("p a (k t e) -> p (a k) t e", k=T // (NT * 2 * E), t=NT)[:, k, :, :] for k in range(5)]

        cursor[0] = region
        cos1 = sb("cos1", [P, S])
        sin1 = sb("sin1", [P, S])
        b1 = sb("b1", [P, 4, DC])
        bv1 = sb("bv1", [P, D])
        bo1 = sb("bo1", [P, DC])
        w1_raw = sb("w1_raw", [P, 6, DC, D])
        w1 = [sb(f"w1_{p}", [P, 6, DC, D], F32R) for p in ("hi", "lo")]
        e1 = sb("e1", [P, 2 * QT, S])
        rc, rs, rr = (e1[:, k:k + 2, :] for k in (0, 2, 4))
        v1 = e1[:, 6, :].rearrange("p (t d) -> p t d", t=2)
        v1s = sb("v1s", [P, B * H1, QT, 2, DH1], F32R)
        qs = sb("qs", [P, 4, S], F32R)
        ks = sb("ks", [P, 4, S], F32R)
        vs = sb("vs", [P, 2, QT, 2, P], F32R)
        nm1 = sb("nm1", [P, 2, 2 * QT])
        nm_s = sb("nm_s", [P, 2, 4 * QT], F32R)
        nmT = sb("nmT", [4 * QT, 2, P], F32R)
        den1 = sb("den1", [B * H1 // 2 * QT, P])
        rden1 = sb("rden1", [B * H1 // 2 * QT, P])
        qk1 = [sb(f"qk1_{p}", [P, 2, DC, T], F32R) for p in ("hi", "lo")]
        p1 = [sb(f"p1_{p}", [P, 2 * QT, S], F32R) for p in ("hi", "lo")]
        assert cursor[0] <= nc.sbuf_usable_end
        after_xT = nc.alloc_sbuf_tensor_at("after_xT", [P, 2, DC, T], F32, offset=xT_at)
        zst = after_xT[0:3 * 2 * DH1, 0, :, S:]
        den_b = aT[:, 0, S:]
        rdenT = aT[:, 1, S:].rearrange("p (i r) -> p i r", i=QT)
        p1z = [w1[k][:, 0:B * DC, :, :].rearrange("p g c d -> p g (c d)") for k in range(2)]
        rden_b = [after_xT[:, 1, g % DC, g // DC * S:(g // DC + 1) * S] for g in range(B * DC - 1)]
        zh = w1_raw[:, 0:4, :, :].rearrange("p g c d -> p g (c d)")
        zl = xn[:, :, :].rearrange("p (g t) d -> p g (t d)", g=B * DC)

        ps = es.enter_context(nc.psum_tensor("ps", [P, 8, BANK], F32))

        cw_dram = [nc.dram_tensor(f"cw_dram{k}", (E, T), F32).ap() for k in range(2)]
        den_dram = nc.dram_tensor("den_dram", (P, P), F32).ap()
        rden_dram = nc.dram_tensor("rden_dram", (P, P), F32).ap()
        stk_dram = [nc.dram_tensor(f"stk_{t}", (N1 * P, S), F32).ap() for t in ("q", "k")]

        def known(v):
            return isinstance(v, int)

        def wait(eng, name, value):
            if not known(value) or value > 0:
                eng.wait_ge(sem(name), value)

        def valid(n, count):
            return not known(n) or 0 <= n < count

        def ln_stats(dve, k, h):
            tiles = range(h * QT, (h + 1) * QT)
            for t in tiles:
                if k == 0:
                    dve.wait_ge(sem("x_ld"), 16)
                else:
                    dve.wait_ge(sem("x_add"), 4 * (k - 1) + t // 2 + 1)
                dve.bn_stats(stats[:, t, :], x[:, t, :]).then_inc(sem("ln_stats"), 1)
            for t in tiles:
                dve.wait_ge(sem("ln_stats"), k * NT + t + 1)
                dve.bn_aggr(meanvar[:, t, :], stats[:, t, :]).then_inc(sem("ln_aggr"), 1)
            dve.wait_ge(sem("ln_aggr"), k * NT + (h + 1) * QT)
            dve.tensor_scalar(vareps[:, tiles.start:tiles.stop], meanvar[:, tiles.start:tiles.stop, 1], LN_EPS, None,
                              ALU.add).then_inc(sem("ln_var"), 1)

        def ln_xn(dve, k, h):
            dve.wait_ge(sem("ln_rstd"), 2 * k + h + 1)
            for t in range(h * QT, (h + 1) * QT):
                dve.tensor_scalar(xn[:, t, :], x[:, t, :], meanvar[:, t, 0:1], rstd[:, t:t + 1],
                                  ALU.subtract, ALU.mult).then_inc(sem("xn"), 1)

        def ln_low(dve, k, h):
            for c in range(DC):
                g = DC * h + c
                dve.wait_ge(sem("xT_hi"), 2 * DC * k + g + 1)
                dve.tensor_tensor(xT_lo[:, c, h * S:(h + 1) * S], ps[:, 4 + g, :],
                                  fp(xT_hi[:, c, h * S:(h + 1) * S]), ALU.subtract).then_inc(sem("xT_lo"), 1)

        def ln_dve(dve, k):
            for h in range(2):
                ln_stats(dve, k, h)
            for h in range(2):
                ln_xn(dve, k, h)
            for h in range(2):
                ln_low(dve, k, h)

        def ln_pool(pool, k, halves=(0, 1)):
            if k == 0:
                pool.memset(minus_half[:, :], -0.5).then_inc(sem("half"), 1)
                pool.wait_ge(sem("half"), 1)
            for h in halves:
                pool.wait_ge(sem("ln_var"), 2 * k + h + 1)
                pool.tensor_tensor(rstd[:, h * QT:(h + 1) * QT], vareps[:, h * QT:(h + 1) * QT], minus_half[:, h * QT:(h + 1) * QT],
                                   ALU.pow).then_inc(sem("ln_rstd"), 1)

        def ln_pe(pe, k, halves=(0, 1)):
            if k == 0:
                pe.wait_ge(sem("ident"), 16)
            for h in halves:
                for c in range(DC):
                    pe.wait_ge(sem("xn"), k * NT + QT * (h + 1))
                    for t in range(QT):
                        last = pe.transpose(ps[:, 4 + DC * h + c, t * P:(t + 1) * P],
                                            xn[:, h * QT + t, c * P:(c + 1) * P], ident[:, :])
                    last.then_inc(sem("xT_ps"), 1)

        def ln_act(act, k):
            for g in range(2 * DC):
                half, c = g // DC, g % DC
                act.wait_ge(sem("xT_ps"), 2 * DC * k + g + 1)
                act.activation(xT_hi[:, c, half * S:(half + 1) * S], ps[:, 4 + g, :], ACT.Copy).then_inc(sem("xT_hi"), 1)

        def back_pe(pe, name, count, banks, tiles):
            for i, bank in enumerate(banks):
                wait(pe, name, count)
                for t2 in range(2):
                    t = tiles[2 * i + t2]
                    for c in range(DC):
                        last = pe.transpose(ps[:, bank, t2 * D + c * P:t2 * D + (c + 1) * P],
                                            aT[:, c, t * P:(t + 1) * P], ident[:, :])
                last.then_inc(sem("back"), 1)

        def back_dve(dve, done, banks, tiles):
            for i, bank in enumerate(banks):
                dve.wait_ge(sem("back"), done + i + 1)
                t = tiles[2 * i]
                dve.tensor_tensor(x[:, t:t + 2, :], x[:, t:t + 2, :],
                                  ps[:, bank, :].rearrange("p (t d) -> p t d", t=2), ALU.add).then_inc(sem("x_add"), 1)

        ROW = [slice(S - P * (qi + 1), S) for qi in range(QT)]
        QORDER = (3, 2, 0, 1)
        SPOT = {3: (2, 0), 2: (3, 0), 0: (3, 3 * P), 1: (4, 0)}
        TSPOT = {0: (7, 0), 1: (5, P), 3: (5, 0), 2: (6, 2 * P)}
        TGROUP = ((0,), (1, 3), (2,))

        def of_tile(n, qi):
            return QT * (n - 1) + QORDER.index(qi) + 1

        def of_pair(n, t):
            return 2 * (n - 1) + t + 1

        def of_group(n, g):
            return len(TGROUP) * (n - 1) + g + 1

        def a0_pe(pe, i):
            if valid(i + 2, N0):
                n = i + 2
                b = n // H0 if known(n) else batch[0]
                wait(pe, "wqk_lo", n + 1)
                wait(pe, "wT_lo", 3 * (n - 2))
                for t in range(2):
                    for j in range(3 * DC):
                        c, (pw, px) = j // 3, PARTS[j % 3]
                        last = pe.matmul(ps[:, 5 + t, :], wqk[pw][:, t, c, :], (xT_hi, xT_lo)[px][:, c, b * S:(b + 1) * S],
                                         start=j == 0, stop=j == 3 * DC - 1)
                    last.then_inc(sem("q_ps"), 1)
            if valid(i + 1, N0):
                n = i + 1
                wait(pe, "qk_lo", 2 * n + 2)
                wait(pe, "v_ev", n)
                wait(pe, "v_lo", n)
                for qi in QORDER:
                    wait(pe, "sgn", of_tile(n, qi))
                    bank, col = SPOT[qi]
                    for j, (pq, pk) in enumerate(PARTS):
                        last = pe.matmul(ps[:, bank, col:col + P * (qi + 1)], qk[pq][:, 0, qi * P:(qi + 1) * P],
                                         qk[pk][:, 1, 0:P * (qi + 1)], start=j == 0, stop=j == 2)
                    last.then_inc(sem("s"), 1)
            if valid(i - 1, N0):
                n = i - 1
                wait(pe, "z_lo", n + 1)
                wait(pe, "wo_lo", n + 1)
                for c in range(DC):
                    for j, (pw, pz) in enumerate(PARTS):
                        last = pe.matmul(ps[:, c, :], wo[pw][:, c * P:(c + 1) * P], z0[pz][:, :],
                                         start=False, stop=j == 2, skip_group_check=True)
                last.then_inc(sem("o"), 1)
            if valid(i, N0):
                n = i
                wait(pe, "w", QT * n + QT)
                wait(pe, "z_lo", n)
                for g, js in enumerate(TGROUP):
                    if g:
                        wait(pe, "q_ev", of_pair(min(n + 3, N0) if known(n) else n + 3, g - 1))
                    for j in js:
                        bank, col = TSPOT[j]
                        for qi in range(j, QT):
                            kc = (QT - 1 - qi + j) * P
                            last = pe.transpose(ps[:, bank, col + (qi - j) * P:col + (qi - j + 1) * P],
                                                w[:, qi, kc:kc + P], ident[:, :])
                    last.then_inc(sem("wT_ps"), 1)
            if valid(i + 1, N0):
                n = i + 1
                b = n // H0 if known(n) else batch[0]
                wait(pe, "wv_lo", n + 1)
                wait(pe, "sgn", of_tile(n + 1, 3))
                for j in range(3 * DC):
                    c, (pw, px) = j // 3, PARTS[j % 3]
                    last = pe.matmul(ps[:, 2, :], wv[pw][:, c, :], (xT_hi, xT_lo)[px][:, c, b * S:(b + 1) * S],
                                     start=j == 0, stop=j == 3 * DC - 1)
                last.then_inc(sem("v_ps"), 1)
            if valid(i, N0):
                n = i
                wait(pe, "v_lo", n + 1)
                wait(pe, "wT_lo", 3 * n + 3)
                for j in range(QT):
                    for m, (pv, pw) in enumerate(PARTS):
                        last = pe.matmul(ps[:, 7, j * P:S], v0[pv][:, j * P:(j + 1) * P], wT[pw][:, j, j * P:S],
                                         start=j == 0 and m == 0, stop=j == QT - 1 and m == 2, skip_group_check=True)
                last.then_inc(sem("pv"), 1)
            if valid(i + 1, N0):
                n = i + 1
                wait(pe, "v_ev", n + 1)
                for t in range(QT):
                    last = pe.transpose(ps[:, 4, t * P:(t + 1) * P], vT[:, t * P:(t + 1) * P], ident[:, :])
                last.then_inc(sem("vt_ps"), 1)

        def a0_act(act, i):
            if valid(i + 2, N0):
                n = i + 2
                for t in range(2):
                    wait(act, "q_ps", of_pair(n + 1, t))
                    wait(act, "q_cos", of_pair(n, t))
                    wait(act, "q_sin", of_pair(n, t))
                    act.activation(q_in[:, t, :], ps[:, 5 + t, :], ACT.Identity,
                                   bias=bqkv0[:, t, bass.ds(n, 1)]).then_inc(sem("q_ev"), 1)
            if valid(i + 3, N0):
                n = i + 3
                wait(act, "wqk_ld", 16 * (n + 1))
                wait(act, "q_ps", 2 * n)
                act.activation(wqk[0][:, :, :, :], wqk_raw[:, :, :, :], ACT.Copy).then_inc(sem("wqk_hi"), 1)
            if valid(i + 1, N0):
                n = i + 1
                for qi in QORDER:
                    wait(act, "s", of_tile(n + 1, qi))
                    if qi == 2:
                        wait(act, "s", of_tile(n + 1, 0))
                    wait(act, "ex", of_tile(n, qi))
                    bank, col = SPOT[qi]
                    src = ps[:, bank, col:col + P * (qi + 1)]
                    act.activation(sabs[:, qi, ROW[qi]], src, ACT.Abs, scale=SCALE0).then_inc(sem("sabs"), 1)
                    wait(act, "w", of_tile(n - 1, qi))
                    act.activation(sgn[:, par(1), qi, ROW[qi]], src, ACT.Sign).then_inc(sem("sgn"), 1)
            if valid(i, N0):
                n = i
                wait(act, "pv", n)
                for g, js in enumerate(TGROUP):
                    wait(act, "wT_ps", of_group(n + 1, g))
                    for j in js:
                        bank, col = TSPOT[j]
                        last = act.activation(wT[0][:, j, j * P:S], ps[:, bank, col:col + S - j * P], ACT.Copy)
                    last.then_inc(sem("wT_hi"), 1)
            if valid(i, N0):
                n = i
                wait(act, "wo_ld", 16 * (n + 1))
                wait(act, "o", n)
                act.activation(wo[0][:, :], wo_raw[:, :], ACT.Copy).then_inc(sem("wo_hi"), 1)
            if valid(i + 1, N0):
                n = i + 1
                wait(act, "v_ps", n + 1)
                wait(act, "vt_ps", n)
                act.activation(vT[:, :], ps[:, 2, :], ACT.Identity,
                               bias=bqkv0[:, 2, bass.ds(n, 1)]).then_inc(sem("v_ev"), 1)

            if valid(i + 1, N0):
                n = i + 1
                for qi in QORDER:
                    wait(act, "nmax", of_tile(n + 1, qi))
                    wait(act, "w", of_tile(n, qi))
                    act.activation(ex[:, qi, ROW[qi]], sabs[:, qi, ROW[qi]], ACT.Exp,
                                   bias=nmax[:, qi:qi + 1]).then_inc(sem("ex"), 1)
            if valid(i, N0):
                n = i
                wait(act, "pv", n + 1)
                wait(act, "o", n)
                act.activation(z0[0][:, :], ps[:, 7, :], ACT.Copy).then_inc(sem("z_hi"), 1)
            if valid(i + 1, N0):
                n = i + 1
                wait(act, "vt_ps", n + 1)
                wait(act, "pv", n)
                act.activation(v0[0][:, :], ps[:, 4, :], ACT.Copy).then_inc(sem("v_hi"), 1)
            if valid(i + 2, N0):
                n = i + 2
                wait(act, "wv_ld", 16 * (n + 1))
                wait(act, "v_ps", n)
                act.activation(wv[0][:, :, :], wv_raw[:, :, :], ACT.Copy).then_inc(sem("wv_hi"), 1)
        def a0_dve(dve, i):
            def rotated(t):
                n = i + 2
                wait(dve, "q_cos", of_pair(n + 1, t))
                wait(dve, "q_sin", of_pair(n + 1, t))
                wait(dve, "qk_lo", of_pair(n, t))
                dve.tensor_tensor(q_rot[:, t, :], q_cos[:, t, :], q_sin[:, t, :], ALU.add).then_inc(sem("q_rot"), 1)
                wait(dve, "q_rot", of_pair(n + 1, t))
                wait(dve, "s", QT * n)
                dve.tensor_copy(qk[0][:, t, :], q_rot[:, t, :]).then_inc(sem("qk_hi"), 1)

            if valid(i + 2, N0):
                n = i + 2
                for t in range(2):
                    wait(dve, "q_ev", of_pair(n + 1, t))
                    wait(dve, "q_rot", of_pair(n, t))
                    dve.tensor_tensor(q_cos[:, t, :], q_in[:, t, :], cos0[:, :], ALU.mult).then_inc(sem("q_cos"), 1)
            if valid(i, N0):
                n = i
                for g, js in enumerate(TGROUP):
                    wait(dve, "wT_hi", of_group(n + 1, g))
                    for j in js:
                        bank, col = TSPOT[j]
                        last = dve.tensor_tensor(wT[1][:, j, j * P:S], ps[:, bank, col:col + S - j * P],
                                                 fp(wT[0][:, j, j * P:S]), ALU.subtract)
                    last.then_inc(sem("wT_lo"), 1)

            if valid(i + 1, N0):
                n = i + 1
                wait(dve, "causal", 2 * n + 1)
                for qi in QORDER:
                    dve.tensor_reduce(nmax[:, qi:qi + 1], sabs[:, qi, ROW[qi]], AX.X, ALU.max,
                                      negate=True).then_inc(sem("nmax"), 1)
            if valid(i + 2, N0):
                rotated(0)
            if valid(i + 2, N0):
                rotated(1)
            if valid(i, N0):
                n = i
                wait(dve, "z_hi", n + 1)
                dve.tensor_tensor(z0[1][:, :], ps[:, 7, :], fp(z0[0][:, :]), ALU.subtract).then_inc(sem("z_lo"), 1)
            if valid(i + 1, N0):
                n = i + 1
                wait(dve, "v_hi", n + 1)
                dve.tensor_tensor(v0[1][:, :], ps[:, 4, :], fp(v0[0][:, :]), ALU.subtract).then_inc(sem("v_lo"), 1)
            if valid(i + 1, N0):
                n = i + 1
                wait(dve, "causal", 2 * n + 2)
                for qi in QORDER:
                    wait(dve, "ex", of_tile(n + 1, qi))
                    dve.scalar_tensor_tensor(out=ex[:, qi, ROW[qi]], in0=sgn[:, par(1), qi, ROW[qi]], scalar=0.0,
                                             in1=ex[:, qi, ROW[qi]], op0=ALU.not_equal, op1=ALU.mult,
                                             accum_out=den[:, qi:qi + 1]).then_inc(sem("den"), 1)
                wait(dve, "den", 4 * n + 4)
                dve.tensor_scalar(dene[:, :], den[:, :], 1e-6, None, ALU.add).then_inc(sem("dene"), 1)
                wait(dve, "dene", n + 1)
                dve.reciprocal(rden[:, :], dene[:, :]).then_inc(sem("rden"), 1)
            if valid(i + 1, N0):
                n = i + 1
                wait(dve, "rden", n + 1)
                wait(dve, "wT_ps", 3 * n)
                for qi in QORDER:
                    dve.scalar_tensor_tensor(out=w[:, qi, ROW[qi]], in0=ex[:, qi, ROW[qi]], scalar=rden[:, qi:qi + 1],
                                             in1=sgn[:, par(1), qi, ROW[qi]], op0=ALU.mult, op1=ALU.mult).then_inc(sem("w"), 1)
        def a0_pool(pool, i):
            if valid(i + 3, N0):
                n = i + 3
                wait(pool, "wqk_hi", n + 1)
                pool.tensor_tensor(wqk[1][:, :, :, :], wqk_raw[:, :, :, :], fp(wqk[0][:, :, :, :]),
                                   ALU.subtract).then_inc(sem("wqk_lo"), 1)
            if valid(i + 1, N0):
                n = i + 1
                wait(pool, "sgn", QT * n + QT)
                pool.sem_inc(sem("signed"), 1)
                for t in (sabs, sgn[:, par(1)]):
                    diag = t[:, :, S - P:S]
                    pool.affine_select(out=diag, in_=diag, compare_op=ALU.is_ge, fill=0.0, base=0,
                                       pattern=[[0, QT], [-1, P]], channel_multiplier=1).then_inc(sem("causal"), 1)
            if valid(i + 2, N0):
                n = i + 2
                for t in range(2):
                    wait(pool, f"swap{t}", 32 * (n + 1))
                    wait(pool, "q_rot", of_pair(n, t))
                    pool.tensor_tensor(q_sin[:, t, :], q_sw[:, t, :], sin0[:, :], ALU.mult).then_inc(sem("q_sin"), 1)
            if valid(i, N0):
                n = i
                wait(pool, "wo_hi", n + 1)
                pool.tensor_tensor(wo[1][:, :], wo_raw[:, :], fp(wo[0][:, :]), ALU.subtract).then_inc(sem("wo_lo"), 1)
            if valid(i + 2, N0):
                n = i + 2
                for t in range(2):
                    wait(pool, "qk_hi", of_pair(n + 1, t))
                    pool.tensor_tensor(qk[1][:, t, :], q_rot[:, t, :], fp(qk[0][:, t, :]),
                                       ALU.subtract).then_inc(sem("qk_lo"), 1)
                wait(pool, "wv_hi", n + 1)
                pool.tensor_tensor(wv[1][:, :, :], wv_raw[:, :, :], fp(wv[0][:, :, :]),
                                   ALU.subtract).then_inc(sem("wv_lo"), 1)

        def a0_sp(sp, i):
            def head(n):
                return n % H0 if known(n) else n - batch[0] * H0

            if valid(i + 2, N0):
                n = i + 2
                for t in range(2):
                    wait(sp, "q_ev", of_pair(n + 1, t))
                    for o in range(2):
                        sp.dma_start(q_sw[o:P:2, t, :], q_in[1 - o:P:2, t, :]).then_inc(sem(f"swap{t}"), 16)
            if valid(i + 1, N0):
                n = i + 1
                src = a["wo0"][head(n)]
                wait(sp, "wo_lo", n)
                sp.dma_start(wo_raw[:, :], src).then_inc(sem("wo_ld"), 16)
            if valid(i + 4, N0):
                n = i + 4
                src = a["wqk0"][head(n)]
                wait(sp, "wqk_lo", n)
                sp.dma_start(wqk_raw[:, :, :, :], src).then_inc(sem("wqk_ld"), 16)
            if valid(i + 3, N0):
                n = i + 3
                src = a["wv0"][head(n)]
                wait(sp, "wv_lo", n)
                sp.dma_start(wv_raw[:, :, :], src).then_inc(sem("wv_ld"), 16)

        batch = [0]
        odd = [0]
        LOOPS0 = {1: (H0 - 6, 0), H0 + 1: (N0 - 6, 1)}

        def par(ahead):
            return (odd[0] + ahead) % 2

        def a0_steps(eng, step, at=None):
            i = -4
            while i <= N0:
                if i in LOOPS0:
                    last, batch[0] = LOOPS0[i]
                    with eng.Fori(i // 2, last // 2) as r:
                        for k in range(2):
                            odd[0] = 1 - k
                            step(eng, 2 * r + 1 + k)
                    i = last + 1
                else:
                    odd[0] = i % 2
                    step(eng, i)
                    if at and i in (H0, N0):
                        at(eng, i // H0 - 1)
                    i += 1

        def a0_zero_pe(pe, b):
            if b == 0:
                pe.wait_ge(sem("zero"), 1)
            else:
                pe.wait_ge(sem("x_add"), 2 * b)
            for c in range(DC):
                pe.matmul(ps[:, c, :], zero_r[:, 0:P], zero_r[:, :], start=True, stop=True, skip_group_check=True)

        def a0_end_pe(pe, b):
            back_pe(pe, "aT", 2 * b + 2, (0, 1), range(QT * b, QT * b + QT))
            if b == 0:
                a0_zero_pe(pe, 1)

        def a0_end_act(act, b):
            act.wait_ge(sem("o"), H0 * (b + 1))
            for c in range(DC):
                act.activation(aT[:, c, b * S:(b + 1) * S], ps[:, c, :], ACT.Identity,
                               bias=bo0[:, c:c + 1]).then_inc(sem("aT"), 1)

        def a0_end_dve(dve, b):
            if b == 0:
                back_dve(dve, 0, (0, 1), range(QT))
            else:
                ln_stats(dve, 1, 0)

        M = E + 1
        PAIR_LOOP = (2, (M - 3) // 2)
        GATE_UP = slice(0, 2 * D)
        DOWN = slice(2 * D, 3 * D)
        PER_LAYER = {"gw_ld": 16, "ebias_ld": 32, "ew_ld_0": 16 * (M + 1) // 2, "ew_ld_1": 16 * (M // 2),
                     "cwb_0": 16 * (E // 2), "cwb_1": 16 * (E // 2 - 1), "cwb_first": 2, "cwb_first_ps": 2, "cw_st": 32, "cwT": 2, "logits": 2, "scoreT": 2, "cwT_ps": NT, "gu": 2 * E, "gu_ps": 4 * M}
        ONCE = ("gw_hi", "gw_lo", "score_ps", "cw")
        TWICE = ("guw", "hid_hi", "hid_lo", "y", "silu")

        def wait_f(eng, f, name, value):
            if not known(value) or value > 0:
                eng.wait_ge(sem(name), value + f * PER_LAYER.get(name, 1 if name in ONCE else 2 * M if name in TWICE else M))

        def ffn_steps(eng, step):
            for m in range(2 * PAIR_LOOP[0]):
                step(m, m // 2, m % 2)
            with eng.Fori(*PAIR_LOOP) as r:
                for p in range(2):
                    step(2 * r + p, r, p)
            for m in range(2 * PAIR_LOOP[1], M + 1):
                step(m, m // 2, m % 2)

        def of_half(m, h):
            return 2 * (m - 1) + h + 1

        def half_of(t, h):
            return t[:, h * S:(h + 1) * S]

        def ffn_sp(sp, f):
            sp.dma_start(gw_raw[:, :, :], a[f"gw{f}"]).then_inc(sem("gw_ld"), 16)
            sp.dma_start(ebias[:, :], a[f"ebias{f}"].partition_broadcast(P)).then_inc(sem("ebias_ld"), 16)
            sp.dma_start(lower4[:, :], a["lower4"].partition_broadcast(P)).then_inc(sem("ebias_ld"), 16)
            for m in range(2):
                sp.dma_start(ew_raw[:, m, :], a[f"ew{f}"][m]).then_inc(sem(f"ew_ld_{m}"), 16)

        def ffn_sp_run(sp, f):
            def load(m, p):
                src = a[f"ew{f}"][m + 2]
                wait_f(sp, f, "down_lo", m + 1)
                sp.dma_start(ew_raw[:, p, :], src).then_inc(sem(f"ew_ld_{p}"), 16)

            load(0, 0)
            for h in range(2):
                wait_f(sp, f, "cwT", h + 1)
                sp.dma_start(half_of(cw_dram[f], h), half_of(cwT, h)).then_inc(sem("cw_st"), 16)
            wait_f(sp, f, "cw_st", 32)

            def step(m, k, p):
                if not known(m) or 0 < m < M - 1:
                    src = cw_dram[f][bass.ds(m, 1), :].rearrange("e t -> (e t)").partition_broadcast(P)
                    wait_f(sp, f, "guw", 2 * m)
                    sp.dma_start(cwb[:, 1 - p, :], src).then_inc(sem(f"cwb_{1 - p}"), 16)
                if not known(m) or 0 < m < M - 2:
                    load(m, p)

            ffn_steps(sp, step)

        def ffn_pe(pe, f):
            def logits(h):
                pe.wait_ge(sem("xT_lo"), DC * (2 * (2 * f + 1) + h + 1))
                for j in range(3 * DC):
                    c, (pw, px) = j // 3, PARTS[j % 3]
                    last = pe.matmul(ps[0:E, 2 + h, :], gw[pw][:, c, :], half_of((xT_hi, xT_lo)[px][:, c, :], h),
                                     start=j == 0, stop=j == 3 * DC - 1)
                last.then_inc(sem("logits"), 1)

            def scores():
                wait_f(pe, f, "scoreT", 2)
                for t in range(NT):
                    last = pe.transpose(ps[:, 2, t * E:(t + 1) * E], cwT[:, t * P:(t + 1) * P], ident[0:E, 0:E])
                last.then_inc(sem("score_ps"), 1)

            def weights():
                wait_f(pe, f, "cw", 1)
                for t in range(NT):
                    last = pe.transpose(ps[:, 2 + t // QT, t % QT * P:(t % QT + 1) * P],
                                        cw[:, t, 0:1].broadcast_to([P, P]), ident[:, :])
                    if t % QT == QT - 1:
                        last.then_inc(sem("cwb_first_ps"), 1)
                wait_f(pe, f, "gu", of_half(1, 1))
                for t in range(NT):
                    pe.transpose(ps[0:E, 6 + t // QT, t % QT * P:(t % QT + 1) * P], cw[:, t, :],
                                 ident[:, :]).then_inc(sem("cwT_ps"), 1)
                wait_f(pe, f, "cwb_first", 2)

            def gate_up(m, p, h):
                if known(m) and (m, h) == (2, 1):
                    wait_f(pe, f, "cwT", 2)
                if h == 0:
                    wait_f(pe, f, "gate_lo", m + 1)
                if known(m) and m == 1:
                    wait_f(pe, f, "guw", of_half(1, h))
                else:
                    wait_f(pe, f, "gu", of_half(m - 1, h))
                for u in range(2):
                    for j in range(3 * DC):
                        c, (pw, px) = j // 3, PARTS[j % 3]
                        col = (u * DC + c) * P
                        last = pe.matmul(ps[:, 4 + 2 * h + u, :], ew[pw][:, p, col:col + P],
                                         half_of((xT_hi, xT_lo)[px][:, c, :], h), start=j == 0, stop=j == 3 * DC - 1)
                    last.then_inc(sem("gu_ps"), 1)

            def down(m, p, h):
                if h == 0:
                    wait_f(pe, f, "down_lo", m + 1)
                wait_f(pe, f, "hid_lo", of_half(m + 1, h))
                first, end = known(m) and m == 0, known(m) and m == M - 1
                for c in range(DC):
                    for j, (pw, px) in enumerate(PARTS):
                        col = DOWN.start + c * P
                        last = pe.matmul(ps[:, 2 * h + c, :], ew[pw][:, p, col:col + P], hid[px][:, h, :],
                                         start=first and j == 0, stop=end and j == 2, skip_group_check=True)
                last.then_inc(sem("y"), 1)

            def step(m, k, p):
                for h in range(2):
                    if not known(m) or m < M and (m, h) != (2, 0):
                        gate_up(m, p, h)
                    if known(m) and m == 0 and h == 0:
                        logits(1)
                        scores()
                    if known(m) and m == 1 and h == 1:
                        gate_up(2, 0, 0)
                        weights()
                    if not known(m) or m > 0:
                        down(m - 1, 1 - p, h)

            ln_pe(pe, 2 * f + 1, (0,))
            wait_f(pe, f, "gw_lo", 1)
            logits(0)
            ln_pe(pe, 2 * f + 1, (1,))
            ffn_steps(pe, step)
            for h in range(2):
                back_pe(pe, "aT", 8 * f + 6 + 2 * h, (4 + 2 * h, 5 + 2 * h), range(QT * h, QT * h + QT))

        def ffn_act(act, f):
            for h in range(2):
                wait_f(act, f, "logits", h + 1)
                act.activation(half_of(cwT, h), ps[0:E, 2 + h, :], ACT.Sigmoid).then_inc(sem("scoreT"), 1)

            def gate(m, h):
                wait_f(act, f, "gu_ps", 4 * m + 2 * h + 1)
                if known(m) and m == 1:
                    wait_f(act, f, "guw", of_half(1, h))
                else:
                    wait_f(act, f, "gu", of_half(m - 1, h))
                act.activation(silu[:, h, :], ps[:, 4 + 2 * h, :], ACT.Silu).then_inc(sem("silu"), 1)

            def hidden(m, h):
                wait_f(act, f, "guw", of_half(m + 1, h))
                wait_f(act, f, "y", of_half(m, h))
                act.activation(hid[0][:, h, :], guw[:, h, :], ACT.Copy).then_inc(sem("hid_hi"), 1)

            def step(m, k, p):
                runs = not known(m) or m < M
                if runs:
                    gate(m, 0)
                if not known(m) or m > 0:
                    hidden(m - 1, 1)
                if runs:
                    gate(m, 1)
                    if known(m) and m == 1:
                        for h in range(2):
                            wait_f(act, f, "cwb_first_ps", h + 1)
                            act.activation(half_of(cwb[:, 1, :], h), ps[:, 2 + h, :], ACT.Copy).then_inc(sem("cwb_first"), 1)
                    hidden(m, 0)

            ffn_steps(act, step)
            for h in range(2):
                wait_f(act, f, "y", of_half(M, h))
                for c in range(DC):
                    act.activation(half_of(aT[:, c, :], h), ps[:, 2 * h + c, :], ACT.Copy).then_inc(sem("aT"), 1)

        def ffn_pool(pool, f):
            def low(m, p, part, cols):
                wait_f(pool, f, f"{part}_hi", m + 1)
                pool.tensor_tensor(ew[1][:, p, cols], ew_raw[:, p, cols], fp(ew[0][:, p, cols]),
                                   ALU.subtract).then_inc(sem(f"{part}_lo"), 1)

            def weighted(m, k, p, h):
                if known(m) and m == 1:
                    wait_f(pool, f, "cwb_first", h + 1)
                elif h == 0:
                    wait_f(pool, f, f"cwb_{p}", 16 * k)
                wait_f(pool, f, "gu", of_half(m, h))
                wait_f(pool, f, "hid_lo", of_half(m, h))
                pool.tensor_tensor(guw[:, h, :], gu[:, h, :], half_of(cwb[:, p, :], h),
                                   ALU.mult).then_inc(sem("guw"), 1)

            def step(m, k, p):
                if known(m) and m == M:
                    return
                routed = not known(m) or m > 0
                if known(m) and m == 1:
                    low(2, 0, "gate", GATE_UP)
                if routed:
                    weighted(m, k, p, 0)
                if not known(m) or m != 1 and m + 1 < M:
                    low(m + 1, 1 - p, "gate", GATE_UP)
                if routed:
                    weighted(m, k, p, 1)
                low(m, p, "down", DOWN)

            def begin():
                wait_f(pool, f, "gw_hi", 1)
                pool.tensor_tensor(gw[1][:, :, :], gw_raw[:, :, :], fp(gw[0][:, :, :]), ALU.subtract).then_inc(sem("gw_lo"), 1)
                low(0, 0, "gate", GATE_UP)
                pool.memset(cwb[:, :, :].rearrange("p a t -> p (a t)")[:, 0:5 * NT * 2 * E], 0.0).then_inc(sem(f"route{f}"), 1)

            ln_pool(pool, 2 * f + 1, (0,))
            begin()
            ln_pool(pool, 2 * f + 1, (1,))
            ffn_steps(pool, step)
            if f == 0:
                w1_low(pool, range(4))

        def ffn_dve(dve, f):
            def high(m, k, p, part, cols):
                if part == "gate":
                    wait_f(dve, f, f"ew_ld_{p}", 16 * (k + 1))
                    wait_f(dve, f, "gu_ps", 4 * (m - 1))
                else:
                    wait_f(dve, f, "y", 2 * (m - 1))
                dve.tensor_copy(ew[0][:, p, cols], ew_raw[:, p, cols]).then_inc(sem(f"{part}_hi"), 1)

            def gated(m, h):
                wait_f(dve, f, "silu", of_half(m + 1, h))
                wait_f(dve, f, "gu_ps", 4 * m + 2 * h + 2)
                if known(m) and m == 0:
                    dve.tensor_tensor(guw[:, h, :], silu[:, h, :], ps[:, 5 + 2 * h, :], ALU.mult).then_inc(sem("guw"), 1)
                else:
                    if not known(m) or m > 1:
                        wait_f(dve, f, "guw", of_half(m, h))
                    dve.tensor_tensor(gu[:, h, :], silu[:, h, :], ps[:, 5 + 2 * h, :], ALU.mult).then_inc(sem("gu"), 1)

            def hidden(m, h):
                wait_f(dve, f, "hid_hi", of_half(m + 1, h))
                dve.tensor_tensor(hid[1][:, h, :], guw[:, h, :], fp(hid[0][:, h, :]), ALU.subtract).then_inc(sem("hid_lo"), 1)

            def step(m, k, p):
                runs, split = not known(m) or m < M, not known(m) or m + 1 < M
                if runs:
                    gated(m, 0)
                if not known(m) or m > 0:
                    hidden(m - 1, 1)
                if split:
                    high(m + 1, k + p, 1 - p, "gate", GATE_UP)
                if known(m) and m < 2:
                    next(route)
                if runs:
                    gated(m, 1)
                    high(m, k, p, "down", DOWN)
                    if known(m) and m == 1:
                        next(route)
                    hidden(m, 0)
                if known(m) and m == 0:
                    next(route)

            def begin():
                wait_f(dve, f, "gw_ld", 16)
                dve.tensor_copy(gw[0][:, :, :], gw_raw[:, :, :]).then_inc(sem("gw_hi"), 1)
                high(0, 0, 0, "gate", GATE_UP)

            route = ffn_route(dve, f)
            begin()
            if f == 0:
                ln_xn(dve, 1, 0)
                back_dve(dve, 2, (0, 1), range(QT, 2 * QT))
            else:
                back_dve(dve, 10, (2, 3), range(QT, 2 * QT))
                ln_xn(dve, 3, 0)
            ln_stats(dve, 2 * f + 1, 1)
            ln_low(dve, 2 * f + 1, 0)
            ln_xn(dve, 2 * f + 1, 1)
            ln_low(dve, 2 * f + 1, 1)
            ffn_steps(dve, step)
            if f == 0:
                w1_high(dve)
            for h in range(2):
                back_dve(dve, 8 * f + 4 + 2 * h, (4 + 2 * h, 5 + 2 * h), range(QT * h, QT * h + QT))

        def ffn_route(dve, f):
            done = [1]

            def then(ins):
                ins.then_inc(sem(f"route{f}"), 1)
                done[0] += 1

            def prev():
                dve.wait_ge(sem(f"route{f}"), done[0])

            def ranked(count, n, value, gt, eq, lower, rank):
                of_j = value.unsqueeze(2).broadcast_to([P, count, n, n])
                of_i = value.unsqueeze(3).broadcast_to([P, count, n, n])
                sq = [v.rearrange("p t (i j) -> p t i j", i=n) for v in (gt, eq)]
                then(dve.tensor_tensor(sq[0], of_j, of_i, ALU.is_gt))
                then(dve.tensor_tensor(sq[1], of_j, of_i, ALU.is_equal))
                prev()
                then(dve.tensor_tensor(eq, eq, lower.unsqueeze(1).broadcast_to([P, count, n * n]), ALU.mult))
                prev()
                then(dve.tensor_tensor(gt, gt, eq, ALU.add))
                prev()
                then(dve.tensor_reduce(rank.rearrange("p (t i) -> p t i", i=n), sq[0], AX.X, ALU.add))
                prev()

            wait_f(dve, f, "ebias_ld", 32)
            wait_f(dve, f, "score_ps", 1)
            then(dve.tensor_copy(score[:, :, :].rearrange("p t e -> p (t e)"), ps[:, 2, 0:NT * E]))
            prev()
            then(dve.tensor_tensor(biased[:, :, :], score[:, :, :], ebias[:, :].unsqueeze(1).broadcast_to([P, NT, E]), ALU.add))
            prev()
            value = biased
            if f == 0:
                grp = biased[:, :, :].rearrange("p t (g i) -> p (t g) i", i=GSIZE)
                for col, gap in ((0, 1), (3, 2), (5, 3)):
                    n = GSIZE - gap
                    then(dve.tensor_tensor(pairsum[:, :, col:col + n], grp[:, :, 0:n], grp[:, :, gap:GSIZE], ALU.add))
                prev()
                then(dve.tensor_reduce(gscore[:, :, :].rearrange("p t g -> p (t g)"), pairsum[:, :, :], AX.X, ALU.max))
                prev()
                ranked(NT, GROUPS, gscore[:, :, :], ggt[:, :, :], geq[:, :, :], lower4[:, :], grank[:, :])
                then(dve.tensor_scalar(gkeep[:, :], grank[:, :], float(GROUP_KEEP), None, ALU.is_lt))
                prev()
                then(dve.tensor_scalar(gpen[:, :], gkeep[:, :], BIG, -BIG, ALU.mult, ALU.add))
                msk = masked[:, :, :].rearrange("p t (g i) -> p (t g) i", i=GSIZE)
                over = [P, NT * GROUPS, GSIZE]
                then(dve.tensor_tensor(msk, grp, gkeep[:, :].unsqueeze(2).broadcast_to(over), ALU.mult))
                prev()
                then(dve.tensor_tensor(msk, msk, gpen[:, :].unsqueeze(2).broadcast_to(over), ALU.add))
                prev()
                value = masked
            yield
            for t in range(NT):
                then(dve.max(out=best[:, t, :], in_=value[:, t, :]))
            prev()
            least = best[:, :, TOPK - 1:TOPK].broadcast_to([P, NT, E])
            then(dve.tensor_tensor(above[:, :, :], value[:, :, :], least, ALU.is_gt))
            then(dve.tensor_tensor(runs[0][:, :, E:], value[:, :, :], least, ALU.is_equal))
            prev()
            then(dve.tensor_reduce(nabove[:, :], above[:, :, :], AX.X, ALU.add))
            for k in range(4):
                gap = 1 << k
                then(dve.tensor_tensor(runs[k + 1][:, :, E:], runs[k][:, :, E:], runs[k][:, :, E - gap:2 * E - gap], ALU.add))
                prev()
            yield
            then(dve.tensor_tensor(fits[:, :, :], runs[4][:, :, E:], nabove[:, :].unsqueeze(2).broadcast_to([P, NT, E]), ALU.add))
            prev()
            then(dve.scalar_tensor_tensor(out=fits[:, :, :], in0=fits[:, :, :], scalar=float(TOPK), in1=runs[0][:, :, E:],
                                          op0=ALU.is_le, op1=ALU.mult))
            prev()
            then(dve.tensor_tensor(chosen[:, :, :], above[:, :, :], fits[:, :, :], ALU.add))
            prev()
            then(dve.tensor_tensor(chosen[:, :, :], chosen[:, :, :], score[:, :, :], ALU.mult))
            prev()
            then(dve.tensor_reduce(wsum[:, :], chosen[:, :, :], AX.X, ALU.add))
            prev()
            then(dve.tensor_scalar(wsume[:, :], wsum[:, :], RENORM_EPS[f], None, ALU.add))
            prev()
            then(dve.reciprocal(wrec[:, :], wsume[:, :]))
            prev()
            dve.scalar_tensor_tensor(out=cw[:, :, :], in0=chosen[:, :, :], scalar=ROUTE_SCALE[f],
                                     in1=wrec[:, :].unsqueeze(2).broadcast_to([P, NT, E]),
                                     op0=ALU.mult, op1=ALU.mult).then_inc(sem("cw"), 1)
            yield
            for k in range(2):
                wait_f(dve, f, "cwT_ps", QT * (k + 1))
                dve.tensor_copy(half_of(cwT, k), ps[0:E, 6 + k, :]).then_inc(sem("cwT"), 1)
            yield

        GROUPS1 = [(t, mt, h) for h in range(2) for mt in range(DC) for t in range(2)]
        CHUNKS = 2 * QT
        BANKS1, SLOTS = QT, CHUNKS
        LOOK = 4
        PARTS_LEAD = 3
        MAX_AHEAD, TAKE_AHEAD = 3, 2
        STAGES = 4
        V_HI, V_LO, V_ONE = (k * 2 * DH1 for k in range(3))
        QUADS = N1 // 4
        HI_DVE, LO_DVE = ((0, 4), (0, 2, 4)), ((0, 4), (0, 2, 4))
        LAST = N1 - MAX_AHEAD

        def is_last(n):
            return known(n) and n >= LAST

        def of_chunk(n, c, own):
            mine = [[k for k in range(CHUNKS) if own(k, last)] for last in (False, True)]
            before = len(mine[0]) * LAST + len(mine[1]) * (n - LAST) if is_last(n) else len(mine[0]) * n
            return before + mine[is_last(n)].index(c) + 1

        def hi_count(n, c):
            on_dve = c in HI_DVE[is_last(n)]
            return ("p_hi_dve" if on_dve else "p_hi_act", of_chunk(n, c, lambda k, last: (k in HI_DVE[last]) == on_dve))

        def lo_count(n, c):
            on_dve = c in LO_DVE[is_last(n)]
            return ("p_lo_dve" if on_dve else "p_lo_pool", of_chunk(n, c, lambda k, last: (k in LO_DVE[last]) == on_dve))

        def is_pair(n):
            return not known(n) or 0 <= n < N1

        HEAD_FROM, V_CHUNKS = 6, 2

        def head_start(step):
            for n in range(-MAX_AHEAD, 0):
                for c in range(CHUNKS):
                    step(n, n // 4, n % 4, c)
                    yield

        def a1_steps(eng, step, rest=()):
            for _ in rest:
                pass
            for n in range(4):
                for c in range(CHUNKS):
                    step(n, n // 4, n % 4, c)
            with eng.Fori(1, QUADS - 1) as r:
                for k in range(4):
                    for c in range(CHUNKS):
                        step(4 * r + k, r, k, c)
            for n in range(N1 - 4, N1):
                for c in range(CHUNKS):
                    step(n, n // 4, n % 4, c)

        TILE_AT = {0: (0,), 1: (1,), 2: (2,), 3: (3,), 5: (4,), 6: (5,), 7: (6, 7)}
        BANK_TURN = {0: 0, 1: 1, 2: 2, 3: 3, "taken": 4, 4: 5, 5: 6, 6: 7, 7: 8}
        MAX_BEFORE = {0: -1, 1: 0, 2: 1, 3: 2, 4: 4, 6: 5, 7: 6}

        V_BANK = (4, 5, 0, 1)
        O_BANK = (0, 2)

        def max_bank(k, what):
            return 6 + (k + BANK_TURN[what]) % 2

        def v_part(v, part):
            return v1s[:, v // 2 * H1:(v // 2 + 1) * H1, v % 2 * 2:v % 2 * 2 + 2, part, :]

        def stored(quad, k):
            return 96 * quad + (32 if known(quad) and quad == QUADS - 1 else 48) * (k // 2)

        def a1_sp(sp):
            sp.wait_ge(sem("x_add"), 4)
            for part in range(6):
                sp.dma_start(w1_raw[:, part, :, :], a["w1"][:, part]).then_inc(sem(f"w1_ld{part // 3}"), 16)
            for dst, name in ((cos1, "cos1"), (sin1, "sin1"), (bo1, "bo1")):
                sp.dma_start(dst[:, :], a[name]).then_inc(sem("tab1"), 16)
            sp.dma_start(b1[:, :, :], a["b1"]).then_inc(sem("tab1"), 16)
            sp.dma_start(bv1[:, :], a["bv1"].partition_broadcast(P)).then_inc(sem("tab1"), 16)
            def load(n, k):
                for t, dst in enumerate((qs, ks)):
                    sp.dma_start(fp(dst[:, k, :]), stk_dram[t][bass.ds(n * P, P), :]).then_inc(sem(f"stage_ld{k}"), 16)

            def store(quad, k):
                p = k % 2
                dst = [t[2 * DH1 * k:2 * DH1 * (k + 1), bass.ds(quad, 1), :].rearrange("p q t -> p (q t)") for t in (zh, zl)]
                wait(sp, "zev_free", 4 * quad + k + 3)
                for j in range(2):
                    sp.dma_start(dst[j], zst[j * 2 * DH1:(j + 1) * 2 * DH1, p, :]).then_inc(sem(f"z_st{p}"), 16)
                if not known(quad) or quad < QUADS - 1:
                    den_rows = den_dram[bass.ds(quad * 8 * QT + k * 2 * QT, 2 * QT), :]
                    dens = zst[V_ONE:V_ONE + 2 * DH1:DH1, p, :].rearrange("h (i q) -> h i q", q=P)
                    sp.dma_start(den_rows, dens).then_inc(sem(f"z_st{p}"), 16)

            def step(n, quad, k, c):
                if c:
                    return
                if known(n):
                    ahead(n)
                if known(n) and n == 0:
                    sp.wait_ge(sem("stk_st"), 16 * 3 * 4)
                if known(n) and n in (1, 2):
                    for g in (2 * n + 2, 2 * n + 3):
                        stack(g)
                if not known(n) or 0 <= n < N1 - STAGES:
                    wait(sp, "st_ps", CHUNKS * (n + 1))
                    load(n + STAGES, k)
                if not known(n) or n > 0:
                    store(quad if k else quad - 1, (k - 1) % 4)
                if known(n) and n == 3:
                    sp.wait_ge(sem("stk_st"), 16 * 3 * len(GROUPS1))
                    ffn_sp(sp, 1)
                if is_pair(n + TAKE_AHEAD):
                    k2 = (k + TAKE_AHEAD) % STAGES
                    wait(sp, "nmT", n + TAKE_AHEAD + 1)
                    for part in range(2):
                        sp.dma_start(fp(qs[ROWS_S + part:P:STK, k2, :]), fp(nmT[part * 2 * QT:(part + 1) * 2 * QT, k % 2, :])
                                     ).then_inc(sem(f"nm_st{k2}"), 16)

            def spread(src, g):
                rows = src[g * 8 * QT:(g + 1) * 8 * QT, :].rearrange("(h i) q -> h (i q)", i=QT)
                return rows.unsqueeze(1).broadcast_to([8, DH1, S])

            def ahead(n):
                if n == N1 - 4:
                    for p in range(2):
                        sp.wait_ge(sem(f"z_st{p}"), 48 * 4)
                    sp.dma_start(den1[:, :], den_dram[0:8 * QT * DC, :]).then_inc(sem("den1_ld"), 16)
                if n == N1 - 3:
                    sp.wait_ge(sem("rden1"), 1)
                    sp.dma_start(rden_dram[0:8 * QT * DC, :], rden1[:, :]).then_inc(sem("rden_st"), 16)
                    for p in range(2):
                        sp.wait_ge(sem(f"z_st{p}"), 48 * 6)
                    sp.dma_start(den_b, spread(den_dram, 2)).then_inc(sem("den2_ld"), 16)
                if n == N1 - 2:
                    sp.wait_ge(sem("rden_st"), 16)
                    for g in range(DC):
                        sp.dma_start(rden_b[g], spread(rden_dram, g)).then_inc(sem("rden_ld"), 16)

            def stack(g):
                t, mt, h = GROUPS1[g]
                rows = stk_dram[t].rearrange("(b h r) s -> b h r s", b=B, r=STK)[h, mt * H1 // 2:(mt + 1) * H1 // 2]
                for part in range(2):
                    sp.wait_ge(sem(f"qk1_{part}"), g + 1)
                    for j in range(3):
                        if PARTS[j][t] == part:
                            sp.dma_start(rows[:, j * DH1:(j + 1) * DH1, :],
                                         fp(qk1[part][:, t, mt, h * S:(h + 1) * S])).then_inc(sem("stk_st"), 16)
            sp.wait_ge(sem("ones_st"), 16 * 8)
            for quad in range(2):
                for g in (2 * quad, 2 * quad + 1):
                    stack(g)
                if quad == 0:
                    sp.wait_ge(sem("stk_st"), 16 * 3 * 2)
                    for n in range(STAGES):
                        load(n, n)
            a1_steps(sp, step, head_start(step))
            store(QUADS - 1, 3)

        def a1_pe(pe):
            pe.sem_inc(sem("pv1"), SLOTS)
            def maximum(n, quad, k, tile):
                hd, qi = tile // QT, tile % QT
                if tile == 0:
                    wait(pe, f"stage_ld{k}", 32 * (quad + 1))
                if tile in MAX_BEFORE:
                    wait(pe, "max", CHUNKS * n + MAX_BEFORE[tile])
                else:
                    wait(pe, "nmT", n)
                    wait(pe, "max", CHUNKS * n + 3)
                rows = slice(hd * STK, hd * STK + ROWS_S)
                pe.matmul(ps[:, max_bank(k - MAX_AHEAD, tile), :], qs[rows, k, qi * P:(qi + 1) * P], ks[rows, k, :],
                          start=True, stop=True).then_inc(sem("s1"), 1)

            def taken(n, k):
                wait(pe, "nm_lo", n + 1)
                wait(pe, "max", CHUNKS * (n + 1) + 3 if not known(n) or n + 1 < N1 else CHUNKS * N1)
                pe.transpose(ps[0:4 * QT, max_bank(k - TAKE_AHEAD, "taken"), 0:P], fp(nm_s[:, k % 2, :]), ident[:, :]
                             ).then_inc(sem("nmT_ps"), 1)

            def scores(n, quad, k, c):
                hd, kt = c // QT, c % QT
                if c == 0:
                    wait(pe, f"nm_st{k}", 32 * (quad + 1))
                wait(pe, "st_free", CHUNKS * n + c + 1)
                rows = slice(hd * STK, hd * STK + ROWS_M)
                pe.matmul(ps[:, kt, :], ks[rows, k, kt * P:(kt + 1) * P], qs[rows, k, :],
                          start=True, stop=True).then_inc(sem("st_ps"), 1)

            def pv(n, k, c):
                hd, kt, p = c // QT, c % QT, k % 2
                if c == 0:
                    wait(pe, "vs", n + 1)
                    wait(pe, "zev_free", n + 1)
                name, count = lo_count(n, c)
                wait(pe, name, count)
                for part in range(2):
                    last = pe.matmul(ps[:, 4 + p, :], vs[:, p, kt, hd, :], p1[part][:, c, :],
                                     start=c == 0 and part == 0, stop=c == CHUNKS - 1 and part == 1, skip_group_check=True)
                last.then_inc(sem("pv1"), 1)

            def step(n, quad, k, c):
                if c + LOOK < CHUNKS:
                    if is_pair(n):
                        scores(n, quad, k, c + LOOK)
                elif is_pair(n + 1):
                    scores(n + 1, quad + (k + 1) // 4, (k + 1) % 4, c + LOOK - CHUNKS)
                if is_pair(n):
                    pv(n, k, c)
                if c == 4 and is_pair(n + TAKE_AHEAD):
                    taken(n + TAKE_AHEAD, (k + TAKE_AHEAD) % 4)
                if is_pair(n + MAX_AHEAD):
                    for tile in TILE_AT.get(c, ()):
                        maximum(n + MAX_AHEAD, quad + (k + MAX_AHEAD) // 4, (k + MAX_AHEAD) % 4, tile)
                if known(n) and n > N1 - 4 and c == 6:
                    denT(n - 1)

            def denT(n):
                k = n % 4
                pe.wait_ge(sem("zev_free"), n + 3)
                if k == 0:
                    pe.wait_ge(sem("max"), CHUNKS * N1)
                elif k < 3:
                    pe.wait_ge(sem("rdenT"), k)
                else:
                    pe.wait_ge(sem("nmT"), N1)
                for i in range(QT):
                    last = pe.transpose(ps[:, 6 + k // 3, i * P + 2 * DH1 * k:i * P + 2 * DH1 * (k + 1)],
                                        zst[V_ONE:V_ONE + 2 * DH1, k % 2, i * P:(i + 1) * P],
                                        ident[V_ONE:V_ONE + 2 * DH1, V_ONE:V_ONE + 2 * DH1])
                last.then_inc(sem("denT"), 1)

            def project(h):
                for m in range(DC):
                    for j in range(3 * DC):
                        ch, (pw, pz) = j // 3, PARTS[j % 3]
                        if m == 0 and j % 3 == 0:
                            pe.wait_ge(sem("zc_lo"), DC * h + ch + 1)
                        last = pe.matmul(ps[:, O_BANK[h] + m, :], w1[pw][:, 5, ch, m * P:(m + 1) * P],
                                         p1z[pz][:, h * DC + ch, :], start=j == 0, stop=j == 3 * DC - 1)
                    last.then_inc(sem("o1"), 1)

            head = head_start(step)
            for g, (t, mt, h) in enumerate(GROUPS1):
                pe.wait_ge(sem("xT_lo"), 2 * DC * 2 + DC * (h + 1))
                wait(pe, "w1_lo", 2 * t + 2)
                wait(pe, "rs", 2 * (g - 2))
                for sw in range(2):
                    for j in range(3 * DC):
                        ch, (pw, px) = j // 3, PARTS[j % 3]
                        last = pe.matmul(ps[:, 2 * (g % 3) + sw, :], w1[pw][:, 2 * t + sw, ch, mt * P:(mt + 1) * P],
                                         half_of((xT_hi, xT_lo)[px][:, ch, :], h), start=j == 0, stop=j == 3 * DC - 1)
                    last.then_inc(sem("qk1_ps"), 1)
                    if g >= HEAD_FROM:
                        next(head)
            pe.wait_ge(sem("w1_lo"), 5)
            for v in range(NT // 2):
                pe.wait_ge(sem("rs"), 2 * (6 + v // 2))
                for t2 in range(2):
                    t = 2 * v + t2
                    for j in range(3 * DC):
                        ch, (pw, px) = j // 3, PARTS[j % 3]
                        last = pe.matmul(ps[:, V_BANK[v], t2 * D:(t2 + 1) * D], (xT_hi, xT_lo)[px][:, ch, t * P:(t + 1) * P],
                                         w1[pw][:, 4, ch, :], start=j == 0, stop=j == 3 * DC - 1)
                last.then_inc(sem("v1_ps"), 1)
                for _ in range(V_CHUNKS):
                    next(head)
            pe.wait_ge(sem("rs"), 16)
            pe.wait_ge(sem("v1"), NT // 2)
            a1_steps(pe, step, head)
            denT(N1 - 1)
            pe.wait_ge(sem("w1_lo"), 6)
            pe.wait_ge(sem("st_free"), CHUNKS * N1 - 2 + BANKS1)
            project(0)
            pe.wait_ge(sem("zev_free"), N1 + 2)
            pe.wait_ge(sem("rdenT"), 4)
            for i in range(QT):
                last = pe.transpose(ps[:, 4, i * P:(i + 1) * P], rdenT[:, i, :], ident[:, :])
            last.then_inc(sem("rd_ps"), 1)
            back_pe(pe, "aT", 10, (0, 1), range(QT))
            pe.wait_ge(sem("st_free"), CHUNKS * N1 + BANKS1)
            project(1)
            back_pe(pe, "aT", 12, (2, 3), range(QT, 2 * QT))

        def a1_act(act):
            act.wait_ge(sem("tab1"), 16 * 5)
            for g, (t, mt, h) in enumerate(GROUPS1):
                act.wait_ge(sem("rr"), g + 1)
                act.activation(half_of(qk1[0][:, t, mt, :], h), rr[:, g % 2, :], ACT.Copy,
                               scale=SCALE1 if t == 0 else 1.0).then_inc(sem("qk1_0"), 1)
            for v in range(NT // 2):
                act.wait_ge(sem("v1"), v + 1)
                act.activation(v_part(v, 0), v1[:, :, :].rearrange("p t (h d) -> p h t d", h=H1),
                               ACT.Copy).then_inc(sem("v1_hi"), 1)
            act.sem_inc(sem("st_free"), BANKS1)
            act.sem_inc(sem("zev_free"), 2)

            def read_out(quad, k):
                n, p = 4 * quad + k, k % 2
                wait(act, "pv1", CHUNKS * n + CHUNKS + SLOTS)
                if not known(n) or n >= 2:
                    wait(act, f"z_st{p}", stored(quad, k))
                if known(n) and n >= N1 - 2:
                    act.wait_ge(sem("denT"), n - (N1 - 2) + 1)
                act.activation(zst[:, p, :], ps[0:3 * 2 * DH1, 4 + p, :], ACT.Copy).then_inc(sem("zev_free"), 1)

            def high(n, c):
                if c not in HI_DVE[is_last(n)]:
                    wait(act, "st_free", CHUNKS * n + c + 1 + BANKS1)
                    wait(act, "pv1", CHUNKS * n + c + 1)
                    act.activation(p1[0][:, c, :], e1[:, c, :], ACT.Copy).then_inc(sem("p_hi_act"), 1)

            def step(n, quad, k, c):
                if is_pair(n):
                    wait(act, "st_ps", CHUNKS * n + c + 1)
                    name, count = lo_count(n - 1, c)
                    wait(act, name, count)
                    act.activation(e1[:, c, :], ps[:, c % BANKS1, :], ACT.Exp).then_inc(sem("st_free"), 1)
                    if c:
                        high(n, c - 1)
                    if c == 3 and (not known(n) or n > 0):
                        read_out(quad if k else quad - 1, (k - 1) % 4)
                    if known(n) and n == N1 - 1 and c in (4, 5, 6):
                        z_high(c - 4)
                if c == 1 and is_pair(n - 1 + TAKE_AHEAD):
                    wait(act, "nmT_ps", n + TAKE_AHEAD)
                    act.activation(nmT[:, (k - 1) % 2, :], ps[0:4 * QT, max_bank(k - 1, "taken"), 0:P],
                                   ACT.Copy).then_inc(sem("nmT"), 1)
                if is_pair(n) and c == CHUNKS - 1:
                    high(n, c)

            def z_high(g):
                act.wait_ge(sem("zn"), g + 1)
                act.activation(p1z[0][:, g, :], zh[:, g, :], ACT.Copy).then_inc(sem("zc_hi"), 1)

            def result(h):
                for m in range(DC):
                    act.wait_ge(sem("o1"), DC * h + m + 1)
                    act.activation(half_of(aT[:, m, :], h), ps[:, O_BANK[h] + m, :], ACT.Identity,
                                   bias=bo1[:, m:m + 1]).then_inc(sem("aT"), 1)

            a1_steps(act, step, head_start(step))
            read_out(QUADS - 1, 3)
            result(0)
            z_high(3)
            result(1)

        def w1_high(dve):
            for part in range(6):
                dve.wait_ge(sem(f"w1_ld{part // 3}"), 48)
                dve.tensor_copy(w1[0][:, part, :, :], w1_raw[:, part, :, :]).then_inc(sem("w1_hi"), 1)

        def w1_low(pool, parts):
            for part in parts:
                pool.wait_ge(sem("w1_hi"), part + 1)
                pool.tensor_tensor(w1[1][:, part, :, :], w1_raw[:, part, :, :], fp(w1[0][:, part, :, :]),
                                   ALU.subtract).then_inc(sem("w1_lo"), 1)

        def a1_pool(pool):
            w1_low(pool, range(4, 6))
            pool.wait_ge(sem("x_add"), 8)
            pool.memset(vs[:, :, :, :, :].bitcast(F32), 0.0).then_inc(sem("vs_zero"), 1)
            pool.wait_ge(sem("vs_zero"), 1)
            for hd in range(2):
                ones = vs[:, :, :, hd, V_ONE + hd * DH1:V_ONE + (hd + 1) * DH1]
                pool.memset(ones.bitcast(F32), 1.0).then_inc(sem("vs_one"), 1)
            for g in range(len(GROUPS1)):
                pool.wait_ge(sem("rs"), 2 * (g + 1))
                wait(pool, "qk1_1", g - 1)
                pool.tensor_tensor(rr[:, g % 2, :], rc[:, g % 2, :], rs[:, g % 2, :], ALU.add).then_inc(sem("rr"), 1)

            def step(n, quad, k, c):
                if is_pair(n) and c not in LO_DVE[is_last(n)]:
                    name, count = hi_count(n, c)
                    wait(pool, name, count)
                    pool.tensor_tensor(p1[1][:, c, :], e1[:, c, :], fp(p1[0][:, c, :]), ALU.subtract).then_inc(sem("p_lo_pool"), 1)

            a1_steps(pool, step)

        def a1_dve(dve):
            dve.wait_ge(sem("tab1"), 16 * 5)

            def low(g):
                t, mt, h = GROUPS1[g]
                dve.wait_ge(sem("qk1_0"), g + 1)
                dve.scalar_tensor_tensor(out=half_of(qk1[1][:, t, mt, :], h), in0=rr[:, g % 2, :],
                                         scalar=SCALE1 if t == 0 else 1.0, in1=fp(half_of(qk1[0][:, t, mt, :], h)),
                                         op0=ALU.mult, op1=ALU.subtract).then_inc(sem("qk1_1"), 1)

            def operand(n, p):
                wait(dve, "pv1", CHUNKS * (n - 1) + SLOTS)
                for hd in range(2):
                    src = v1s[:, bass.ds(2 * n + hd, 1), :, :, :].rearrange("p h t u d -> p t (h u) d")
                    dst = vs[:, p, :, hd, V_HI:V_ONE].rearrange("p t (u h d) -> p t u h d", u=2, h=2)[:, :, :, hd, :]
                    if not known(n):
                        dve.sem_inc(sem("vs_go"), 1)
                    last = dve.tensor_copy(dst, src)
                last.then_inc(sem("vs"), 1)

            def maximum(n, p, k, tile):
                wait(dve, "s1", CHUNKS * n + tile + 1)
                dve.tensor_reduce(nm1[:, p, tile:tile + 1], ps[:, max_bank(k - MAX_AHEAD, tile), :], AX.X, ALU.max,
                                  negate=True).then_inc(sem("max"), 1)
                if tile == CHUNKS - 1:
                    wait(dve, "max", CHUNKS * n + CHUNKS)
                    dve.tensor_copy(nm_s[:, p, 0:CHUNKS], nm1[:, p, :]).then_inc(sem("nm_hi"), 1)
                    wait(dve, "nm_hi", n + 1)
                    dve.tensor_tensor(nm_s[:, p, CHUNKS:], nm1[:, p, :], fp(nm_s[:, p, 0:CHUNKS]), ALU.subtract).then_inc(sem("nm_lo"), 1)

            def parts(n, c):
                if not is_pair(n):
                    return
                if c in HI_DVE[is_last(n)]:
                    wait(dve, "st_free", CHUNKS * n + c + 1 + BANKS1)
                    wait(dve, "pv1", CHUNKS * n + c + 1)
                    dve.tensor_copy(p1[0][:, c, :], e1[:, c, :]).then_inc(sem("p_hi_dve"), 1)
                if c in LO_DVE[is_last(n)]:
                    name, count = hi_count(n, c)
                    wait(dve, name, count)
                    dve.tensor_tensor(p1[1][:, c, :], e1[:, c, :], fp(p1[0][:, c, :]), ALU.subtract).then_inc(sem("p_lo_dve"), 1)

            def step(n, quad, k, c):
                if c + PARTS_LEAD < CHUNKS:
                    parts(n, c + PARTS_LEAD)
                else:
                    parts(n + 1, c + PARTS_LEAD - CHUNKS)
                if c == 4 and is_pair(n + 1):
                    operand(n + 1, (k + 1) % 2)
                if is_pair(n + MAX_AHEAD):
                    for tile in TILE_AT.get(c, ()):
                        maximum(n + MAX_AHEAD, (k + MAX_AHEAD) % 2, (k + MAX_AHEAD) % 4, tile)
                if known(n):
                    ahead(n, c)

            def z_sum(g):
                for p in range(2):
                    dve.wait_ge(sem(f"z_st{p}"), stored(g, 4))
                dve.tensor_tensor(zh[:, g, :], zh[:, g, :], zl[:, g, :], ALU.add).then_inc(sem("zsum"), 1)

            def reciprocal(cols):
                dve.reciprocal(rden_b[2][:, cols], den_b[:, cols]).then_inc(sem("rden_b"), 1)

            def reciprocalT(k):
                dve.wait_ge(sem("denT"), k + 1)
                rows = slice(2 * DH1 * k, 2 * DH1 * (k + 1))
                dve.reciprocal(rdenT[:, :, rows], ps[:, 6 + k // 3, :].rearrange("p (i r) -> p i r", i=QT)[:, :, rows]).then_inc(sem("rdenT"), 1)

            def z_norm(g):
                dve.wait_ge(sem("zsum"), g + 1)
                name, count = (("rden_ld", 16 * DC), ("rden_ld", 16 * DC), ("rden_b", QT), ("rd_ps", 1))[g]
                dve.wait_ge(sem(name), count)
                dve.tensor_tensor(zh[:, g, :], zh[:, g, :], rden_b[g] if g < 3 else ps[:, 4, :], ALU.mult).then_inc(sem("zn"), 1)

            def z_low(g):
                dve.wait_ge(sem("zc_hi"), g + 1)
                dve.tensor_tensor(p1z[1][:, g, :], zh[:, g, :], fp(p1z[0][:, g, :]), ALU.subtract).then_inc(sem("zc_lo"), 1)

            def ahead(n, c):
                if (n, c) == (N1 - 4, 4):
                    dve.wait_ge(sem("den1_ld"), 16)
                    dve.reciprocal(rden1[:, :], den1[:, :]).then_inc(sem("rden1"), 1)
                if (n, c) == (N1 - 3, 5):
                    for g in range(DC):
                        z_sum(g)
                if (n, c) == (N1 - 2, 1):
                    z_sum(2)
                    dve.wait_ge(sem("den2_ld"), 16)
                if n == N1 - 2 and 1 <= c <= QT:
                    reciprocal(slice((c - 1) * P, c * P))
                if (n, c) == (N1 - 2, 6):
                    for g in range(DC):
                        z_norm(g)
                if (n, c) == (N1 - 1, 0):
                    z_norm(2)
                if n >= N1 - 2 and c == 0:
                    reciprocalT(n - (N1 - 2))
                if (n, c) == (N1 - 1, 2):
                    for g in range(DC):
                        z_low(g)
                if (n, c) == (N1 - 1, 4):
                    z_low(2)

            head = head_start(step)
            for g, (t, mt, h) in enumerate(GROUPS1):
                for sw, (dst, table) in enumerate(((rc, cos1), (rs, sin1))):
                    dve.wait_ge(sem("qk1_ps"), 2 * g + sw + 1)
                    wait(dve, "rr", g - 1)
                    dve.scalar_tensor_tensor(out=dst[:, g % 2, :], in0=ps[:, 2 * (g % 3) + sw, :],
                                             scalar=b1[:, 2 * t + sw, mt:mt + 1], in1=table[:, :],
                                             op0=ALU.add, op1=ALU.mult).then_inc(sem("rs"), 1)
                    if g >= HEAD_FROM:
                        next(head)
                if g:
                    low(g - 1)
            low(len(GROUPS1) - 1)
            for v in range(NT // 2):
                dve.wait_ge(sem("v1_ps"), v + 1)
                wait(dve, "v1_lo", v)
                dve.tensor_tensor(v1[:, :, :], ps[:, V_BANK[v], :].rearrange("p (t d) -> p t d", t=2),
                                  bv1[:, :].unsqueeze(1).broadcast_to([P, 2, D]), ALU.add).then_inc(sem("v1"), 1)
                for _ in range(V_CHUNKS):
                    next(head)
                dve.wait_ge(sem("v1_hi"), v + 1)
                dve.tensor_tensor(v_part(v, 1), v1[:, :, :].rearrange("p t (h d) -> p h t d", h=H1),
                                  fp(v_part(v, 0)), ALU.subtract).then_inc(sem("v1_lo"), 1)
            dve.wait_ge(sem("vs_one"), 2)
            dve.wait_ge(sem("v1_lo"), NT // 2)
            a1_steps(dve, step, head)
            reciprocalT(2)
            reciprocalT(3)
            z_sum(3)
            z_norm(3)
            z_low(3)
            back_dve(dve, 8, (0, 1), range(QT))
            ln_stats(dve, 3, 0)
        block = es.enter_context(nc.Block())

        @block.sync
        def _(sp):
            sp.dma_start(x[:, :, :], a["x"].rearrange("(t p) d -> p t d", p=P)).then_inc(sem("x_ld"), 16)
            sp.dma_start(ident[:, :], a["ident"]).then_inc(sem("ident"), 16)
            for dst, name in ((cos0, "cos0"), (sin0, "sin0"), (bo0, "bo0")):
                sp.dma_start(dst[:, :], a[name]).then_inc(sem("tab0"), 16)
            sp.dma_start(bqkv0[:, :, :], a["bqkv0"]).then_inc(sem("tab0"), 16)
            sp.wait_ge(sem("ones"), 1)
            for t in range(2):
                rows = stk_dram[t].rearrange("(b h r) s -> b h r s", b=B, r=STK)
                for g in range(DC):
                    for h in range(B):
                        sp.dma_start(rows[h, g * H1 // 2:(g + 1) * H1 // 2, ROWS_S:STK, :],
                                     fp(ones_r[:, :])).then_inc(sem("ones_st"), 16)
            a0_steps(sp, a0_sp)
            ffn_sp(sp, 0)
            ffn_sp_run(sp, 0)
            a1_sp(sp)
            ffn_sp_run(sp, 1)
            for h in range(2):
                sp.wait_ge(sem("x_add"), 4 * 4 - 2 + 2 * h)
                sp.dma_start(out.rearrange("(t p) d -> p t d", p=P)[:, h * QT:(h + 1) * QT, :],
                             x[:, h * QT:(h + 1) * QT, :]).then_inc(sem("out"), 16)
            sp.wait_ge(sem("out"), 32)

        @block.tensor
        def _(pe):
            ln_pe(pe, 0)
            a0_zero_pe(pe, 0)
            pe.wait_ge(sem("xT_lo"), 2 * DC)
            a0_steps(pe, a0_pe, a0_end_pe)
            ffn_pe(pe, 0)
            ln_pe(pe, 2)
            a1_pe(pe)
            ffn_pe(pe, 1)

        @block.scalar
        def _(act):
            ln_act(act, 0)
            act.wait_ge(sem("tab0"), 64)
            a0_steps(act, a0_act, a0_end_act)
            ln_act(act, 1)
            ffn_act(act, 0)
            ln_act(act, 2)
            a1_act(act)
            ln_act(act, 3)
            ffn_act(act, 1)

        @block.vector
        def _(dve):
            dve.memset(zero_r[:, :].bitcast(F32), 0.0).then_inc(sem("zero"), 1)
            dve.memset(ones_r[:, :].bitcast(F32), 1.0).then_inc(sem("ones"), 1)
            ln_dve(dve, 0)
            dve.wait_ge(sem("tab0"), 64)
            a0_steps(dve, a0_dve, a0_end_dve)
            ffn_dve(dve, 0)
            ln_dve(dve, 2)
            a1_dve(dve)
            ffn_dve(dve, 1)

        @block.gpsimd
        def _(pool):
            ln_pool(pool, 0)
            pool.wait_ge(sem("tab0"), 64)
            a0_steps(pool, a0_pool)
            ffn_pool(pool, 0)
            ln_pool(pool, 2)
            a1_pool(pool)
            ffn_pool(pool, 1)


def _rope_tables():
    pos = np.arange(S, dtype=np.float32)
    inv0 = (1.0 / np.float32(10000.0) ** (np.arange(0, DH0, 2, dtype=np.float32) / np.float32(DH0))).astype(np.float32)
    f0 = (pos[None, :] * inv0[:, None]).astype(np.float32)
    cos0, sin0 = np.repeat(np.cos(f0), 2, 0), np.repeat(np.sin(f0), 2, 0)
    sin0[0::2] *= -1.0
    inv1 = (1.0 / np.float32(10000.0) ** (np.arange(0, DH1, 2, dtype=np.float32) / np.float32(DH1))).astype(np.float32)
    f1 = (pos[None, :] * inv1[:, None]).astype(np.float32)
    cos1 = np.tile(np.concatenate([np.cos(f1), np.cos(f1)]), (P // DH1, 1))
    sin1 = np.tile(np.concatenate([-np.sin(f1), np.sin(f1)]), (P // DH1, 1))
    return cos0, sin0, cos1, sin1


def _layout(i):
    def chunks(m):
        return m.reshape(-1, P, m.shape[-1]).transpose(1, 0, 2)

    i = {k: np.asarray(v) for k, v in i.items()}
    d = {"x": i["L0_attn_resid_pre"].reshape(T, D), "ident": np.eye(P, dtype=np.float32)}
    d["cos0"], d["sin0"], d["cos1"], d["sin1"] = _rope_tables()

    def heads(wt):
        return wt.reshape(H0, DC, P, DH0).transpose(0, 2, 1, 3)

    d["wqk0"] = np.stack([heads(i["L0_attn_W_Q"]), heads(i["L0_attn_W_K"])], axis=2)
    d["wv0"] = heads(i["L0_attn_W_V"])
    d["wo0"] = i["L0_attn_W_O"].reshape(H0, DH0, D)
    bias = np.stack([i["L0_attn_b_Q"], i["L0_attn_b_K"], i["L0_attn_b_V"]])
    d["bqkv0"] = np.tile(bias.transpose(2, 0, 1), (1, 1, B))
    d["bo0"] = i["L0_attn_b_O"].reshape(DC, P).T

    lower = np.arange(GROUPS)[None, :] < np.arange(GROUPS)[:, None]
    d["lower4"] = lower.astype(np.float32).reshape(-1)
    names = (("gate_weight", "expert_bias", "gate_proj", "up_proj", "down_proj", "shared_gate", "shared_up", "shared_down"),
             ("gate_w", "expert_bias", "w_gate", "w_up", "w_down", "sw_gate", "sw_up", "sw_down"))
    for f in range(2):
        gate_w, ebias, g, u, dn, sg, su, sd = (i[f"L{f}_ffn_{n}"] for n in names[f])
        d[f"gw{f}"] = chunks(gate_w.T)
        d[f"ebias{f}"] = ebias
        every = [(sg, su, sd)] + [(g[e], u[e], dn[e]) for e in range(E)]
        d[f"ew{f}"] = np.stack([np.concatenate([chunks(g_.T).reshape(P, D), chunks(u_.T).reshape(P, D), dn_.T], axis=1)
                                for g_, u_, dn_ in every])

    swap = (np.arange(D) // DH1) * DH1 + (np.arange(D) + DH1 // 2) % DH1
    q, k = i["L1_attn_q_w"], i["L1_attn_k_w"]
    d["w1"] = np.stack([chunks(m.T) for m in (q, q[swap], k, k[swap], i["L1_attn_v_w"], i["L1_attn_out_w"])], axis=1)
    qb, kb = i["L1_attn_q_b"], i["L1_attn_k_b"]
    d["b1"] = np.stack([v.reshape(DC, P).T for v in (qb, qb[swap], kb, kb[swap])], axis=1)
    d["bv1"] = i["L1_attn_v_b"]
    d["bo1"] = i["L1_attn_out_b"].reshape(DC, P).T
    return {k: np.ascontiguousarray(v) for k, v in d.items()}


def kernel(**inputs):
    import concourse.bacc as bacc
    from concourse.bass_utils import run_bass_kernel_spmd

    nc = bacc.Bacc("TRN2", target_bir_lowering=False, num_devices=1)
    arrays = {f"in_{k}": v for k, v in _layout(inputs).items()}
    aps = {k[3:]: nc.dram_tensor(k, v.shape, mybir.dt.from_np(v.dtype), kind="ExternalInput").ap() for k, v in arrays.items()}
    out = nc.dram_tensor("out", (T, D), F32, kind="ExternalOutput").ap()
    build_program(nc, aps, out)
    r = run_bass_kernel_spmd(nc, [arrays], core_ids=[0])
    return r.results[0]["out"].reshape(B, S, D)
```
